# Optimizing a Trainium2 kernel written in Bass

```python
import numpy as np
import jax
import jax.numpy as jnp

def _softmax(x, axis=-1):
    return jax.nn.softmax(x, axis=axis)

def _gelu(x):
    return jax.nn.gelu(x, approximate=True)

def _silu(x):
    return jax.nn.silu(x)

def _sigmoid(x):
    return jax.nn.sigmoid(x)

def _layernorm(x, axis=-1, eps=1e-05):
    m = jnp.mean(x, axis=axis, keepdims=True)
    v = jnp.var(x, axis=axis, keepdims=True)
    return (x - m) / jnp.sqrt(v + eps)

def _scatter_add(tgt, idx, src, axis=0):
    return tgt.at[idx].add(src)

def _segment_sum(src, seg, n):
    return jax.ops.segment_sum(src, seg, n)
kernel_name = 'mk_vit_tower_cls_d2_tok_img768_r4_f303fc'

def setup_inputs(seed: int=0):
    np.random.seed(seed)
    _w = jnp.asarray

    def _rec_inputs():
        import jax
        import jax.numpy as jnp
        _rk = jax.random.key(seed)
        x = 7.57192e-06 + 1.00007 * jax.random.normal(jax.random.fold_in(_rk, 1), (64, 3, 84, 84), jnp.float32)
        cls_tok = 0.02 * jax.random.normal(jax.random.fold_in(_rk, 5), (1, 1, 192), jnp.float32)
        return (x, cls_tok)
    x, cls_tok = _rec_inputs()

    def _L0_tok_setup():
        import jax, jax.numpy as jnp
        import numpy as np
        K = 4
        STRIDE = 4
        EPS = 1e-05
        SLOPE = 0.01

        def conv2d(x, w, b, stride):
            out = jax.lax.conv_general_dilated(x, w, (stride, stride), 'VALID', dimension_numbers=('NCHW', 'OIHW', 'NCHW'))
            return out + b[None, :, None, None]

        def batchnorm(x, g, b, m, v):
            inv = g / jnp.sqrt(v + EPS)
            return x * inv[None, :, None, None] + (b - m * inv)[None, :, None, None]

        def leaky_relu(x):
            return jnp.where(x >= 0, x, SLOPE * x)

        def deform_conv(x, offset, w, b):
            B, C, H, W = x.shape
            Ho, Wo = (offset.shape[2], offset.shape[3])
            KK = K * K
            off = offset.reshape(B, KK, 2, Ho, Wo)
            kh = jnp.repeat(jnp.arange(K), K).astype(x.dtype)
            kw = jnp.tile(jnp.arange(K), K).astype(x.dtype)
            base_y = (jnp.arange(Ho) * STRIDE).astype(x.dtype)
            base_x = (jnp.arange(Wo) * STRIDE).astype(x.dtype)
            py = base_y[None, None, :, None] + kh[None, :, None, None] + off[:, :, 0]
            px = base_x[None, None, None, :] + kw[None, :, None, None] + off[:, :, 1]
            y0 = jnp.floor(py)
            x0 = jnp.floor(px)
            wy = py - y0
            wx = px - x0

            def corner(yc, xc):
                yi = yc.astype(jnp.int32)
                xi = xc.astype(jnp.int32)
                valid = (yi >= 0) & (yi < H) & (xi >= 0) & (xi < W)
                yi = jnp.clip(yi, 0, H - 1)
                xi = jnp.clip(xi, 0, W - 1)
                v = jax.vmap(lambda img, a, c: img[:, a, c])(x, yi, xi)
                return v * valid[:, None].astype(x.dtype)
            v00 = corner(y0, x0)
            v01 = corner(y0, x0 + 1)
            v10 = corner(y0 + 1, x0)
            v11 = corner(y0 + 1, x0 + 1)
            wy_ = wy[:, None]
            wx_ = wx[:, None]
            sampled = v00 * (1 - wy_) * (1 - wx_) + v01 * (1 - wy_) * wx_ + v10 * wy_ * (1 - wx_) + v11 * wy_ * wx_
            out = jnp.einsum('bckhw,ock->bohw', sampled, w.reshape(w.shape[0], C, KK))
            return out + b[None, :, None, None]
        key = jax.random.key(seed)
        ks = jax.random.split(key, 16)
        f32 = jnp.float32
        inp = {'x': jax.random.normal(ks[0], (64, 3, 224, 224), f32), 'stem_w': jax.random.normal(ks[1], (96, 3, 4, 4), f32) * 0.1, 'stem_b': jax.random.normal(ks[2], (96,), f32) * 0.05, 'bn1_g': jax.random.uniform(ks[3], (96,), f32, 0.5, 1.5), 'bn1_b': jax.random.normal(ks[4], (96,), f32) * 0.05, 'bn1_m': jax.random.normal(ks[5], (96,), f32) * 0.05, 'bn1_v': jax.random.uniform(ks[6], (96,), f32, 0.5, 1.5), 'off_w': jax.random.normal(ks[7], (32, 96, 4, 4), f32) * 0.02, 'off_b': jax.random.normal(ks[8], (32,), f32) * 0.02, 'dcn_w': jax.random.normal(ks[9], (192, 96, 4, 4), f32) * 0.05, 'dcn_b': jax.random.normal(ks[10], (192,), f32) * 0.05, 'bn2_g': jax.random.uniform(ks[11], (192,), f32, 0.5, 1.5), 'bn2_b': jax.random.normal(ks[12], (192,), f32) * 0.05, 'bn2_m': jax.random.normal(ks[13], (192,), f32) * 0.05, 'bn2_v': jax.random.uniform(ks[14], (192,), f32, 0.5, 1.5)}
        return inp
    _L0_tok_all = _L0_tok_setup()
    _L0_tok_in = {k: v for k, v in _L0_tok_all.items() if k in ('stem_w', 'stem_b', 'bn1_g', 'bn1_b', 'bn1_m', 'bn1_v', 'off_w', 'off_b', 'dcn_w', 'dcn_b', 'bn2_g', 'bn2_b', 'bn2_m', 'bn2_v')}
    del _L0_tok_all

    def _L0_attn_setup():
        import jax, jax.numpy as jnp
        import numpy as np
        B, N, C = (8, 256, 192)
        H = 12
        D = C // H
        SCALE = D ** (-0.5)
        EPS = 1e-05

        def _layer_norm(x):
            mean = x.mean(-1, keepdims=True)
            var = ((x - mean) ** 2).mean(-1, keepdims=True)
            return (x - mean) / jnp.sqrt(var + EPS)
        key = jax.random.key(seed)
        k1, k2, k3 = jax.random.split(key, 3)
        x = jax.random.normal(k1, (B, N, C), dtype=jnp.float32)
        qkv_weight = jax.random.normal(k2, (3 * C, C), dtype=jnp.float32) * C ** (-0.5)
        proj_weight = jax.random.normal(k3, (C, C), dtype=jnp.float32) * C ** (-0.5)
        return {'x': x, 'qkv_weight': qkv_weight, 'proj_weight': proj_weight}
    _L0_attn_all = _L0_attn_setup()
    _L0_attn_in = {k: v for k, v in _L0_attn_all.items() if k in ('qkv_weight', 'proj_weight')}
    del _L0_attn_all

    def _L0_ffn_setup():
        import jax, jax.numpy as jnp
        import numpy as np
        QN, QP = (-8, 7)

        def round_pass(x):
            return x + jax.lax.stop_gradient(jnp.round(x) - x)

        def _quant_act(x, alpha_a):
            a = alpha_a.mean()
            return round_pass(jnp.clip(x / a, QN, QP))

        def _quant_w(w, alpha_w):
            return round_pass(jnp.clip(w / alpha_w[:, None], QN, QP))
        key = jax.random.key(seed)
        ks = jax.random.split(key, 9)
        B, S, D, H = (16, 256, 192, 768)

        def unif(k, shape):
            return jax.random.uniform(k, shape, jnp.float32, 0.02, 0.1)
        return {'x0': jax.random.normal(ks[0], (B, S, D), jnp.float32), 'w1': jax.random.normal(ks[1], (H, D), jnp.float32) * 0.02, 'b1': jax.random.normal(ks[2], (H,), jnp.float32) * 0.02, 'alpha_w1': unif(ks[3], (H,)), 'alpha_a1': unif(ks[4], (D,)), 'w2': jax.random.normal(ks[5], (D, H), jnp.float32) * 0.02, 'b2': jax.random.normal(ks[6], (D,), jnp.float32) * 0.02, 'alpha_w2': unif(ks[7], (D,)), 'alpha_a2': unif(ks[8], (H,))}
    _L0_ffn_all = _L0_ffn_setup()
    _L0_ffn_in = {k: v for k, v in _L0_ffn_all.items() if k in ('w1', 'b1', 'alpha_w1', 'alpha_a1', 'w2', 'b2', 'alpha_w2', 'alpha_a2')}
    del _L0_ffn_all

    def _L1_attn_setup():
        import jax, jax.numpy as jnp
        import numpy as np
        D_MODEL = 192
        NHEAD = 12
        HEAD_DIM = D_MODEL // NHEAD
        MAX_REL = 16
        B, T = (4, 256)
        key = jax.random.key(seed)
        ks = jax.random.split(key, 6)
        s = 0.02
        return {'x': jax.random.normal(ks[0], (B, T, D_MODEL), dtype=jnp.float32), 'qkv_w': jax.random.normal(ks[1], (3 * D_MODEL, D_MODEL), dtype=jnp.float32) * s, 'qkv_b': jax.random.normal(ks[2], (3 * D_MODEL,), dtype=jnp.float32) * s, 'out_w': jax.random.normal(ks[3], (D_MODEL, D_MODEL), dtype=jnp.float32) * s, 'out_b': jax.random.normal(ks[4], (D_MODEL,), dtype=jnp.float32) * s, 'rel_pos_emb': jax.random.normal(ks[5], (2 * MAX_REL + 1, HEAD_DIM), dtype=jnp.float32)}
    _L1_attn_all = _L1_attn_setup()
    _L1_attn_in = {k: v for k, v in _L1_attn_all.items() if k in ('qkv_w', 'qkv_b', 'out_w', 'out_b', 'rel_pos_emb')}
    del _L1_attn_all

    def _L1_ffn_setup():
        import jax, jax.numpy as jnp
        import numpy as np
        B, S, D, F, E = (4, 512, 192, 768, 8)
        key = jax.random.key(seed)
        ks = jax.random.split(key, 5)
        return {'x': jax.random.normal(ks[0], (B, S, D), dtype=jnp.float32), 'Ws': jax.random.normal(ks[1], (D, E), dtype=jnp.float32) * 0.02, 'bs': jnp.zeros((E,), dtype=jnp.float32), 'W1': jax.random.normal(ks[2], (E, D, F), dtype=jnp.float32) * 0.02, 'b1': jnp.zeros((E, F), dtype=jnp.float32), 'W2': jax.random.normal(ks[3], (E, F, D), dtype=jnp.float32) * 0.02, 'b2': jnp.zeros((E, D), dtype=jnp.float32)}
    _L1_ffn_all = _L1_ffn_setup()
    _L1_ffn_in = {k: v for k, v in _L1_ffn_all.items() if k in ('Ws', 'bs', 'W1', 'b1', 'W2', 'b2')}
    del _L1_ffn_all
    return {'x': x, 'cls_tok': cls_tok, 'L0_tok_stem_w': _L0_tok_in['stem_w'], 'L0_tok_stem_b': _L0_tok_in['stem_b'], 'L0_tok_bn1_g': _L0_tok_in['bn1_g'], 'L0_tok_bn1_b': _L0_tok_in['bn1_b'], 'L0_tok_bn1_m': _L0_tok_in['bn1_m'], 'L0_tok_bn1_v': _L0_tok_in['bn1_v'], 'L0_tok_off_w': _L0_tok_in['off_w'], 'L0_tok_off_b': _L0_tok_in['off_b'], 'L0_tok_dcn_w': _L0_tok_in['dcn_w'], 'L0_tok_dcn_b': _L0_tok_in['dcn_b'], 'L0_tok_bn2_g': _L0_tok_in['bn2_g'], 'L0_tok_bn2_b': _L0_tok_in['bn2_b'], 'L0_tok_bn2_m': _L0_tok_in['bn2_m'], 'L0_tok_bn2_v': _L0_tok_in['bn2_v'], 'L0_attn_qkv_weight': _L0_attn_in['qkv_weight'], 'L0_attn_proj_weight': _L0_attn_in['proj_weight'], 'L0_ffn_w1': _L0_ffn_in['w1'], 'L0_ffn_b1': _L0_ffn_in['b1'], 'L0_ffn_alpha_w1': _L0_ffn_in['alpha_w1'], 'L0_ffn_alpha_a1': _L0_ffn_in['alpha_a1'], 'L0_ffn_w2': _L0_ffn_in['w2'], 'L0_ffn_b2': _L0_ffn_in['b2'], 'L0_ffn_alpha_w2': _L0_ffn_in['alpha_w2'], 'L0_ffn_alpha_a2': _L0_ffn_in['alpha_a2'], 'L1_attn_qkv_w': _L1_attn_in['qkv_w'], 'L1_attn_qkv_b': _L1_attn_in['qkv_b'], 'L1_attn_out_w': _L1_attn_in['out_w'], 'L1_attn_out_b': _L1_attn_in['out_b'], 'L1_attn_rel_pos_emb': _L1_attn_in['rel_pos_emb'], 'L1_ffn_Ws': _L1_ffn_in['Ws'], 'L1_ffn_bs': _L1_ffn_in['bs'], 'L1_ffn_W1': _L1_ffn_in['W1'], 'L1_ffn_b1': _L1_ffn_in['b1'], 'L1_ffn_W2': _L1_ffn_in['W2'], 'L1_ffn_b2': _L1_ffn_in['b2']}

def reference(x, cls_tok, L0_tok_stem_w, L0_tok_stem_b, L0_tok_bn1_g, L0_tok_bn1_b, L0_tok_bn1_m, L0_tok_bn1_v, L0_tok_off_w, L0_tok_off_b, L0_tok_dcn_w, L0_tok_dcn_b, L0_tok_bn2_g, L0_tok_bn2_b, L0_tok_bn2_m, L0_tok_bn2_v, L0_attn_qkv_weight, L0_attn_proj_weight, L0_ffn_w1, L0_ffn_b1, L0_ffn_alpha_w1, L0_ffn_alpha_a1, L0_ffn_w2, L0_ffn_b2, L0_ffn_alpha_w2, L0_ffn_alpha_a2, L1_attn_qkv_w, L1_attn_qkv_b, L1_attn_out_w, L1_attn_out_b, L1_attn_rel_pos_emb, L1_ffn_Ws, L1_ffn_bs, L1_ffn_W1, L1_ffn_b1, L1_ffn_W2, L1_ffn_b2):
    import jax
    import jax.numpy as jnp

    def _L0_tok_ref(x, stem_w, stem_b, bn1_g, bn1_b, bn1_m, bn1_v, off_w, off_b, dcn_w, dcn_b, bn2_g, bn2_b, bn2_m, bn2_v):
        import jax, jax.numpy as jnp
        import numpy as np
        K = 4
        STRIDE = 4
        EPS = 1e-05
        SLOPE = 0.01

        def conv2d(x, w, b, stride):
            out = jax.lax.conv_general_dilated(x, w, (stride, stride), 'VALID', dimension_numbers=('NCHW', 'OIHW', 'NCHW'))
            return out + b[None, :, None, None]

        def batchnorm(x, g, b, m, v):
            inv = g / jnp.sqrt(v + EPS)
            return x * inv[None, :, None, None] + (b - m * inv)[None, :, None, None]

        def leaky_relu(x):
            return jnp.where(x >= 0, x, SLOPE * x)

        def deform_conv(x, offset, w, b):
            B, C, H, W = x.shape
            Ho, Wo = (offset.shape[2], offset.shape[3])
            KK = K * K
            off = offset.reshape(B, KK, 2, Ho, Wo)
            kh = jnp.repeat(jnp.arange(K), K).astype(x.dtype)
            kw = jnp.tile(jnp.arange(K), K).astype(x.dtype)
            base_y = (jnp.arange(Ho) * STRIDE).astype(x.dtype)
            base_x = (jnp.arange(Wo) * STRIDE).astype(x.dtype)
            py = base_y[None, None, :, None] + kh[None, :, None, None] + off[:, :, 0]
            px = base_x[None, None, None, :] + kw[None, :, None, None] + off[:, :, 1]
            y0 = jnp.floor(py)
            x0 = jnp.floor(px)
            wy = py - y0
            wx = px - x0

            def corner(yc, xc):
                yi = yc.astype(jnp.int32)
                xi = xc.astype(jnp.int32)
                valid = (yi >= 0) & (yi < H) & (xi >= 0) & (xi < W)
                yi = jnp.clip(yi, 0, H - 1)
                xi = jnp.clip(xi, 0, W - 1)
                v = jax.vmap(lambda img, a, c: img[:, a, c])(x, yi, xi)
                return v * valid[:, None].astype(x.dtype)
            v00 = corner(y0, x0)
            v01 = corner(y0, x0 + 1)
            v10 = corner(y0 + 1, x0)
            v11 = corner(y0 + 1, x0 + 1)
            wy_ = wy[:, None]
            wx_ = wx[:, None]
            sampled = v00 * (1 - wy_) * (1 - wx_) + v01 * (1 - wy_) * wx_ + v10 * wy_ * (1 - wx_) + v11 * wy_ * wx_
            out = jnp.einsum('bckhw,ock->bohw', sampled, w.reshape(w.shape[0], C, KK))
            return out + b[None, :, None, None]
        h = conv2d(x, stem_w, stem_b, 4)
        h = leaky_relu(batchnorm(h, bn1_g, bn1_b, bn1_m, bn1_v))
        offset = conv2d(h, off_w, off_b, 4)
        h = deform_conv(h, offset, dcn_w, dcn_b)
        h = leaky_relu(batchnorm(h, bn2_g, bn2_b, bn2_m, bn2_v))
        B, C, Ho, Wo = h.shape
        return h.reshape(B, C, Ho * Wo).transpose(0, 2, 1)

    def _L0_attn_ref(x, qkv_weight, proj_weight):
        import jax, jax.numpy as jnp
        import numpy as np
        B, N, C = (8, 256, 192)
        H = 12
        D = C // H
        SCALE = D ** (-0.5)
        EPS = 1e-05

        def _layer_norm(x):
            mean = x.mean(-1, keepdims=True)
            var = ((x - mean) ** 2).mean(-1, keepdims=True)
            return (x - mean) / jnp.sqrt(var + EPS)
        Bx, Nx, Cx = x.shape
        qkv = x @ qkv_weight.T
        qkv = qkv.reshape(Bx, Nx, 3, H, D).transpose(2, 0, 3, 1, 4)
        q, k, v = (qkv[0], qkv[1], qkv[2])
        q = _layer_norm(q) * SCALE
        k = _layer_norm(k)
        attn = jnp.einsum('bhnd,bhmd->bhnm', q, k)
        attn = jax.nn.softmax(attn, axis=-1)
        out = jnp.einsum('bhnm,bhmd->bhnd', attn, v)
        out = out.transpose(0, 2, 1, 3).reshape(Bx, Nx, Cx)
        return out @ proj_weight.T

    def _L0_ffn_ref(x0, w1, b1, alpha_w1, alpha_a1, w2, b2, alpha_w2, alpha_a2):
        import jax, jax.numpy as jnp
        import numpy as np
        QN, QP = (-8, 7)

        def round_pass(x):
            return x + jax.lax.stop_gradient(jnp.round(x) - x)

        def _quant_act(x, alpha_a):
            a = alpha_a.mean()
            return round_pass(jnp.clip(x / a, QN, QP))

        def _quant_w(w, alpha_w):
            return round_pass(jnp.clip(w / alpha_w[:, None], QN, QP))
        xq = _quant_act(x0, alpha_a1)
        wq1 = _quant_w(w1, alpha_w1)
        x1 = jnp.einsum('bsd,hd->bsh', xq, wq1)
        x1 = x1 * alpha_w1 * alpha_a1.mean() + b1
        x1 = jax.nn.gelu(x1, approximate=False)
        x1 = jnp.clip(x1, -10.0, 10.0)
        hq = _quant_act(x1, alpha_a2)
        wq2 = _quant_w(w2, alpha_w2)
        x2 = jnp.einsum('bsh,dh->bsd', hq, wq2)
        x2 = x2 * alpha_w2 * alpha_a2.mean() + b2
        return x2

    def _L1_attn_ref(x, qkv_w, qkv_b, out_w, out_b, rel_pos_emb):
        import jax, jax.numpy as jnp
        import numpy as np
        D_MODEL = 192
        NHEAD = 12
        HEAD_DIM = D_MODEL // NHEAD
        MAX_REL = 16
        B, T = (4, 256)
        Bx, Tx, _ = x.shape
        scale = HEAD_DIM ** (-0.5)
        qkv = x @ qkv_w.T + qkv_b
        qkv = qkv.reshape(Bx, Tx, 3, NHEAD, HEAD_DIM)
        q = qkv[:, :, 0].transpose(0, 2, 1, 3)
        k = qkv[:, :, 1].transpose(0, 2, 1, 3)
        v = qkv[:, :, 2].transpose(0, 2, 1, 3)
        attn_scores = jnp.einsum('bhtd,bhsd->bhts', q, k)
        rng = jnp.arange(Tx)
        rel_pos = jnp.clip(rng[None, :] - rng[:, None], -MAX_REL, MAX_REL) + MAX_REL
        rel_emb = rel_pos_emb[rel_pos]
        rel_scores = jnp.einsum('bhtd,tsd->bhts', q, rel_emb)
        attn = jax.nn.softmax((attn_scores + rel_scores) * scale, axis=-1)
        out = jnp.einsum('bhts,bhsd->bhtd', attn, v)
        out = out.transpose(0, 2, 1, 3).reshape(Bx, Tx, D_MODEL)
        return out @ out_w.T + out_b

    def _L1_ffn_ref(x, Ws, bs, W1, b1, W2, b2):
        import jax, jax.numpy as jnp
        import numpy as np
        B, S, D, F, E = (4, 512, 192, 768, 8)
        b, s, d = x.shape
        xt = x.reshape(-1, d)
        logits = xt @ Ws + bs
        probs = jax.nn.softmax(logits, axis=-1)
        routes = jnp.argmax(probs, axis=-1)
        prob_max = jnp.max(probs, axis=-1)
        h = jax.nn.gelu(jnp.einsum('td,edf->etf', xt, W1) + b1[:, None, :], approximate=False)
        y = jnp.einsum('etf,efd->etd', h, W2) + b2[:, None, :]
        out = jnp.take_along_axis(y, routes[None, :, None], axis=0)[0]
        out = out * prob_max[:, None]
        return out.reshape(b, s, d)
    h = _L0_tok_ref(x, L0_tok_stem_w, L0_tok_stem_b, L0_tok_bn1_g, L0_tok_bn1_b, L0_tok_bn1_m, L0_tok_bn1_v, L0_tok_off_w, L0_tok_off_b, L0_tok_dcn_w, L0_tok_dcn_b, L0_tok_bn2_g, L0_tok_bn2_b, L0_tok_bn2_m, L0_tok_bn2_v)
    h = jnp.concatenate([jnp.broadcast_to(cls_tok, (h.shape[0], 1, h.shape[2])), h], axis=1)
    h = h + _L0_attn_ref(_layernorm(h, axis=-1), L0_attn_qkv_weight, L0_attn_proj_weight)
    h = h + _L0_ffn_ref(_layernorm(h, axis=-1), L0_ffn_w1, L0_ffn_b1, L0_ffn_alpha_w1, L0_ffn_alpha_a1, L0_ffn_w2, L0_ffn_b2, L0_ffn_alpha_w2, L0_ffn_alpha_a2)
    h = h + _L1_attn_ref(_layernorm(h, axis=-1), L1_attn_qkv_w, L1_attn_qkv_b, L1_attn_out_w, L1_attn_out_b, L1_attn_rel_pos_emb)
    h = h + _L1_ffn_ref(_layernorm(h, axis=-1), L1_ffn_Ws, L1_ffn_bs, L1_ffn_W1, L1_ffn_b1, L1_ffn_W2, L1_ffn_b2)
    return h

_drawn_inputs = setup_inputs


def setup_inputs(seed=0):
    import zlib

    import numpy as np

    out = dict(_drawn_inputs(seed))
    spreads = {'L1_ffn_bs': (0.0, 0.502), 'L1_ffn_b1': (0.0, 0.8), 'L1_ffn_b2': (0.0, 0.449)}
    factors = {'L0_ffn_b1': 5.081,
     'L0_ffn_alpha_w1': 2.736,
     'L0_ffn_alpha_a1': 8.0,
     'L0_ffn_alpha_a2': 64.0,
     'L1_attn_qkv_b': 8.0,
     'L1_attn_out_b': 2.722,
     'L1_attn_rel_pos_emb': 8.0,
     'L1_ffn_W1': 3.782,
     'L1_ffn_W2': 3.552}
    for name, (base, spread) in spreads.items():
        noise = np.random.default_rng([zlib.crc32(name.encode()), seed]).standard_normal(out[name].shape)
        drawn = base * np.exp(spread * noise) if base else spread * noise
        out[name] = jnp.asarray(drawn.astype(out[name].dtype))
    for name, factor in factors.items():
        out[name] = (out[name] * factor).astype(out[name].dtype)
    return out
```

```python
import numpy as np
import concourse.bass as bass
from concourse import mybir
from contextlib import ExitStack

F32 = mybir.dt.float32
BF16 = mybir.dt.bfloat16
U32 = mybir.dt.uint32
I32 = mybir.dt.int32
ALU = mybir.AluOpType
ACT = mybir.ActivationFunctionType
AX = mybir.AxisListType

B, CIN, IMG = 64, 3, 84
KP = 4
G1 = IMG // KP
PIX = G1 * G1
G2 = (G1 - KP) // KP + 1
POS = G2 * G2
TOK = POS + 1
TAPS = KP * KP
C1, D = 96, 192
IPT = 4
NT = B // IPT
TT = IPT * TOK
TP = IPT * POS
PK = 111
NK = 4
PIXP = NK * PK
H, DH = 12, 16
KC = 96
FF, FM = 768, 6
E = 8
NREL, MAXREL = 2 * TOK - 1, 16
NS = (B * TOK + E * 127) // 128
EPS = 1e-5
SLOPE = 0.01
MAGIC = 12582912.0


def view(ap, dims, off=0, whole=False):
    return bass.AP(ap.tensor, ap.offset + off, ([] if whole else [list(ap.ap[0])]) + [list(d) for d in dims])


def build(nc, io, out, debug_stage=None):
    ctx = ExitStack()
    with ctx:
        def sb(name, shape, dt=F32, scope=ctx):
            return scope.enter_context(nc.sbuf_tensor(name, shape, dt))

        def sem(name):
            return ctx.enter_context(nc.semaphore(name))

        psum = ctx.enter_context(nc.psum_tensor("psum", [128, 8, 512], F32))
        bank = [psum[:, i, :] for i in range(8)]

        ident = sb("ident", [128, 128])
        eps = sb("eps", [128, D])
        mhalf = sb("mhalf", [128, D])

        h = sb("h", [TT, NT, D])

        wqkv = [sb(f"wqkv{l}", [KC + 1, 2, 3 * D]) for l in range(2)]
        wproj = [sb(f"wproj{l}", [KC + 1, 2, D]) for l in range(2)]
        mask = sb("mask", [TT, IPT])
        epsdh = sb("epsdh", [TT, 2 * H])
        maskdh = sb("maskdh", [TT, IPT])
        sel = sb("sel", [TT, TOK])
        wq1 = sb("wq1", [KC, 2, FF], BF16)
        wq2 = sb("wq2", [128, FM, D], BF16)
        s1 = sb("s1", [128, FM])
        fb1 = sb("fb1", [128, FM])
        row2 = sb("row2", [TT, D])
        fb2 = sb("fb2", [TT, D])
        am = sb("am", [128, 2])
        ram = sb("ram", [128, 2])
        identb = sb("identb", [128, 128], BF16)
        tri = sb("tri", [TT, 2, TT])
        rev = sb("rev", [TT, E])
        upto = sb("upto", [TT, E, E])
        tidx = sb("tidx", [1, NS])
        ones = sb("ones", [1, 128])
        zeros = sb("zeros", [128, D])
        tick = sb("tick", [1, 1])

        wr = sb("wr", [KC + 1, 2, E])

        tk = ExitStack()
        iota21 = sb("iota21", [TP, G1], scope=tk)
        base = sb("base", [TP, 2 * TAPS], scope=tk)
        off_bias = sb("off_bias", [TP, 2 * TAPS], scope=tk)
        posbase = sb("posbase", [TP, 2 * TAPS], scope=tk)
        notcls = sb("notcls", [1, TT], scope=tk)
        clsmat = sb("clsmat", [TT, D], scope=tk)
        wstem = sb("wstem", [49, C1], scope=tk)
        bn1 = sb("bn1", [49, 4, C1], scope=tk)
        inv1 = sb("inv1", [49, C1], scope=tk)
        shift1 = sb("shift1", [1, C1], scope=tk)
        woff = sb("woff", [C1, TAPS, 2 * TAPS], scope=tk)
        wdcn = sb("wdcn", [C1, TAPS, D], scope=tk)
        bn2 = sb("bn2", [C1, 5, D], scope=tk)
        inv2 = sb("inv2", [C1, D], scope=tk)
        shift2 = sb("shift2", [1, D], scope=tk)
        xcol = [sb(f"xcol{u}", [49, IPT, PIXP], scope=tk) for u in range(2)]
        leak = [sb(f"leak{i}", [PK, NK * C1], scope=tk) for i in range(2)]
        hpix = [sb(f"hpix{u}", [PK, IPT, NK, C1], scope=tk) for u in range(2)]
        hch = sb("hch", [C1, TAPS, TP], scope=tk)
        pxy = sb("pxy", [TP, 2 * TAPS], scope=tk)
        dist = sb("dist", [TP, 2 * TAPS, G1], scope=tk)
        tent = sb("tent", [TP, 2 * TAPS, G1], scope=tk)
        wmap = [sb(f"wmap{i}", [TP, PIXP], scope=tk) for i in range(4)]
        wmapT = [sb(f"wmapT{u}", [PK, NK, TAPS, TP], scope=tk) for u in range(2)]
        samp = sb("samp", [C1, TAPS, IPT, TOK], scope=tk)
        dleak = sb("dleak", [TT, D], scope=tk)
        dmax = sb("dmax", [TT, D], scope=tk)

        tk.close()

        w1 = sb("w1", [KC + 1, E, 2, FF])
        w2 = sb("w2", [128, E, FM, D])
        eb2 = sb("eb2", [1, E, D])
        blk = ExitStack()
        a2 = lambda name, shape, dt=F32: [sb(f"{name}{u}", shape, dt, scope=blk) for u in range(2)]
        stat = a2("stat", [TT, 6])
        mv = a2("mv", [TT, 2])
        rstd = a2("rstd", [TT, 1])
        xn = a2("xn", [TT, D])
        xT = a2("xT", [KC + 1, 2, TT])
        hsum = a2("hsum", [TT, 2 * H])
        hmean = a2("hmean", [TT, 2 * H])
        hvar = a2("hvar", [TT, 2 * H])
        cen = a2("cen", [TT, 2 * H, DH])
        qmask = a2("qmask", [TT, 2 * H, IPT])
        qkx = a2("qkx", [128, 2, H, IPT, DH])
        qx = [qkx[u][:TT, 0] for u in range(2)]
        kx = [qkx[u][:TT, 1] for u in range(2)]
        qT = a2("qT", [128, H // 2, TT])
        ke = a2("ke", [128, H // 2, TOK + NREL])
        vsb = a2("vsb", [TT, D])
        se = a2("se", [TT, 2, H // 2 * (TOK + NREL)])
        rel = a2("rel", [TT, H, TOK])
        sc = a2("sc", [TT, H, TOK])
        smax = a2("smax", [TT, H])
        prob = a2("prob", [TT, H, TOK])
        rsum = a2("rsum", [TT, H])
        pmask = a2("pmask", [TT, H, IPT])
        px = a2("px", [TT, H, TT])
        pT = [view(qkx[u][:TT], [[TT, H], [1, TT]]) for u in range(2)]
        osb = a2("osb", [TT, D])
        oT = a2("oT", [KC + 1, 2, TT])
        bmask = sb("bmask", [TT, 2 * H, IPT], scope=blk)
        raw1 = sb("raw1", [KC, 2, FF], scope=blk)
        raw2 = sb("raw2", [128, FM, D], scope=blk)
        alw1 = sb("alw1", [KC, FF], scope=blk)
        alw1c = sb("alw1c", [128, FM], scope=blk)
        alw2 = sb("alw2", [128, D], scope=blk)
        ala1 = sb("ala1", [128, D], scope=blk)
        ala2 = sb("ala2", [128, FF], scope=blk)
        xq = a2("xq", [TT, D], BF16)
        xqT = sb("xqT", [KC, 2, IPT * TT], BF16, scope=blk)
        gel = a2("gel", [128, IPT * TT])
        hq = view(qkx[0][:].bitcast(BF16), [[IPT * TT, FM], [1, IPT * TT]])
        f2 = osb
        blk.close()

        moe = ctx
        m2 = lambda name, shape, dt=F32: [sb(f"{name}{u}", shape, dt) for u in range(2)]
        mstat = m2("mstat", [TT, 6])
        mmv = m2("mmv", [TT, 2])
        mrstd = m2("mrstd", [TT, 1])
        mxn = sb("mxn", [TT, NT, D])
        mx1 = m2("mx1", [TT, D])
        mxT = m2("mxT", [KC + 1, 2, TT])
        lmax = m2("lmax", [TT, 1])
        lsh = m2("lsh", [TT, E])
        lex = m2("lex", [TT, E])
        lsum = m2("lsum", [TT, 1])
        cand = m2("cand", [TT, E])
        cmax = m2("cmax", [TT, 1])
        pmax = sb("pmax", [TT, NT])
        hot = sb("hot", [TT, NT, E])
        rank = sb("rank", [TT, NT, E])
        cnt = m2("cnt", [TT, E])
        ntile = sb("ntile", [TT, E])
        cum = sb("cum", [TT, E, E])
        ends = sb("ends", [TT, E])
        start = sb("start", [TT, E])
        slotw = sb("slotw", [TT, NT, E])
        slotf = sb("slotf", [TT, NT])
        slot = sb("slot", [TT, NT], U32)
        past = sb("past", [1, NS, E])
        own = sb("own", [1, NS])
        owner = sb("owner", [1, NS], I32)
        xg = m2("xg", [128, D])
        xgT = m2("xgT", [KC + 1, 2, 128])
        hid = m2("hid", [128, FF])
        hT = m2("hT", [128, FM, 128])
        yo = sb("yo", [128, NS, D])
        yg = sb("yg", [TT, NT, D])

        par_in = sem("par_in")
        x_in = [sem(f"x_in{u}") for u in range(2)]
        pool_const = sem("pool_const")
        bn_pow = sem("bn_pow")
        fold = sem("fold")
        par_ready = sem("par_ready")
        stem_ready = sem("stem_ready")
        leak_ready = sem("leak_ready")
        hpix_ready = sem("hpix_ready")
        tr_ready = sem("tr_ready")
        tr_evac = sem("tr_evac")
        off_ready = sem("off_ready")
        pxy_ready = sem("pxy_ready")
        dist_ready = sem("dist_ready")
        abs_ready = sem("abs_ready")
        tent_ready = sem("tent_ready")
        wmap_ready = sem("wmap_ready")
        samp_ready = sem("samp_ready")
        samp_evac = sem("samp_evac")
        dcn_ready = sem("dcn_ready")
        dleak_ready = sem("dleak_ready")
        dmax_ready = sem("dmax_ready")
        h0_ready = sem("h0_ready")
        out_done = sem("out_done")

        names = ("maskdh_ready wt_in moe_in ms_small attn_par quant_pool quant_dve ln_raw ln_stat ln_eps ln_rstd ln_norm xT_tr xT_evac "
                 "qkv_ready v_evac hs_ready hm_ready cen_ready sq_ready hv_ready hv_eps hrstd_ready qmask_ready "
                 "qx_ready kx_ready qT_tr kT_ready qT_evac ke_evac s_ready se_ready sr_ready smax_ready sc_ready "
                 "exp_ready rs_ready rr_ready pmask_ready px_ready pT_tr pT_evac o_ready o_evac oT_tr oT_evac "
                 "proj_ready hattn_ready "
                 "fq1 fq2 fq3 xqT_tr xqT_evac fh_ready gel_ready fc_done hq_ready f2_ready f2_scaled f2_sum hffn_ready "
                 "mxn_ready lg_ready lmax_ready lsh_ready lex_ready lsum_ready cand_ready candm_ready cmax_ready pmax_ready "
                 "hot_ready rk_ready rank_ready cnt_ready plan slot_ready owner_ready zero_in scat_done "
                 "hout xgT_tr xgT_evac hid_ready hgel_ready hT_tr hTa_evac hTb_evac y_ready y_evac gath_done").split()
        S = {k: sem(k) for k in names}
        qr_out = [sem(f"qr_out{u}") for u in range(2)]
        rel_in = [sem(f"rel_in{u}") for u in range(2)]
        xg_in = [sem(f"xg_in{u}") for u in range(2)]
        y_out = [sem(f"y_out{u}") for u in range(2)]

        TG = IPT + TAPS
        stem_ps = [bank[2], bank[3]]
        samp_ps = [bank[4], bank[5]]
        off_ps = bank[6][:TP, 0:2 * TAPS]
        dcn_ps = bank[7][:TT, 0:D]

        small = [(ident, "ident"), (iota21, "iota21"), (base, "base"), (off_bias, "off_b"), (notcls, "notcls"),
                 (wstem, "stem_rows"), (woff, "off_w"), (wdcn, "dcn_w")]
        NPAR = len(small) + 2 + IPT
        weights = [(wqkv[0], "qkv0"), (wqkv[1], "qkv1"), (wproj[0], "proj0"), (wproj[1], "proj1"), (mask, "mask"),
                   (sel, "sel"), (fb1, "f_b1"), (fb2, "f_b2"), (tri, "tri"), (rev, "rev"), (upto, "upto"),
                   (tidx, "tidx"), (wr, "router")]
        NW = len(weights)
        late = [(bmask, "bmask"), (raw1, "f_w1"), (raw2, "f_w2"), (alw1, "f_aw1"), (alw1c, "f_aw1c"), (alw2, "f_aw2"),
                (ala1, "f_aa1"), (ala2, "f_aa2")]
        NL = len(late) + 2
        NQ = IPT * (TOK * H * NREL)
        scr = nc.dram_tensor("rel_scratch", [NT, NQ], F32).ap()
        xs = nc.dram_tensor("slots_in", [NS * 128, D], F32).ap()
        ys = nc.dram_tensor("slots_out", [NS * 128, D], F32).ap()

        def bcast(name, dst):
            src = io[name]
            if src.shape[0] == 1 and dst.shape[0] > 1:
                n = int(np.prod(src.shape))
                return bass.AP(src.tensor, 0, [[0, dst.shape[0]], [1, n]])
            return src

        FINAL = NT
        block = ctx.enter_context(nc.Block())

        def load_x(eng, t, u):
            eng.dma_start(xcol[u][1:49, :, :], io["xcol"][bass.ds(t, 1), :, :, :]).then_inc(x_in[u], 16)

        @block.sync
        def _(sp):
            for dst, name in small:
                src = io[name]
                if name == "off_b":
                    src = bass.AP(src.tensor, src.offset, [[0, TP], [1, 2 * TAPS]])
                sp.dma_start(dst[:], src).then_inc(par_in, 16)
            sp.dma_start(bn1[:], bass.AP(io["bn1"].tensor, 0, [[0, 49], [1, 4 * C1]])).then_inc(par_in, 16)
            sp.dma_start(bn2[:], bass.AP(io["bn2"].tensor, 0, [[0, C1], [1, 5 * D]])).then_inc(par_in, 16)
            sp.wait_ge(pool_const, 4)
            for i in range(IPT):
                sp.dma_start(clsmat[TOK * i:TOK * i + 1, :], io["cls"]).then_inc(par_in, 16)
            load_x(sp, 0, 0)
            load_x(sp, 1, 1)
            sp.wait_ge(stem_ready, IPT)
            load_x(sp, 2, 0)
            with sp.Fori(1, NT - 3, 2) as t1:
                for u in (1, 0):
                    t = t1 + (1 - u)
                    sp.wait_ge(stem_ready, IPT * t + IPT)
                    load_x(sp, t + 2, u)
            sp.wait_ge(stem_ready, IPT * (NT - 3) + IPT)
            load_x(sp, NT - 1, 1)
            for dst, name in weights:
                sp.dma_start(dst[:], bcast(name, dst)).then_inc(S["wt_in"], 16)
            sp.wait_ge(S["ms_small"], 2)
            sp.dma_start(xs.rearrange("(j p) d -> p j d", p=128), view(zeros[:], [[0, NS], [1, D]])).then_inc(S["zero_in"], 16)
            sp.wait_ge(h0_ready, NT)
            for dst, name in late:
                sp.dma_start(dst[:], bcast(name, dst)).then_inc(S["attn_par"], 16)
            for u in range(2):
                sp.dma_start(ke[u][:, :, TOK:], io["rel_emb"]).then_inc(S["attn_par"], 16)
            for dst, name in ((w1, "e_w1"), (w2, "e_w2"), (eb2, "e_b2")):
                sp.dma_start(dst[:], io[name]).then_inc(S["moe_in"], 16)
            with sp.Fori(0, NT - 1, 2) as t0:
                for u in range(2):
                    t = t0 + u
                    sp.wait_ge(S["se_ready"], t + 1)
                    sp.dma_start(view(scr[bass.ds(t, 1), :], [[H * NREL, TT], [NREL, H], [1, NREL]], whole=True),
                                 view(se[u][:], [[TOK + NREL, H], [1, NREL]], TOK)).then_inc(qr_out[u], 16)
                for u in range(2):
                    t = t0 + u
                    sp.wait_ge(qr_out[u], 8 * t0 + 16)
                    for i in range(IPT):
                        sp.dma_start(rel[u][TOK * i:TOK * i + TOK, :, :],
                                     view(scr[bass.ds(t, 1), :], [[H * NREL - 1, TOK], [NREL, H], [1, TOK]],
                                          i * TOK * H * NREL + TOK - 1, whole=True)).then_inc(rel_in[u], 16)
            sp.wait_ge(S["scat_done"], 16 * NT)
            for j in range(2):
                sp.dma_start(xg[j][:], xs[128 * j:128 * j + 128, :]).then_inc(xg_in[j], 16)
            with sp.Fori(0, NS - 3, 2) as j0:
                for u in range(2):
                    sp.wait_ge(S["xgT_tr"], j0 + u + 1)
                    sp.dma_start(xg[u][:], xs[bass.ds((j0 + u + 2) * 128, 128), :]).then_inc(xg_in[u], 16)
                for u in range(2):
                    sp.wait_ge(S["y_evac"], j0 + u + 3)
                    sp.dma_start(ys[bass.ds((j0 + u) * 128, 128), :], yo[:, bass.ds(j0 + u, 1), :]).then_inc(y_out[u], 16)
            for u in range(2):
                sp.wait_ge(S["y_evac"], NS + u + 1)
                sp.dma_start(ys[(NS - 2 + u) * 128:(NS - 1 + u) * 128, :], yo[:, NS - 2 + u, :]).then_inc(y_out[u], 16)
            sp.wait_ge(S["hout"], FINAL)
            for i in range(IPT):
                sp.dma_start(out.rearrange("(t i) n d -> i n t d", i=IPT)[i], h[TOK * i:TOK * i + TOK, :, :]).then_inc(out_done, 16)
            sp.wait_ge(out_done, 16 * IPT)

        @block.gpsimd
        def _(pool):
            g = nc.gpsimd
            g.memset(eps[:], EPS).then_inc(pool_const, 1)
            g.memset(mhalf[:], -0.5).then_inc(pool_const, 1)
            g.memset(samp[:], 0.0).then_inc(pool_const, 1)
            g.memset(clsmat[:], 0.0).then_inc(pool_const, 1)
            for u in range(2):
                g.memset(xcol[u][0:1, :, :], 1.0).then_inc(pool_const, 1)
            for i in range(4):
                g.memset(wmap[i][:, PIX:PIXP], 0.0).then_inc(pool_const, 1)
            pool.wait_ge(pool_const, 10)
            pool.wait_ge(par_in, 16 * NPAR)
            g.tensor_tensor(inv1[:], bn1[:, 3, :], eps[:49, 0:C1], ALU.add).then_inc(bn_pow, 1)
            g.tensor_tensor(inv2[:], bn2[:, 3, :], eps[:C1, :], ALU.add).then_inc(bn_pow, 1)
            pool.wait_ge(bn_pow, 2)
            g.tensor_tensor(inv1[:], inv1[:], mhalf[:49, 0:C1], ALU.pow).then_inc(bn_pow, 1)
            g.tensor_tensor(inv2[:], inv2[:], mhalf[:C1, :], ALU.pow).then_inc(bn_pow, 1)
            pool.wait_ge(bn_pow, 4)
            g.tensor_tensor(inv1[:], inv1[:], bn1[:, 0, :], ALU.mult).then_inc(bn_pow, 1)
            g.tensor_tensor(inv2[:], inv2[:], bn2[:, 0, :], ALU.mult).then_inc(bn_pow, 1)

            g.memset(zeros[:], 0.0).then_inc(S["ms_small"], 1)
            g.memset(ones[:], 1.0).then_inc(S["ms_small"], 1)
            pool.wait_ge(S["ms_small"], 2)

            def ln_root(i, t, u, mvt, rst):
                n = i * NT + t + 1
                pool.wait_ge(S["ln_stat"], n)
                g.tensor_tensor(rst[u][:], mvt[u][:, 1:2], eps[:TT, 0:1], ALU.add).then_inc(S["ln_eps"], 1)
                pool.wait_ge(S["ln_eps"], n)
                g.tensor_tensor(rst[u][:], rst[u][:], mhalf[:TT, 0:1], ALU.pow).then_inc(S["ln_rstd"], 1)

            pool.wait_ge(h0_ready, NT)
            for u in range(2):
                g.memset(xT[u][KC:KC + 1, :, :], 1.0).then_inc(S["ms_small"], 1)
                g.memset(oT[u][KC:KC + 1, :, :], 1.0).then_inc(S["ms_small"], 1)
            pool.wait_ge(S["ms_small"], 6)
            pool.wait_ge(S["wt_in"], 16 * NW)

            def attention(l):
                with pool.Fori(0, NT - 1, 2) as t0:
                    for u in range(2):
                        ln_root(2 * l, t0 + u, u, mv, rstd)
                    if l == 0:
                        for u in range(2):
                            n = t0 + u + 1
                            pool.wait_ge(S["hv_ready"], n)
                            g.tensor_tensor(hvar[u][:], hvar[u][:], epsdh[:], ALU.add).then_inc(S["hv_eps"], 1)
                            pool.wait_ge(S["hv_eps"], n)
                            g.tensor_tensor(hvar[u][:], hvar[u][:], mhalf[:TT, 0:2 * H], ALU.pow).then_inc(S["hrstd_ready"], 1)
                            pool.wait_ge(S["hrstd_ready"], n)
                            g.tensor_tensor(qmask[u][:], view(hvar[u][:], [[1, 2 * H], [0, IPT]]),
                                            view(maskdh[:], [[0, 2 * H], [1, IPT]]), ALU.mult).then_inc(S["qmask_ready"], 1)
                    for u in range(2):
                        n = l * NT + t0 + u + 1
                        if l == 0:
                            pool.wait_ge(S["qmask_ready"], n)
                        pool.wait_ge(S["cen_ready"], n)
                        m = (bmask if l else qmask[u])
                        g.tensor_tensor(kx[u], view(cen[u][:, H, :], [[DH, H], [0, IPT], [1, DH]]),
                                        view(m[:, H, :], [[IPT, H], [1, IPT], [0, DH]]), ALU.mult).then_inc(S["kx_ready"], 1)

            g.memset(epsdh[:], DH * EPS).then_inc(S["maskdh_ready"], 1)
            g.tensor_scalar(maskdh[:], mask[:], DH ** 0.5, None, ALU.mult).then_inc(S["maskdh_ready"], 1)
            pool.wait_ge(S["maskdh_ready"], 2)
            pool.wait_ge(S["attn_par"], 16 * NL)
            attention(0)

            pool.wait_ge(S["quant_dve"], 4)
            c = S["quant_pool"]
            for n, (raw, al, q) in enumerate(((raw1, view(alw1[:], [[0, 2], [1, FF]]), wq1),
                                              (raw2, view(alw2[:], [[0, FM], [1, D]]), wq2))):
                g.tensor_tensor(raw[:], raw[:], al, ALU.mult).then_inc(c, 1)
                pool.wait_ge(c, 4 * n + 1)
                g.tensor_scalar(raw[:], raw[:], -8.0, 7.0, ALU.max, ALU.min).then_inc(c, 1)
                pool.wait_ge(c, 4 * n + 2)
                g.tensor_scalar(raw[:], raw[:], MAGIC, None, ALU.add).then_inc(c, 1)
                pool.wait_ge(c, 4 * n + 3)
                g.tensor_scalar(q[:], raw[:], -MAGIC, None, ALU.add).then_inc(c, 1)

            with pool.Fori(0, NT - IPT + 1, IPT) as t0:
                for i in range(IPT):
                    ln_root(1, t0 + i, i % 2, mv, rstd)
            attention(1)

            pool.wait_ge(S["hattn_ready"], 2 * NT)
            for u in range(2):
                g.memset(mxT[u][KC:KC + 1, :, :], 1.0).then_inc(S["ms_small"], 1)
                g.memset(xgT[u][KC:KC + 1, :, :], 1.0).then_inc(S["ms_small"], 1)
            pool.wait_ge(S["ms_small"], 10)
            with pool.Fori(0, NT - 1, 2) as t0:
                for u in range(2):
                    ln_root(3, t0 + u, u, mmv, mrstd)
            pool.wait_ge(S["slot_ready"], 1)
            pool.wait_ge(S["mxn_ready"], NT)
            pool.wait_ge(S["zero_in"], 16)
            for t in range(NT):
                g.indirect_dma_start(out=xs, out_offset=bass.IndirectOffsetOnAxis(ap=slot[:, t:t + 1], axis=0),
                                     in_=mxn[:, t, :], in_offset=None).then_inc(S["scat_done"], 16)
            for u in range(2):
                pool.wait_ge(y_out[u], 16 * (NS // 2))
            for t in range(NT):
                g.indirect_dma_start(out=yg[:, t, :], out_offset=None, in_=ys,
                                     in_offset=bass.IndirectOffsetOnAxis(ap=slot[:, t:t + 1], axis=0)).then_inc(S["gath_done"], 16)

        @block.tensor
        def _(pe):
            mm = nc.tensor.matmul

            def front(t, u, first=False):
                pe.wait_ge(x_in[u], 16 if first else 8 * (t - u) + 16)
                for b in range(IPT):
                    if not (first and b < 2):
                        pe.wait_ge(hpix_ready, IPT * t + b - 1)
                    for k in range(NK):
                        m = mm(stem_ps[b % 2][:PK, k * C1:(k + 1) * C1], xcol[u][:, b, k * PK:(k + 1) * PK],
                               wstem[:, :], start=True, stop=True)
                    m.then_inc(stem_ready, 1)
                for b in range(IPT):
                    pe.wait_ge(hpix_ready, IPT * t + b + 1)
                    if not (first and b < 2):
                        pe.wait_ge(tr_evac, TG * t + b - 1)
                    for k in range(NK):
                        m = nc.tensor.transpose(bank[b % 2][:C1, k * PK:(k + 1) * PK], hpix[u][:, b, k, :],
                                                ident[:PK, :PK])
                    m.then_inc(tr_ready, 1)
                pe.wait_ge(tr_evac, TG * t + IPT)
                for k in range(TAPS):
                    m = mm(off_ps, hch[:, k, :], woff[:, k, :], start=(k == 0), stop=(k == TAPS - 1))
                m.then_inc(off_ready, 1)

            def turn_map(t, k):
                pe.wait_ge(wmap_ready, TAPS * t + k + 1)
                pe.wait_ge(tr_evac, TG * t + IPT + k - 1)
                for j in range(NK):
                    m = nc.tensor.transpose(bank[k % 2][:PK, j * TP:(j + 1) * TP],
                                            wmap[k % 4][:, j * PK:(j + 1) * PK], ident[:TP, :TP])
                m.then_inc(tr_ready, 1)

            def back(t, u, nxt):
                pe.wait_ge(tr_evac, TG * t + TG)
                for b in range(IPT):
                    if isinstance(t, int) and t == 0 and b < 2:
                        pass
                    else:
                        pe.wait_ge(samp_evac, IPT * t + b - 1)
                    for k in range(NK):
                        m = mm(samp_ps[b % 2][:C1, 0:TAPS * POS], hpix[u][:, b, k, :],
                               wmapT[u][:, k, :, b * POS:(b + 1) * POS], start=(k == 0), stop=(k == NK - 1))
                        if k == NK - 1:
                            m.then_inc(samp_ready, 1)
                        if nxt:
                            turn_map(t + 1, NK * b + k)
                pe.wait_ge(samp_evac, IPT * t + IPT)
                for k in range(TAPS):
                    mm(dcn_ps, view(samp[:, k, 0, 0:1], [[1, TT]]), wdcn[:, k, :], start=(k == 0), stop=False)
                mm(dcn_ps, notcls[:], shift2[:], start=False, stop=True).then_inc(dcn_ready, 1)

            pe.wait_ge(par_ready, 4)
            pe.wait_ge(pool_const, 10)
            front(0, 0, first=True)
            for k in range(TAPS):
                turn_map(0, k)
            front(1, 1)
            back(0, 0, True)
            with pe.Fori(1, NT - 1, 2) as t:
                for u in (1, 0):
                    front(t + (2 - u), 1 - u)
                    back(t + (1 - u), u, True)
            back(NT - 1, 1, False)

            tr = nc.tensor.transpose
            W = TOK + NREL
            pe.wait_ge(S["wt_in"], 16 * NW)
            pe.wait_ge(S["ms_small"], 6)

            def attention(l):
                with pe.Fori(0, NT - 1, 2) as t0:
                    w = W if l else TOK
                    for u in range(2):
                        n, b0 = l * NT + t0 + u + 1, bank[4 * u]
                        pe.wait_ge(S["ln_norm"], 2 * l * NT + t0 + u + 1)
                        for c in range(2):
                            m = tr(b0[:KC, c * TT:c * TT + TT], xn[u][:, c * KC:c * KC + KC], ident[:TT, :TT])
                        m.then_inc(S["xT_tr"], 1)
                    for u in range(2):
                        n, b1, b2 = l * NT + t0 + u + 1, bank[4 * u + 1], bank[4 * u + 2]
                        pe.wait_ge(S["xT_evac"], n)
                        for c in range(2):
                            mm(b1[:TT, 0:2 * D], xT[u][0:KC + c, c, :], wqkv[l][0:KC + c, c, 0:2 * D], start=(c == 0), stop=(c == 1))
                        for c in range(2):
                            m = mm(b2[:TT, 0:D], xT[u][0:KC + c, c, :], wqkv[l][0:KC + c, c, 2 * D:3 * D], start=(c == 0), stop=(c == 1))
                        m.then_inc(S["qkv_ready"], 1)
                    for u in range(2):
                        n, b0, b2, b3 = l * NT + t0 + u + 1, bank[4 * u], bank[4 * u + 2], bank[4 * u + 3]
                        pe.wait_ge(S["qx_ready"], n)
                        for p in range(H // 2):
                            m = tr((b3 if p > 2 else b0)[:, (p % 3) * TT:(p % 3 + 1) * TT],
                                   view(qx[u][:, 2 * p, :, :], [[1, 128]]), ident[:TT, :TT])
                        m.then_inc(S["qT_tr"], 1)
                        pe.wait_ge(S["kx_ready"], n)
                        pe.wait_ge(S["v_evac"], n)
                        for p in range(H // 2):
                            m = mm(b2[:, 256 + p * TOK:256 + (p + 1) * TOK], view(kx[u][:, 2 * p, :, :], [[1, 128]]), sel[:],
                                   start=True, stop=True)
                        m.then_inc(S["kT_ready"], 1)
                    for u in range(2):
                        n = l * NT + t0 + u + 1
                        pe.wait_ge(S["qT_evac"], n)
                        pe.wait_ge(S["ke_evac"], n)
                        for p in range(H // 2):
                            for r in range(2):
                                m = mm(bank[4 * u + 1 + r][:TT, p * w:(p + 1) * w], qT[u][64 * r:64 * r + 64, p, :],
                                       ke[u][64 * r:64 * r + 64, p, 0:w], start=True, stop=True)
                        m.then_inc(S["s_ready"], 1)
                    for u in range(2):
                        n = l * NT + t0 + u + 1
                        pe.wait_ge(S["px_ready"], n)
                        for k in range(H):
                            dst = bank[4 * u + (0, 3, 1)[k // 4]]
                            m = tr(dst[:TT, (k % 4) * TT:(k % 4 + 1) * TT], px[u][:, k, :], ident[:TT, :TT])
                        m.then_inc(S["pT_tr"], 1)
                    for u in range(2):
                        n = l * NT + t0 + u + 1
                        pe.wait_ge(S["pT_evac"], n)
                        for k in range(H):
                            hd = 2 * (k % 6) + k // 6
                            m = mm(bank[4 * u + 2][:TT, hd * DH:(hd + 1) * DH], pT[u][:, k, :], vsb[u][:, hd * DH:(hd + 1) * DH],
                                   start=True, stop=True)
                        m.then_inc(S["o_ready"], 1)
                    for u in range(2):
                        n = l * NT + t0 + u + 1
                        pe.wait_ge(S["o_evac"], n)
                        for c in range(2):
                            m = tr(bank[4 * u][:KC, c * TT:c * TT + TT], osb[u][:, c * KC:c * KC + KC], ident[:TT, :TT])
                        m.then_inc(S["oT_tr"], 1)
                    for u in range(2):
                        n = l * NT + t0 + u + 1
                        pe.wait_ge(S["oT_evac"], n)
                        for c in range(2):
                            m = mm(bank[4 * u + 3][:TT, 0:D], oT[u][0:KC + c, c, :], wproj[l][0:KC + c, c, :], start=(c == 0), stop=(c == 1))
                        m.then_inc(S["proj_ready"], 1)

            attention(0)
            pe.wait_ge(S["quant_pool"], 8)
            pe.wait_ge(S["quant_dve"], 9)
            with pe.Fori(0, NT // IPT) as c4:
                for i in range(IPT):
                    t = IPT * c4 + i
                    pe.wait_ge(S["fq3"], t + 1)
                    if i >= 2:
                        pe.wait_ge(S["xqT_evac"], t - 1)
                    for c in range(2):
                        m = tr(bank[i % 2][:KC, :].bitcast(BF16)[:, c * TT:c * TT + TT], xq[i % 2][:, c * KC:c * KC + KC], identb[:TT, :TT])
                    m.then_inc(S["xqT_tr"], 1)
                pe.wait_ge(S["xqT_evac"], IPT * c4 + IPT)
                for k in range(FM):
                    if k >= 4:
                        pe.wait_ge(S["gel_ready"], FM * c4 + k - 3)
                    for c in range(2):
                        m = mm(bank[2 + k % 4][:, 0:IPT * TT], wq1[:, c, 128 * k:128 * k + 128], xqT[:, c, :], start=(c == 0), stop=(c == 1))
                    m.then_inc(S["fh_ready"], 1)
                pe.wait_ge(S["hq_ready"], FM * c4 + FM)
                for i in range(IPT):
                    if i >= 2:
                        pe.wait_ge(S["f2_scaled"], IPT * c4 + i - 1)
                    for k in range(FM):
                        m = mm(bank[i % 2][:TT, 0:D], hq[:, k, i * TT:(i + 1) * TT], wq2[:, k, :], start=(k == 0), stop=(k == FM - 1))
                    m.then_inc(S["f2_ready"], 1)

            pe.wait_ge(S["attn_par"], 16 * NL)
            attention(1)

            pe.wait_ge(S["ms_small"], 10)
            with pe.Fori(0, NT - 1, 2) as t0:
                for u in range(2):
                    pe.wait_ge(S["ln_norm"], 3 * NT + t0 + u + 1)
                    for c in range(2):
                        m = tr(bank[4 * u][:KC, c * TT:c * TT + TT], mx1[u][:, c * KC:c * KC + KC], ident[:TT, :TT])
                    m.then_inc(S["xT_tr"], 1)
                for u in range(2):
                    pe.wait_ge(S["xT_evac"], 2 * NT + t0 + u + 1)
                    for c in range(2):
                        m = mm(bank[4 * u + 1][:TT, 0:E], mxT[u][0:KC + c, c, :], wr[0:KC + c, c, :], start=(c == 0), stop=(c == 1))
                    m.then_inc(S["lg_ready"], 1)
                for u in range(2):
                    pe.wait_ge(S["hot_ready"], t0 + u + 1)
                    for c in range(2):
                        m = mm(bank[4 * u + 2][:TT, c * E:(c + 1) * E], tri[:, c, :], hot[:, bass.ds(t0 + u, 1), :], start=True, stop=True)
                    m.then_inc(S["rk_ready"], 1)
            pe.wait_ge(S["moe_in"], 48)
            pe.wait_ge(S["owner_ready"], 1)
            with pe.Fori(0, NS - 1, 2) as j0:
                ex = []
                for u in range(2):
                    ex.append(nc.tensor.value_load(owner[0:1, bass.ds(j0 + u, 1)], min_val=0, max_val=E - 1))
                for u in range(2):
                    pe.wait_ge(xg_in[u], 8 * j0 + 16)
                    for c in range(2):
                        m = tr(bank[4 * u][:KC, c * 128:c * 128 + 128], xg[u][:, c * KC:c * KC + KC], ident[:])
                    m.then_inc(S["xgT_tr"], 1)
                for u in range(2):
                    pe.wait_ge(S["xgT_evac"], j0 + u + 1)
                    pe.wait_ge(S["y_evac"], j0 + u + 1)
                    for f in range(2):
                        for c in range(2):
                            wv = w1[0:KC + c, bass.ds(ex[u], 1), c, f * 384:(f + 1) * 384]
                            m = mm(bank[4 * u + 1 + f][:, 0:384], xgT[u][0:KC + c, c, :], wv, start=(c == 0), stop=(c == 1))
                    m.then_inc(S["hid_ready"], 1)
                for u in range(2):
                    pe.wait_ge(S["hgel_ready"], j0 + u + 1)
                    for k in range(FM):
                        m = tr(bank[4 * u + 3 * (k // 3)][:, (k % 3) * 128:(k % 3 + 1) * 128], hid[u][:, k * 128:(k + 1) * 128], ident[:])
                    m.then_inc(S["hT_tr"], 1)
                for u in range(2):
                    pe.wait_ge(S["hTa_evac"], j0 + u + 1)
                    pe.wait_ge(S["hTb_evac"], j0 + u + 1)
                    for k in range(FM):
                        mm(bank[4 * u + 1][:, 0:D], hT[u][:, k, :], w2[:, bass.ds(ex[u], 1), k, :], start=(k == 0), stop=False)
                    mm(bank[4 * u + 1][:, 0:D], ones[:], eb2[:, bass.ds(ex[u], 1), :], start=False, stop=True).then_inc(S["y_ready"], 1)

        @block.scalar
        def _(act):
            def front(t, u, first=False):
                for b in range(IPT):
                    act.wait_ge(stem_ready, IPT * t + b + 1)
                    if not (first and b < 2):
                        act.wait_ge(hpix_ready, IPT * t + b - 1)
                    nc.scalar.activation(leak[b % 2][:], stem_ps[b % 2][:PK, 0:NK * C1], ACT.Copy,
                                         scale=SLOPE).then_inc(leak_ready, 1)
                for b in range(IPT):
                    act.wait_ge(tr_ready, TG * t + b + 1)
                    for kh in range(KP):
                        m = nc.scalar.activation(
                            view(hch[:, KP * kh, b * POS:], [[TP, KP], [G2, G2], [1, G2]]),
                            view(bank[b % 2][:C1, kh * G1:], [[1, KP], [KP * G1, G2], [KP, G2]]), ACT.Copy)
                    m.then_inc(tr_evac, 1)
                act.wait_ge(dist_ready, t + 1)
                nc.scalar.activation(dist[:], dist[:], ACT.Abs).then_inc(abs_ready, 1)
                act.wait_ge(abs_ready, t + 1)
                nc.scalar.activation(tent[:], dist[:], ACT.Relu, bias=1.0, scale=-1.0).then_inc(tent_ready, 1)

            def turn_map(t, u, k):
                act.wait_ge(tr_ready, TG * t + IPT + k + 1)
                nc.scalar.activation(wmapT[u][:, :, k, :],
                                     view(bank[k % 2][:PK, 0:1], [[TP, NK], [1, TP]]), ACT.Copy).then_inc(tr_evac, 1)

            def back(t, u, nxt):
                for k in range(TAPS):
                    if nxt:
                        turn_map(t + 1, 1 - u, k)
                act.wait_ge(dcn_ready, t + 1)
                nc.scalar.activation(dleak[:], dcn_ps, ACT.Copy, scale=SLOPE).then_inc(dleak_ready, 1)

            front(0, 0, first=True)
            for k in range(TAPS):
                turn_map(0, 0, k)
            front(1, 1)
            back(0, 0, True)
            with act.Fori(1, NT - 1, 2) as t:
                for u in (1, 0):
                    front(t + (2 - u), 1 - u)
                    back(t + (1 - u), u, True)
            back(NT - 1, 1, False)

            def copy(dst, src):
                return nc.scalar.activation(dst, src, ACT.Copy)

            def attention(l):
                with act.Fori(0, NT - 1, 2) as t0:
                    for u in range(2):
                        act.wait_ge(S["xT_tr"], l * NT + t0 + u + 1)
                        copy(xT[u][0:KC, :, :], bank[4 * u][:KC, 0:2 * TT]).then_inc(S["xT_evac"], 1)
                    for u in range(2):
                        n = l * NT + t0 + u + 1
                        act.wait_ge(S["qkv_ready"], n)
                        if l:
                            copy(cen[u][:], bank[4 * u + 1][:TT, 0:2 * D]).then_inc(S["cen_ready"], 1)
                        copy(vsb[u][:], bank[4 * u + 2][:TT, 0:D]).then_inc(S["v_evac"], 1)
                        if not l:
                            act.wait_ge(S["cen_ready"], n)
                            nc.scalar.activation(view(px[u][:], [[1, 2 * D]]), cen[u][:], ACT.Square).then_inc(S["sq_ready"], 1)
                    for u in range(2):
                        n = l * NT + t0 + u + 1
                        act.wait_ge(S["qT_tr"], n)
                        copy(qT[u][:, 0:3, :], bank[4 * u][:, 0:3 * TT])
                        copy(qT[u][:, 3:6, :], bank[4 * u + 3][:, 0:3 * TT]).then_inc(S["qT_evac"], 1)
                        act.wait_ge(S["kT_ready"], n)
                        copy(ke[u][:, :, 0:TOK], view(bank[4 * u + 2][:, 256:], [[TOK, H // 2], [1, TOK]])).then_inc(S["ke_evac"], 1)
                    if l:
                        for u in range(2):
                            act.wait_ge(S["s_ready"], NT + t0 + u + 1)
                            copy(se[u][:], psum[:TT, 4 * u + 1:4 * u + 3, 0:H // 2 * (TOK + NREL)]).then_inc(S["se_ready"], 1)
                    for u in range(2):
                        act.wait_ge(S["sc_ready"], l * NT + t0 + u + 1)
                        nc.scalar.activation(prob[u][:], sc[u][:], ACT.Exp, scale=DH ** -0.5).then_inc(S["exp_ready"], 1)
                    for u in range(2):
                        act.wait_ge(S["pT_tr"], l * NT + t0 + u + 1)
                        for q in range(3):
                            m = copy(pT[u][:, 4 * q:4 * q + 4, :], bank[4 * u + (0, 3, 1)[q]][:TT, 0:4 * TT])
                        m.then_inc(S["pT_evac"], 1)
                    for u in range(2):
                        act.wait_ge(S["o_ready"], l * NT + t0 + u + 1)
                        copy(osb[u][:], bank[4 * u + 2][:TT, 0:D]).then_inc(S["o_evac"], 1)
                    for u in range(2):
                        act.wait_ge(S["oT_tr"], l * NT + t0 + u + 1)
                        copy(oT[u][0:KC, :, :], bank[4 * u][:KC, 0:2 * TT]).then_inc(S["oT_evac"], 1)

            attention(0)
            act.wait_ge(S["quant_dve"], 9)
            with act.Fori(0, NT // IPT) as c4:
                for i in range(IPT):
                    act.wait_ge(S["xqT_tr"], IPT * c4 + i + 1)
                    copy(xqT[:, :, i * TT:(i + 1) * TT], view(bank[i % 2][:KC, :].bitcast(BF16), [[TT, 2], [1, TT]])).then_inc(S["xqT_evac"], 1)
                for k in range(FM):
                    act.wait_ge(S["fh_ready"], FM * c4 + k + 1)
                    if k >= 2:
                        act.wait_ge(S["hq_ready"], FM * c4 + k - 1)
                    nc.scalar.activation(gel[k % 2][:], bank[2 + k % 4][:, 0:IPT * TT], ACT.Gelu, bias=fb1[:, k:k + 1],
                                         scale=s1[:, k:k + 1]).then_inc(S["gel_ready"], 1)
            attention(1)
            with act.Fori(0, NT - 1, 2) as t0:
                for u in range(2):
                    act.wait_ge(S["xT_tr"], 2 * NT + t0 + u + 1)
                    copy(mxT[u][0:KC, :, :], bank[4 * u][:KC, 0:2 * TT]).then_inc(S["xT_evac"], 1)
                for u in range(2):
                    act.wait_ge(S["lsh_ready"], t0 + u + 1)
                    nc.scalar.activation(lex[u][:], lsh[u][:], ACT.Exp).then_inc(S["lex_ready"], 1)
            with act.Fori(0, NS - 1, 2) as j0:
                for u in range(2):
                    act.wait_ge(S["xgT_tr"], j0 + u + 1)
                    copy(xgT[u][0:KC, :, :], bank[4 * u][:KC, 0:256]).then_inc(S["xgT_evac"], 1)
                for u in range(2):
                    act.wait_ge(S["hid_ready"], j0 + u + 1)
                    nc.scalar.activation(hid[u][:], psum[:, 4 * u + 1:4 * u + 3, 0:384], ACT.Gelu).then_inc(S["hgel_ready"], 1)
                for u in range(2):
                    act.wait_ge(S["hT_tr"], j0 + u + 1)
                    copy(hT[u][:, 0:3, :], bank[4 * u][:, 0:384]).then_inc(S["hTa_evac"], 1)

        @block.vector
        def _(dve):
            v = nc.vector
            dve.wait_ge(bn_pow, 6)
            dve.wait_ge(par_in, 16 * NPAR)
            v.tensor_tensor(wstem[:], wstem[:], inv1[:], ALU.mult).then_inc(fold, 1)
            v.tensor_tensor(wdcn[:], wdcn[:], view(inv2[:], [[0, TAPS], [1, D]]), ALU.mult).then_inc(par_ready, 1)
            v.tensor_tensor(shift1[:], bn1[0:1, 2, :], inv1[0:1, :], ALU.mult).then_inc(fold, 1)
            v.tensor_tensor(shift2[:], bn2[0:1, 4, :], bn2[0:1, 2, :], ALU.subtract).then_inc(fold, 1)
            v.tensor_tensor(posbase[:], base[:], off_bias[:], ALU.add).then_inc(par_ready, 1)
            dve.wait_ge(fold, 3)
            v.tensor_tensor(shift1[:], bn1[0:1, 1, :], shift1[:], ALU.subtract).then_inc(fold, 1)
            v.tensor_tensor(shift2[:], shift2[:], inv2[0:1, :], ALU.mult).then_inc(fold, 1)
            dve.wait_ge(fold, 5)
            v.tensor_tensor(wstem[0:1, :], wstem[0:1, :], shift1[:], ALU.add).then_inc(par_ready, 1)
            v.tensor_tensor(shift2[:], shift2[:], bn2[0:1, 1, :], ALU.add).then_inc(par_ready, 1)
            dve.wait_ge(par_ready, 4)
            dve.wait_ge(pool_const, 10)

            def front(t, u, first=False):
                for b in range(IPT):
                    dve.wait_ge(leak_ready, IPT * t + b + 1)
                    v.tensor_tensor(hpix[u][:, b, :, :], stem_ps[b % 2][:PK, 0:NK * C1], leak[b % 2][:],
                                    ALU.max).then_inc(hpix_ready, 1)
                dve.wait_ge(off_ready, t + 1)
                v.tensor_tensor(pxy[:], off_ps, posbase[:], ALU.add).then_inc(pxy_ready, 1)
                dve.wait_ge(pxy_ready, t + 1)
                v.tensor_tensor(dist[:], view(pxy[:], [[1, 2 * TAPS], [0, G1]]),
                                view(iota21[:], [[0, 2 * TAPS], [1, G1]]), ALU.subtract).then_inc(dist_ready, 1)
                dve.wait_ge(tent_ready, t + 1)

            def make_map(t, k):
                if k >= 4:
                    dve.wait_ge(tr_ready, TG * t + k + 1)
                v.tensor_tensor(view(wmap[k % 4][:], [[G1, G1], [1, G1]]),
                                view(tent[:, k, :], [[1, G1], [0, G1]]),
                                view(tent[:, TAPS + k, :], [[0, G1], [1, G1]]), ALU.mult).then_inc(wmap_ready, 1)

            def back(t, u, nxt):
                for b in range(IPT):
                    if nxt:
                        for k in range(NK):
                            make_map(t + 1, NK * b + k)
                    dve.wait_ge(samp_ready, IPT * t + b + 1)
                    v.tensor_copy(samp[:, :, b, 1:TOK],
                                  view(samp_ps[b % 2][:C1, 0:1], [[POS, TAPS], [1, POS]])).then_inc(samp_evac, 1)
                dve.wait_ge(dleak_ready, t + 1)
                v.tensor_tensor(dmax[:], dcn_ps, dleak[:], ALU.max).then_inc(dmax_ready, 1)
                dve.wait_ge(dmax_ready, t + 1)
                v.tensor_tensor(h[:, bass.ds(t, 1), :], dmax[:], clsmat[:], ALU.add).then_inc(h0_ready, 1)

            front(0, 0, first=True)
            for k in range(TAPS):
                make_map(0, k)
            front(1, 1)
            back(0, 0, True)
            with dve.Fori(1, NT - 1, 2) as t:
                for u in (1, 0):
                    front(t + (2 - u), 1 - u)
                    back(t + (1 - u), u, True)
            back(NT - 1, 1, False)

            def mean(t0, i, x_sem, stt, mvt):
                for u in range(2):
                    dve.wait_ge(x_sem, t0 + u + 1 + (NT if i == 3 else 0))
                    v.bn_stats(stt[u][:], h[:, bass.ds(t0 + u, 1), :]).then_inc(S["ln_raw"], 1)
                dve.wait_ge(S["ln_raw"], i * NT + t0 + 2)
                v.memset(tick[:], 0.0)
                for u in range(2):
                    v.bn_aggr(mvt[u][:], stt[u][:]).then_inc(S["ln_stat"], 1)

            def norm(t, i, u, mvt, rst, dst):
                dve.wait_ge(S["ln_rstd"], i * NT + t + 1)
                v.tensor_scalar(dst, h[:, bass.ds(t, 1), :], mvt[u][:, 0:1], rst[u][:, 0:1],
                                ALU.subtract, ALU.mult).then_inc(S["ln_norm"], 1)

            q = S["quant_dve"]
            dve.wait_ge(S["attn_par"], 16 * NL)
            dve.wait_ge(S["wt_in"], 16 * NW)
            v.tensor_reduce(am[:, 0:1], ala1[:], AX.X, ALU.add).then_inc(S["fc_done"], 1)
            v.tensor_reduce(am[:, 1:2], ala2[:], AX.X, ALU.add).then_inc(S["fc_done"], 1)
            dve.wait_ge(S["fc_done"], 2)
            v.tensor_scalar(am[:, 0:1], am[:, 0:1], 1.0 / D, None, ALU.mult).then_inc(q, 1)
            v.tensor_scalar(am[:, 1:2], am[:, 1:2], 1.0 / FF, None, ALU.mult).then_inc(q, 1)
            dve.wait_ge(q, 2)
            v.tensor_tensor(row2[:], alw2[:TT, :], view(am[:TT, 1:2], [[0, D]]), ALU.mult).then_inc(S["fc_done"], 1)
            dve.wait_ge(S["fc_done"], 3)
            v.reciprocal(alw1[:], alw1[:]).then_inc(q, 1)
            v.reciprocal(alw2[:], alw2[:]).then_inc(q, 1)
            v.reciprocal(ram[:], am[:]).then_inc(q, 1)
            v.tensor_scalar(s1[:], alw1c[:], am[:, 0:1], None, ALU.mult).then_inc(q, 1)
            v.tensor_copy(identb[:], ident[:]).then_inc(q, 3)

            def attention(l):
                W = TOK + NREL
                with dve.Fori(0, NT - 1, 2) as t0:
                    mean(t0, 2 * l, S["hffn_ready"] if l else h0_ready, stat, mv)
                    for u in range(2):
                        norm(t0 + u, 2 * l, u, mv, rstd, xn[u][:])
                    if l == 0:
                        for u in range(2):
                            n = t0 + u + 1
                            qk = view(bank[4 * u + 1][:TT, :], [[DH, 2 * H], [1, DH]])
                            dve.wait_ge(S["qkv_ready"], n)
                            v.tensor_reduce(hsum[u][:], qk, AX.X, ALU.add).then_inc(S["hs_ready"], 1)
                            dve.wait_ge(S["hs_ready"], n)
                            v.tensor_scalar(hmean[u][:], hsum[u][:], 1.0 / DH, None, ALU.mult).then_inc(S["hm_ready"], 1)
                            dve.wait_ge(S["hm_ready"], n)
                            v.tensor_tensor(cen[u][:], qk, view(hmean[u][:], [[1, 2 * H], [0, DH]]),
                                            ALU.subtract).then_inc(S["cen_ready"], 1)
                        for u in range(2):
                            dve.wait_ge(S["sq_ready"], t0 + u + 1)
                            v.tensor_reduce(hvar[u][:], view(px[u][:], [[DH, 2 * H], [1, DH]]), AX.X, ALU.add).then_inc(S["hv_ready"], 1)
                    for u in range(2):
                        n = l * NT + t0 + u + 1
                        dve.wait_ge(S["cen_ready"], n)
                        if l == 0:
                            dve.wait_ge(S["qmask_ready"], n)
                        v.tensor_tensor(qx[u], view(cen[u][:], [[DH, H], [0, IPT], [1, DH]]),
                                        view((bmask if l else qmask[u])[:], [[IPT, H], [1, IPT], [0, DH]]), ALU.mult).then_inc(S["qx_ready"], 1)
                    for u in range(2):
                        n = l * NT + t0 + u + 1
                        if l == 0:
                            dve.wait_ge(S["s_ready"], n)
                            src = view(psum[:TT, 4 * u + 1, :], [[512, 2], [TOK, H // 2], [1, TOK]])
                        else:
                            dve.wait_ge(S["se_ready"], t0 + u + 1)
                            dve.wait_ge(rel_in[u], 32 * t0 + 64)
                            v.tensor_tensor(sc[u][:], view(se[u][:], [[W, H], [1, TOK]]), rel[u][:], ALU.add).then_inc(S["sr_ready"], 1)
                            dve.wait_ge(S["sr_ready"], t0 + u + 1)
                            src = view(sc[u][:], [[6 * TOK, 2], [TOK, H // 2], [1, TOK]])
                        v.tensor_reduce(smax[u][:], src, AX.X, ALU.max).then_inc(S["smax_ready"], 1)
                        dve.wait_ge(S["smax_ready"], n)
                        v.tensor_tensor(view(sc[u][:], [[6 * TOK, 2], [TOK, H // 2], [1, TOK]]), src,
                                        view(smax[u][:], [[6, 2], [1, 6], [0, TOK]]), ALU.subtract).then_inc(S["sc_ready"], 1)
                    for u in range(2):
                        n = l * NT + t0 + u + 1
                        dve.wait_ge(S["exp_ready"], n)
                        v.tensor_reduce(rsum[u][:], prob[u][:], AX.X, ALU.add).then_inc(S["rs_ready"], 1)
                        dve.wait_ge(S["rs_ready"], n)
                        v.reciprocal(rsum[u][:], rsum[u][:]).then_inc(S["rr_ready"], 1)
                        dve.wait_ge(S["rr_ready"], n)
                        v.tensor_tensor(pmask[u][:], view(rsum[u][:], [[1, H], [0, IPT]]), view(mask[:], [[0, H], [1, IPT]]),
                                        ALU.mult).then_inc(S["pmask_ready"], 1)
                        dve.wait_ge(S["pmask_ready"], n)
                        v.tensor_tensor(view(px[u][:], [[TT, H], [TOK, IPT], [1, TOK]]), view(prob[u][:], [[TOK, H], [0, IPT], [1, TOK]]),
                                        view(pmask[u][:], [[IPT, H], [1, IPT], [0, TOK]]), ALU.mult).then_inc(S["px_ready"], 1)
                    for u in range(2):
                        t = t0 + u
                        dve.wait_ge(S["proj_ready"], l * NT + t + 1)
                        v.tensor_tensor(h[:, bass.ds(t, 1), :], h[:, bass.ds(t, 1), :], bank[4 * u + 3][:TT, 0:D],
                                        ALU.add).then_inc(S["hattn_ready"], 1)

            attention(0)
            with dve.Fori(0, NT // IPT) as c4:
                for i in range(IPT):
                    u, t = i % 2, IPT * c4 + i
                    if u == 0:
                        mean(t, 1, S["hattn_ready"], stat, mv)
                    norm(t, 1, u, mv, rstd, xn[u][:])
                    dve.wait_ge(S["ln_norm"], NT + t + 1)
                    v.tensor_scalar(xn[u][:], xn[u][:], ram[:TT, 0:1], -8.0, ALU.mult, ALU.max).then_inc(S["fq1"], 1)
                    dve.wait_ge(S["fq1"], t + 1)
                    v.tensor_scalar(xn[u][:], xn[u][:], 7.0, MAGIC, ALU.min, ALU.add).then_inc(S["fq2"], 1)
                    dve.wait_ge(S["fq2"], t + 1)
                    if i >= 2:
                        dve.wait_ge(S["xqT_tr"], t - 1)
                    v.tensor_scalar(xq[u][:], xn[u][:], -MAGIC, None, ALU.add).then_inc(S["fq3"], 1)
                for k in range(FM):
                    gk, base_ = gel[k % 2], 3 * FM * c4 + 3 * k + 3
                    dve.wait_ge(S["gel_ready"], FM * c4 + k + 1)
                    v.tensor_scalar(gk[:], gk[:], -10.0, 10.0, ALU.max, ALU.min).then_inc(S["fc_done"], 1)
                    dve.wait_ge(S["fc_done"], base_ + 1)
                    v.tensor_scalar(gk[:], gk[:], ram[:, 1:2], -8.0, ALU.mult, ALU.max).then_inc(S["fc_done"], 1)
                    dve.wait_ge(S["fc_done"], base_ + 2)
                    v.tensor_scalar(gk[:], gk[:], 7.0, MAGIC, ALU.min, ALU.add).then_inc(S["fc_done"], 1)
                    dve.wait_ge(S["fc_done"], base_ + 3)
                    v.tensor_scalar(hq[:, k, :], gk[:], -MAGIC, None, ALU.add).then_inc(S["hq_ready"], 1)
                for i in range(IPT):
                    u, t = i % 2, IPT * c4 + i
                    ht = h[:, bass.ds(t, 1), :]
                    dve.wait_ge(S["f2_ready"], t + 1)
                    v.tensor_tensor(f2[u][:], bank[u][:TT, 0:D], row2[:], ALU.mult).then_inc(S["f2_scaled"], 1)
                    dve.wait_ge(S["f2_scaled"], t + 1)
                    v.tensor_tensor(f2[u][:], f2[u][:], ht, ALU.add).then_inc(S["f2_sum"], 1)
                    dve.wait_ge(S["f2_sum"], t + 1)
                    v.tensor_tensor(ht, f2[u][:], fb2[:], ALU.add).then_inc(S["hffn_ready"], 1)

            attention(1)

            v.memset(cnt[1][:], 0.0).then_inc(S["cnt_ready"], 1)
            with dve.Fori(0, NT - 1, 2) as t0:
                mean(t0, 3, S["hattn_ready"], mstat, mmv)
                for u in range(2):
                    norm(t0 + u, 3, u, mmv, mrstd, mx1[u][:])
                for u in range(2):
                    t = t0 + u
                    dve.wait_ge(S["ln_norm"], 3 * NT + t + 1)
                    v.tensor_copy(mxn[:, bass.ds(t, 1), :], mx1[u][:]).then_inc(S["mxn_ready"], 1)
                for u in range(2):
                    t, n, lg = t0 + u, t0 + u + 1, bank[4 * u + 1][:TT, 0:E]
                    dve.wait_ge(S["lg_ready"], n)
                    v.tensor_reduce(lmax[u][:], lg, AX.X, ALU.max).then_inc(S["lmax_ready"], 1)
                    dve.wait_ge(S["lmax_ready"], n)
                    v.tensor_scalar(lsh[u][:], lg, lmax[u][:, 0:1], None, ALU.subtract).then_inc(S["lsh_ready"], 1)
                    dve.wait_ge(S["lsh_ready"], n)
                    v.scalar_tensor_tensor(cand[u][:], lsh[u][:], 0.0, rev[:], ALU.is_ge, ALU.mult).then_inc(S["cand_ready"], 1)
                    dve.wait_ge(S["cand_ready"], n)
                    v.tensor_reduce(cmax[u][:], cand[u][:], AX.X, ALU.max).then_inc(S["cmax_ready"], 1)
                    dve.wait_ge(S["cmax_ready"], n)
                    v.tensor_scalar(hot[:, bass.ds(t, 1), :], cand[u][:], cmax[u][:, 0:1], None, ALU.is_equal).then_inc(S["hot_ready"], 1)
                for u in range(2):
                    t, n = t0 + u, t0 + u + 1
                    dve.wait_ge(S["lex_ready"], n)
                    v.tensor_reduce(lsum[u][:], lex[u][:], AX.X, ALU.add).then_inc(S["lsum_ready"], 1)
                    dve.wait_ge(S["lsum_ready"], n)
                    v.reciprocal(pmax[:, bass.ds(t, 1)], lsum[u][:]).then_inc(S["pmax_ready"], 1)
                for u in range(2):
                    t, n = t0 + u, t0 + u + 1
                    dve.wait_ge(S["rk_ready"], n)
                    dve.wait_ge(S["cnt_ready"], n)
                    v.tensor_tensor(rank[:, bass.ds(t, 1), :], bank[4 * u + 2][:TT, 0:E], cnt[1 - u][:], ALU.add).then_inc(S["rank_ready"], 1)
                    v.tensor_tensor(cnt[u][:], bank[4 * u + 2][:TT, E:2 * E], cnt[1 - u][:], ALU.add).then_inc(S["cnt_ready"], 1)
            done = S["plan"]
            dve.wait_ge(S["cnt_ready"], NT + 1)
            v.tensor_scalar(ntile[:], cnt[1][:], 63.5, 1.0 / 128, ALU.add, ALU.mult).then_inc(done, 1)
            dve.wait_ge(done, 1)
            v.tensor_scalar(ntile[:], ntile[:], MAGIC, None, ALU.add).then_inc(done, 1)
            dve.wait_ge(done, 2)
            v.tensor_scalar(ntile[:], ntile[:], -MAGIC, None, ALU.add).then_inc(done, 1)
            dve.wait_ge(done, 3)
            v.tensor_tensor(cum[:], view(ntile[:], [[0, E], [1, E]]), upto[:], ALU.mult).then_inc(done, 1)
            dve.wait_ge(done, 4)
            v.tensor_reduce(ends[:], cum[:], AX.X, ALU.add).then_inc(done, 1)
            dve.wait_ge(done, 5)
            v.tensor_tensor(start[:], ends[:], ntile[:], ALU.subtract).then_inc(done, 1)
            dve.wait_ge(done, 6)
            v.tensor_scalar(start[:], start[:], 128.0, None, ALU.mult).then_inc(done, 1)
            dve.wait_ge(done, 7)
            dve.wait_ge(S["rank_ready"], NT)
            v.tensor_tensor(slotw[:], rank[:], view(start[:], [[0, NT], [1, E]]), ALU.add).then_inc(done, 1)
            dve.wait_ge(done, 8)
            v.tensor_tensor(slotw[:], slotw[:], hot[:], ALU.mult).then_inc(done, 1)
            dve.wait_ge(done, 9)
            v.tensor_reduce(slotf[:], slotw[:], AX.X, ALU.add).then_inc(done, 1)
            dve.wait_ge(done, 10)
            v.tensor_copy(slot[:], slotf[:]).then_inc(S["slot_ready"], 1)
            v.tensor_tensor(past[:], view(ends[0:1, :], [[0, NS], [1, E]]), view(tidx[:], [[1, NS], [0, E]]), ALU.is_le).then_inc(done, 1)
            dve.wait_ge(done, 11)
            v.tensor_reduce(own[:], past[:], AX.X, ALU.add).then_inc(done, 1)
            dve.wait_ge(done, 12)
            v.tensor_scalar(own[:], own[:], float(E - 1), None, ALU.min).then_inc(done, 1)
            dve.wait_ge(done, 13)
            v.tensor_copy(owner[:], own[:]).then_inc(S["owner_ready"], 1)
            v.memset(lsum[0][:], 0.0).then_inc(S["y_evac"], 2)
            with dve.Fori(0, NS - 1, 2) as j0:
                for u in range(2):
                    dve.wait_ge(S["hT_tr"], j0 + u + 1)
                    v.tensor_copy(hT[u][:, 3:6, :], bank[4 * u + 3][:, 0:384]).then_inc(S["hTb_evac"], 1)
                for u in range(2):
                    dve.wait_ge(S["y_ready"], j0 + u + 1)
                    v.tensor_copy(yo[:, bass.ds(j0 + u, 1), :], bank[4 * u + 1][:, 0:D]).then_inc(S["y_evac"], 1)
            dve.wait_ge(S["gath_done"], 16 * NT)
            dve.wait_ge(S["pmax_ready"], NT)
            with dve.Fori(0, NT) as t:
                ht = h[:, bass.ds(t, 1), :]
                v.scalar_tensor_tensor(ht, yg[:, bass.ds(t, 1), :], pmax[:, bass.ds(t, 1)], ht, ALU.mult, ALU.add).then_inc(S["hout"], 1)


def kernel(**a):
    import numpy as np
    import concourse.bacc as bacc
    from concourse import mybir as mb
    from concourse.bass_utils import run_bass_kernel_spmd

    n = {k: np.asarray(v) for k, v in a.items()}
    f = np.float32
    arr = {}
    x = n["x"].reshape(NT, IPT, CIN, G1, KP, G1, KP).transpose(0, 2, 4, 6, 1, 3, 5).reshape(NT, 48, IPT, PIX)
    arr["xcol"] = np.pad(x, ((0, 0), (0, 0), (0, 0), (0, PIXP - PIX)))
    arr["ident"] = np.eye(128, dtype=f)
    arr["iota21"] = np.broadcast_to(np.arange(G1, dtype=f), (TP, G1))
    pos = np.arange(TP) % POS
    tap = np.arange(TAPS)
    arr["base"] = np.concatenate([(KP * (pos // G2))[:, None] + (tap // KP)[None],
                                  (KP * (pos % G2))[:, None] + (tap % KP)[None]], 1).astype(f)
    arr["off_b"] = n["L0_tok_off_b"].reshape(TAPS, 2).T.reshape(1, -1)
    arr["off_w"] = n["L0_tok_off_w"].reshape(TAPS, 2, C1, TAPS).transpose(2, 3, 1, 0).reshape(C1, TAPS, 2 * TAPS)
    arr["notcls"] = (np.arange(TT) % TOK != 0).astype(f)[None]
    arr["cls"] = n["cls_tok"].reshape(1, D)
    arr["stem_rows"] = np.concatenate([n["L0_tok_stem_b"][None], n["L0_tok_stem_w"].reshape(C1, 48).T], 0)
    arr["bn1"] = np.stack([n["L0_tok_bn1_" + s] for s in "gbmv"])
    arr["bn2"] = np.stack([n["L0_tok_bn2_" + s] for s in "gbmv"] + [n["L0_tok_dcn_b"]])
    arr["dcn_w"] = n["L0_tok_dcn_w"].reshape(D, C1, TAPS).transpose(1, 2, 0)

    def rows(w, b=None):
        wt = w.T.reshape(2, KC, -1).transpose(1, 0, 2)
        last = np.zeros((1, 2, w.shape[0]), f)
        if b is not None:
            last[0, 1] = b
        return np.concatenate([wt, last], 0)

    arr["qkv0"] = rows(n["L0_attn_qkv_weight"])
    arr["qkv1"] = rows(n["L1_attn_qkv_w"], n["L1_attn_qkv_b"])
    arr["proj0"] = rows(n["L0_attn_proj_weight"])
    arr["proj1"] = rows(n["L1_attn_out_w"], n["L1_attn_out_b"])
    arr["router"] = rows(n["L1_ffn_Ws"].T, n["L1_ffn_bs"])
    tok = np.arange(TT)
    arr["mask"] = (tok[:, None] // TOK == np.arange(IPT)).astype(f)
    arr["bmask"] = np.broadcast_to(arr["mask"][:, None, :], (TT, 2 * H, IPT))
    arr["sel"] = (tok[:, None] % TOK == np.arange(TOK)).astype(f)
    emb = n["L1_attn_rel_pos_emb"][np.clip(np.arange(NREL) - (TOK - 1), -MAXREL, MAXREL) + MAXREL]
    arr["rel_emb"] = np.broadcast_to(np.tile(emb.T, (2 * IPT, 1))[:, None, :], (128, H // 2, NREL))
    arr["f_b1"] = n["L0_ffn_b1"].reshape(FM, 128).T
    arr["f_b2"] = n["L0_ffn_b2"][None]
    arr["f_w1"] = n["L0_ffn_w1"].T.reshape(2, KC, FF).transpose(1, 0, 2)
    arr["f_w2"] = n["L0_ffn_w2"].T.reshape(FM, 128, D).transpose(1, 0, 2)
    arr["f_aw1"] = n["L0_ffn_alpha_w1"][None]
    arr["f_aw1c"] = n["L0_ffn_alpha_w1"].reshape(FM, 128).T
    arr["f_aw2"] = n["L0_ffn_alpha_w2"][None]
    arr["f_aa1"] = n["L0_ffn_alpha_a1"][None]
    arr["f_aa2"] = n["L0_ffn_alpha_a2"][None]
    arr["tri"] = np.stack([np.triu(np.ones((TT, TT), f), 1), np.ones((TT, TT), f)], 1)
    arr["rev"] = np.broadcast_to(E - np.arange(E, dtype=f), (TT, E))
    arr["upto"] = np.broadcast_to(np.tril(np.ones((E, E), f)), (TT, E, E))
    arr["tidx"] = np.arange(NS, dtype=f)[None]
    ew = n["L1_ffn_W1"].reshape(E, 2, KC, FF).transpose(2, 0, 1, 3)
    eb = np.stack([np.zeros((E, FF), f), n["L1_ffn_b1"]], 1)[None]
    arr["e_w1"] = np.concatenate([ew, eb], 0)
    arr["e_w2"] = n["L1_ffn_W2"].reshape(E, FM, 128, D).transpose(2, 0, 1, 3)
    arr["e_b2"] = n["L1_ffn_b2"][None]

    nc = bacc.Bacc("TRN2", target_bir_lowering=False, num_devices=1)
    io, feed = {}, {}
    for k, v in arr.items():
        v = np.ascontiguousarray(v)
        feed[f"in_{k}"] = v
        io[k] = nc.dram_tensor(f"in_{k}", v.shape, mb.dt.from_np(v.dtype), kind="ExternalInput").ap()
    out = nc.dram_tensor("out_0", (B, TOK, D), F32, kind="ExternalOutput").ap()
    build(nc, io, out)
    r = run_bass_kernel_spmd(nc, [feed], core_ids=[0])
    return r.results[0]["out_0"]
```

```python
import numpy as np
import concourse.bass as bass
from concourse import mybir
from contextlib import ExitStack

F32 = mybir.dt.float32
BF16 = mybir.dt.bfloat16
U32 = mybir.dt.uint32
I32 = mybir.dt.int32
ALU = mybir.AluOpType
ACT = mybir.ActivationFunctionType
AX = mybir.AxisListType

B, CIN, IMG = 64, 3, 84
KP = 4
G1 = IMG // KP
PIX = G1 * G1
G2 = (G1 - KP) // KP + 1
POS = G2 * G2
TOK = POS + 1
TAPS = KP * KP
C1, D = 96, 192
IPT = 4
NT = B // IPT
TT = IPT * TOK
TP = IPT * POS
PK = 111
NK = 4
PIXP = NK * PK
H, DH = 12, 16
KC = 96
FF, FM = 768, 6
E = 8
NREL, MAXREL = 2 * TOK - 1, 16
NS = (B * TOK + E * 127) // 128
EPS = 1e-5
SLOPE = 0.01
MAGIC = 12582912.0


def view(ap, dims, off=0, whole=False):
    return bass.AP(ap.tensor, ap.offset + off, ([] if whole else [list(ap.ap[0])]) + [list(d) for d in dims])


def build(nc, io, out, debug_stage=None):
    ctx = ExitStack()
    with ctx:
        def sb(name, shape, dt=F32, scope=ctx):
            return scope.enter_context(nc.sbuf_tensor(name, shape, dt))

        def sem(name):
            return ctx.enter_context(nc.semaphore(name))

        psum = ctx.enter_context(nc.psum_tensor("psum", [128, 8, 512], F32))
        bank = [psum[:, i, :] for i in range(8)]

        ident = sb("ident", [128, 128])
        eps = sb("eps", [128, D])
        mhalf = sb("mhalf", [128, D])

        h = sb("h", [TT, NT, D])

        wqkv = [sb(f"wqkv{l}", [KC + 1, 2, 3 * D]) for l in range(2)]
        wproj = [sb(f"wproj{l}", [KC + 1, 2, D]) for l in range(2)]
        mask = sb("mask", [TT, IPT])
        sel = sb("sel", [TT, TOK])
        wq1 = sb("wq1", [KC, 2, FF], BF16)
        wq2 = sb("wq2", [128, FM, D], BF16)
        s1 = sb("s1", [128, FM])
        fb1 = sb("fb1", [128, FM])
        row2 = sb("row2", [TT, D])
        fb2 = sb("fb2", [TT, D])
        am = sb("am", [128, 2])
        ram = sb("ram", [128, 2])
        identb = sb("identb", [128, 128], BF16)
        tri = sb("tri", [TT, 2, TT])
        rev = sb("rev", [TT, E])
        upto = sb("upto", [TT, E, E])
        tidx = sb("tidx", [1, NS])
        ones = sb("ones", [1, 128])
        zeros = sb("zeros", [128, D])
        tick = sb("tick", [1, 1])

        wr = sb("wr", [KC + 1, 2, E])

        tk = ExitStack()
        iota21 = sb("iota21", [TP, G1], scope=tk)
        base = sb("base", [TP, 2 * TAPS], scope=tk)
        off_bias = sb("off_bias", [TP, 2 * TAPS], scope=tk)
        posbase = sb("posbase", [TP, 2 * TAPS], scope=tk)
        notcls = sb("notcls", [1, TT], scope=tk)
        clsmat = sb("clsmat", [TT, D], scope=tk)
        wstem = sb("wstem", [64 + 49, C1], scope=tk)
        bn1 = sb("bn1", [64 + 49, 4, C1], scope=tk)
        inv1 = sb("inv1", [64 + 49, C1], scope=tk)
        shift1 = sb("shift1", [64 + 49, C1], scope=tk)
        woff = sb("woff", [C1, TAPS, 2 * TAPS], scope=tk)
        wdcn = sb("wdcn", [C1, TAPS, D], scope=tk)
        bn2 = sb("bn2", [C1, 5, D], scope=tk)
        inv2 = sb("inv2", [C1, D], scope=tk)
        bnw = sb("bnw", [128, D], scope=tk)
        ala2 = sb("ala2", [128, FF], scope=tk)
        ala1 = sb("ala1", [128, D], scope=tk)
        alw2 = sb("alw2", [128, D], scope=tk)
        alw1c = sb("alw1c", [128, FM], scope=tk)
        alw1 = sb("alw1", [KC, FF], scope=tk)
        raw2 = sb("raw2", [128, FM, D], scope=tk)
        raw1 = sb("raw1", [KC, 2, FF], scope=tk)
        shift2 = sb("shift2", [1, D], scope=tk)
        xcol = [sb(f"xcol{u}", [64 + 49, IPT // 2, PIXP], scope=tk) for u in range(2)]
        leak = [sb(f"leak{i}", [PK, NK * C1], scope=tk) for i in range(2)]
        hpix = [sb(f"hpix{u}", [PK, IPT, NK, C1], scope=tk) for u in range(2)]
        hch = sb("hch", [C1, IPT, PIXP], scope=tk)
        offsb = sb("offsb", [2 * TAPS, TP], scope=tk)
        pxy = sb("pxy", [TP, 2 * TAPS], scope=tk)
        dist = sb("dist", [TP, 2 * TAPS, G1], scope=tk)
        tent = sb("tent", [TP, 2 * TAPS, G1], scope=tk)
        wmap = [sb(f"wmap{i}", [TP, PIXP], scope=tk) for i in range(4)]
        wmapT = [sb(f"wmapT{u}", [PK, NK, TAPS, TP], scope=tk) for u in range(2)]
        samp = sb("samp", [C1, TAPS, IPT, TOK], scope=tk)
        dleak = sb("dleak", [TT, D], scope=tk)
        dmax = sb("dmax", [TT, D], scope=tk)

        tk.close()

        w1 = sb("w1", [KC + 1, E, 2, FF])
        w2 = sb("w2", [128, E, FM, D])
        eb2 = sb("eb2", [1, E, D])
        blk = ExitStack()
        a2 = lambda name, shape, dt=F32: [sb(f"{name}{u}", shape, dt, scope=blk) for u in range(2)]
        stat = a2("stat", [TT, 6])
        mv = a2("mv", [TT, 2])
        rstd = a2("rstd", [TT, 1])
        xn = a2("xn", [TT, D])
        xT = a2("xT", [KC + 1, 2, TT])
        hvar = a2("hvar", [TT, 2 * H])
        hroot = a2("hroot", [TT, 2 * H])
        hwork = a2("hwork", [TT, 2 * H])
        wmean = sb("wmean", [KC + 1, 2, 2 * H], scope=blk)
        kcp = a2("kcp", [TT, D])
        qkx = a2("qkx", [128, 2, H, IPT, DH])
        qx = [qkx[u][:TT, 0] for u in range(2)]
        kx = [qkx[u][:TT, 1] for u in range(2)]
        qkp = [view(qkx[u][:TT], [[32, 2 * H], [1, 32]]) for u in range(2)]
        qT = a2("qT", [128, H // 2, TT])
        ke = a2("ke", [128, H // 2, TOK + NREL])
        vaug = a2("vaug", [TT, H, DH + 1])
        vz = a2("vz", [TT, 2, H // 2, KC])
        se = a2("se", [TT, 2, H // 2 * (TOK + NREL)])
        rel = a2("rel", [TT, H, TOK])
        sc = a2("sc", [TT, H, TOK])
        smax = a2("smax", [TT, H])
        prob = a2("prob", [TT, H, TOK])
        rsum = a2("rsum", [TT, H])
        pmask = a2("pmask", [TT, H, IPT])
        px = a2("px", [TT, H, TT])
        pT0 = px
        pT = [sb("pT", [TT, H, TT], scope=blk)] * 2
        osb = a2("osb", [TT, D])
        oT = a2("oT", [KC + 1, 2, TT])
        bmask = sb("bmask", [TT, 2 * H, IPT], scope=blk)
        xq = a2("xq", [TT, D], BF16)
        xqT = sb("xqT", [KC, 2, IPT * TT], BF16, scope=blk)
        gel = a2("gel", [128, IPT * TT])
        hq = view(qkx[0][:].bitcast(BF16), [[IPT * TT, FM], [1, IPT * TT]])
        f2 = osb
        blk.close()

        moe = ctx
        m2 = lambda name, shape, dt=F32: [sb(f"{name}{u}", shape, dt) for u in range(2)]
        mstat = m2("mstat", [TT, 6])
        mmv = m2("mmv", [TT, 2])
        mrstd = m2("mrstd", [TT, 1])
        mxn = sb("mxn", [TT, NT, D])
        mx1 = m2("mx1", [TT, D])
        mxT = m2("mxT", [KC + 1, 2, TT])
        lmax = m2("lmax", [TT, 1])
        lsh = m2("lsh", [TT, E])
        lex = m2("lex", [TT, E])
        lsum = m2("lsum", [TT, 1])
        cand = m2("cand", [TT, E])
        cmax = m2("cmax", [TT, 1])
        pmax = sb("pmax", [TT, NT])
        hot = sb("hot", [TT, NT, E])
        rank = sb("rank", [TT, NT, E])
        cnt = m2("cnt", [TT, E])
        ntile = sb("ntile", [TT, E])
        cum = sb("cum", [TT, E, E])
        ends = sb("ends", [TT, E])
        start = sb("start", [TT, E])
        slotw = sb("slotw", [TT, NT, E])
        slotf = sb("slotf", [TT, NT])
        slot = sb("slot", [TT, NT], U32)
        past = sb("past", [1, NS, E])
        own = sb("own", [1, NS])
        owner = sb("owner", [1, NS], I32)
        xg = m2("xg", [128, D])
        xgT = m2("xgT", [KC + 1, 2, 128])
        hid = m2("hid", [128, FF])
        hT = m2("hT", [128, FM, 128])
        yo = sb("yo", [128, NS, D])
        yg = sb("yg", [TT, NT, D])

        par_in = sem("par_in")
        x_in = [sem(f"x_in{u}") for u in range(2)]
        pool_const = sem("pool_const")
        bn_pow = sem("bn_pow")
        fold = sem("fold")
        par_ready = sem("par_ready")
        stem_ready = sem("stem_ready")
        leak_ready = sem("leak_ready")
        hpix_ready = sem("hpix_ready")
        tr_ready = sem("tr_ready")
        tr_evac = sem("tr_evac")
        ones_ready = sem("ones_ready")
        off_ready = sem("off_ready")
        off_evac = sem("off_evac")
        offT_ready = sem("offT_ready")
        pxy_ready = sem("pxy_ready")
        dist_ready = sem("dist_ready")
        abs_ready = sem("abs_ready")
        tent_ready = sem("tent_ready")
        wmap_ready = sem("wmap_ready")
        samp_ready = sem("samp_ready")
        samp_evac = sem("samp_evac")
        dcn_ready = sem("dcn_ready")
        dleak_ready = sem("dleak_ready")
        dmax_ready = sem("dmax_ready")
        h0_ready = sem("h0_ready")
        out_done = sem("out_done")

        names = ("quant_in kcp_ready ke_ready blk_const hr_ready exp1_ready wc wt_in moe_in ms_small attn_par quant_pool quant_dve ln_raw ln_stat ln_eps ln_rstd ln_norm xT_tr xT_evac "
                 "qkv_ready v_evac sq_ready hv_ready "
                 "qx_ready kx_ready qT_tr kT_ready qT_evac s_ready se_ready sr_ready smax_ready sc_ready "
                 "exp_ready rs_ready rr_ready pmask_ready px_ready pT_tr pT_evac o_ready o_evac oT_tr oT_evac "
                 "proj_ready hattn_ready "
                 "fq1 fq2 fq3 xqT_tr xqT_evac fh_ready gel_ready fc_done hq_ready f2_ready f2_scaled f2_sum hffn_ready "
                 "mxn_ready lg_ready lmax_ready lsh_ready lex_ready lsum_ready cand_ready candm_ready cmax_ready pmax_ready "
                 "hot_ready rk_ready rank_ready cnt_ready plan slot_ready owner_ready zero_in scat_done "
                 "hout xgT_tr xgT_evac hid_ready hgel_ready hT_tr hTa_evac hTb_evac y_ready y_evac gath_done").split()
        S = {k: sem(k) for k in names}
        qr_out = [sem(f"qr_out{u}") for u in range(2)]
        rel_in = [sem(f"rel_in{u}") for u in range(2)]
        xg_in = [sem(f"xg_in{u}") for u in range(2)]
        y_out = [sem(f"y_out{u}") for u in range(2)]

        TG = IPT + TAPS
        stem_ps = [bank[2], bank[3]]
        samp_ps = [bank[4], bank[5]]
        off_ps = bank[6][:2 * TAPS, 0:TP]
        qk_ps, v_ps, xT_ps = bank[1][:TT, 0:2 * D], bank[2][:TT, 0:D], bank[2][:KC, D:D + 2 * TT]
        proj0_ps, proj1_ps = bank[2][:TT, 0:D], bank[3][:TT, 0:D]
        offT_ps = bank[6][:TP, 128:128 + 2 * TAPS]
        dcn_ps = bank[7][:TT, 0:D]

        small = [(ident, "ident"), (iota21, "iota21"), (base, "base"), (off_bias, "off_b"), (notcls, "notcls"),
                 (wstem, "stem_rows"), (woff, "off_w"), (wdcn, "dcn_w")]
        NPAR = len(small) + 2 + IPT
        weights = [(wqkv[0], "qkv0"), (wqkv[1], "qkv1"), (wproj[0], "proj0"), (wproj[1], "proj1"), (mask, "mask"),
                   (sel, "sel"), (fb1, "f_b1"), (fb2, "f_b2"), (tri, "tri"), (rev, "rev"), (upto, "upto"),
                   (tidx, "tidx"), (wr, "router")]
        NW = len(weights)
        quant = [(raw1, "f_w1"), (raw2, "f_w2"), (alw1, "f_aw1"), (alw1c, "f_aw1c"), (alw2, "f_aw2"),
                 (ala1, "f_aa1"), (ala2, "f_aa2")]
        late = [(bmask, "bmask")]
        NL = len(late) + 2
        NQ = IPT * (TOK * H * NREL)
        scr = nc.dram_tensor("rel_scratch", [NT, NQ], F32).ap()
        xs = nc.dram_tensor("slots_in", [NS * 128, D], F32).ap()
        ys = nc.dram_tensor("slots_out", [NS * 128, D], F32).ap()

        def bcast(name, dst):
            src = io[name]
            if src.shape[0] == 1 and dst.shape[0] > 1:
                n = int(np.prod(src.shape))
                return bass.AP(src.tensor, 0, [[0, dst.shape[0]], [1, n]])
            return src

        FINAL = NT
        def has(t):
            return not isinstance(t, int) or t < NT

        def pipelined(eng, body):
            with eng.Fori(0, NT - 5, 2) as t0:
                for u in range(2):
                    body(t0 + u, u)
            for t in range(NT - 4, NT):
                body(t, t % 2)

        block = ctx.enter_context(nc.Block())

        def load_x(eng, t, u):
            for r in range(2):
                eng.dma_start(xcol[u][64 * r + 1:64 * r + 49, :, :], io["xcol"][bass.ds(t, 1), r, :, :, :]).then_inc(x_in[u], 16)

        @block.sync
        def _(sp):
            load_x(sp, 0, 0)
            for dst, name in small:
                src = io[name]
                if name == "off_b":
                    src = bass.AP(src.tensor, src.offset, [[0, TP], [1, 2 * TAPS]])
                sp.dma_start(dst[:], src).then_inc(par_in, 16)
            sp.dma_start(bn1[:], bass.AP(io["bn1"].tensor, 0, [[0, 64 + 49], [1, 4 * C1]])).then_inc(par_in, 16)
            sp.dma_start(bn2[:], bass.AP(io["bn2"].tensor, 0, [[0, C1], [1, 5 * D]])).then_inc(par_in, 16)
            load_x(sp, 1, 1)
            sp.wait_ge(pool_const, 1)
            for i in range(IPT):
                sp.dma_start(clsmat[TOK * i:TOK * i + 1, :], io["cls"]).then_inc(par_in, 16)
            for dst, name in quant:
                sp.dma_start(dst[:], bcast(name, dst)).then_inc(S["quant_in"], 16)
            sp.wait_ge(stem_ready, IPT)
            load_x(sp, 2, 0)
            with sp.Fori(1, NT - 3, 2) as t1:
                for u in (1, 0):
                    t = t1 + (1 - u)
                    sp.wait_ge(stem_ready, IPT * t + IPT)
                    load_x(sp, t + 2, u)
            sp.wait_ge(stem_ready, IPT * (NT - 3) + IPT)
            load_x(sp, NT - 1, 1)
            for dst, name in weights:
                sp.dma_start(dst[:], bcast(name, dst)).then_inc(S["wt_in"], 16)
            sp.wait_ge(S["ms_small"], 2)
            sp.dma_start(xs.rearrange("(j p) d -> p j d", p=128), view(zeros[:], [[0, NS], [1, D]])).then_inc(S["zero_in"], 16)
            sp.wait_ge(h0_ready, NT)
            for dst, name in late:
                sp.dma_start(dst[:], bcast(name, dst)).then_inc(S["attn_par"], 16)
            for u in range(2):
                sp.dma_start(ke[u][:, :, TOK:], io["rel_emb"]).then_inc(S["attn_par"], 16)
            for dst, name in ((w1, "e_w1"), (w2, "e_w2"), (eb2, "e_b2")):
                sp.dma_start(dst[:], io[name]).then_inc(S["moe_in"], 16)
            with sp.Fori(0, NT - 1, 2) as t0:
                for u in range(2):
                    t = t0 + u
                    sp.wait_ge(S["se_ready"], t + 1)
                    sp.dma_start(view(scr[bass.ds(t, 1), :], [[H * NREL, TT], [NREL, H], [1, NREL]], whole=True),
                                 view(se[u][:], [[TOK + NREL, H], [1, NREL]], TOK)).then_inc(qr_out[u], 16)
                    sp.wait_ge(qr_out[u], 8 * t0 + 16)
                    for i in range(IPT):
                        sp.dma_start(rel[u][TOK * i:TOK * i + TOK, :, :],
                                     view(scr[bass.ds(t, 1), :], [[H * NREL - 1, TOK], [NREL, H], [1, TOK]],
                                          i * TOK * H * NREL + TOK - 1, whole=True)).then_inc(rel_in[u], 16)
            sp.wait_ge(S["scat_done"], 16 * NT)
            for j in range(2):
                sp.dma_start(xg[j][:], xs[128 * j:128 * j + 128, :]).then_inc(xg_in[j], 16)
            with sp.Fori(0, NS - 3, 2) as j0:
                for u in range(2):
                    sp.wait_ge(S["xgT_tr"], j0 + u + 1)
                    sp.dma_start(xg[u][:], xs[bass.ds((j0 + u + 2) * 128, 128), :]).then_inc(xg_in[u], 16)
                for u in range(2):
                    sp.wait_ge(S["y_evac"], j0 + u + 3)
                    sp.dma_start(ys[bass.ds((j0 + u) * 128, 128), :], yo[:, bass.ds(j0 + u, 1), :]).then_inc(y_out[u], 16)
            for u in range(2):
                sp.wait_ge(S["y_evac"], NS + u + 1)
                sp.dma_start(ys[(NS - 2 + u) * 128:(NS - 1 + u) * 128, :], yo[:, NS - 2 + u, :]).then_inc(y_out[u], 16)
            sp.wait_ge(S["hout"], FINAL)
            for i in range(IPT):
                sp.dma_start(out.rearrange("(t i) n d -> i n t d", i=IPT)[i], h[TOK * i:TOK * i + TOK, :, :]).then_inc(out_done, 16)
            sp.wait_ge(out_done, 16 * IPT)

        @block.gpsimd
        def _(pool):
            g = nc.gpsimd
            g.memset(clsmat[:], 0.0).then_inc(pool_const, 1)
            g.memset(eps[:], EPS).then_inc(pool_const, 1)
            g.memset(mhalf[:], -0.5).then_inc(pool_const, 1)
            g.memset(samp[:, :, :, 0:1], 0.0).then_inc(pool_const, 1)
            for i in range(4):
                g.memset(wmap[i][:, PIX:PIXP], 0.0).then_inc(pool_const, 1)
            pool.wait_ge(S["quant_dve"], 4)
            c = S["quant_pool"]
            for n, (raw, al, q) in enumerate(((raw1, view(alw1[:], [[0, 2], [1, FF]]), wq1),
                                              (raw2, view(alw2[:], [[0, FM], [1, D]]), wq2))):
                g.tensor_tensor(raw[:], raw[:], al, ALU.mult).then_inc(c, 1)
                pool.wait_ge(c, 4 * n + 1)
                g.tensor_scalar(raw[:], raw[:], -8.0, 7.0, ALU.max, ALU.min).then_inc(c, 1)
                pool.wait_ge(c, 4 * n + 2)
                g.tensor_scalar(raw[:], raw[:], MAGIC, None, ALU.add).then_inc(c, 1)
                pool.wait_ge(c, 4 * n + 3)
                g.tensor_scalar(q[:], raw[:], -MAGIC, None, ALU.add).then_inc(c, 1)

            g.memset(zeros[:], 0.0).then_inc(S["ms_small"], 1)
            g.memset(ones[:], 1.0).then_inc(S["ms_small"], 1)
            pool.wait_ge(S["ms_small"], 2)

            def ln_root(i, t, u, mvt, rst):
                n = i * NT + t + 1
                pool.wait_ge(S["ln_stat"], n)
                g.tensor_tensor(rst[u][:], mvt[u][:, 1:2], eps[:TT, 0:1], ALU.add).then_inc(S["ln_eps"], 1)
                pool.wait_ge(S["ln_eps"], n)
                g.tensor_tensor(rst[u][:], rst[u][:], mhalf[:TT, 0:1], ALU.pow).then_inc(S["ln_rstd"], 1)

            pool.wait_ge(h0_ready, NT)
            for u in range(2):
                g.memset(xT[u][KC:KC + 1, :, :], 1.0).then_inc(S["ms_small"], 1)
                g.memset(oT[u][KC:KC + 1, :, :], 1.0).then_inc(S["ms_small"], 1)
            pool.wait_ge(S["ms_small"], 6)
            pool.wait_ge(S["wt_in"], 16 * NW)

            def attention(l):
                with pool.Fori(0, NT - 1, 2) as t0:
                    for u in range(2):
                        ln_root(2 * l, t0 + u, u, mv, rstd)
                    if l == 0:
                        for u in range(2):
                            n = t0 + u + 1
                            pool.wait_ge(S["hv_ready"], n)
                            g.tensor_tensor(hvar[u][:], hvar[u][:], epsdh[:], ALU.add).then_inc(S["hv_eps"], 1)
                            pool.wait_ge(S["hv_eps"], n)
                            g.tensor_tensor(hvar[u][:], hvar[u][:], mhalf[:TT, 0:2 * H], ALU.pow).then_inc(S["hrstd_ready"], 1)
                            pool.wait_ge(S["hrstd_ready"], n)
                            g.tensor_tensor(qmask[u][:], view(hvar[u][:], [[1, 2 * H], [0, IPT]]),
                                            view(maskdh[:], [[0, 2 * H], [1, IPT]]), ALU.mult).then_inc(S["qmask_ready"], 1)
                    for u in range(2):
                        n = l * NT + t0 + u + 1
                        if l == 0:
                            pool.wait_ge(S["qmask_ready"], n)
                        pool.wait_ge(S["cen_ready"], n)
                        m = (bmask if l else qmask[u])
                        g.tensor_tensor(kx[u], view(cen[u][:, H, :], [[DH, H], [0, IPT], [1, DH]]),
                                        view(m[:, H, :], [[IPT, H], [1, IPT], [0, DH]]), ALU.mult).then_inc(S["kx_ready"], 1)

            for t in range(3):
                ln_root(0, t, t % 2, mv, rstd)

            def roots0(t, u):
                if has(t + 3):
                    ln_root(0, t + 3, 1 - u, mv, rstd)
            pipelined(pool, roots0)

            with pool.Fori(0, NT - IPT + 1, IPT) as t0:
                for i in range(IPT):
                    ln_root(1, t0 + i, i % 2, mv, rstd)
            def spread_keys(t, u):
                pool.wait_ge(S["kcp_ready"], t + 1)
                g.tensor_tensor(kx[u], view(kcp[u][:], [[DH, H], [0, IPT], [1, DH]]),
                                view(bmask[:], [[IPT, H], [1, IPT], [0, DH]]), ALU.mult).then_inc(S["kx_ready"], 1)

            for t in range(3):
                ln_root(2, t, t % 2, mv, rstd)
                if t < 2:
                    spread_keys(t, t)

            def roots1(t, u):
                if has(t + 2):
                    spread_keys(t + 2, u)
                if has(t + 3):
                    ln_root(2, t + 3, 1 - u, mv, rstd)
            pipelined(pool, roots1)

            pool.wait_ge(S["hattn_ready"], 2 * NT)
            for u in range(2):
                g.memset(mxT[u][KC:KC + 1, :, :], 1.0).then_inc(S["ms_small"], 1)
                g.memset(xgT[u][KC:KC + 1, :, :], 1.0).then_inc(S["ms_small"], 1)
            pool.wait_ge(S["ms_small"], 10)
            with pool.Fori(0, NT - 1, 2) as t0:
                for u in range(2):
                    ln_root(3, t0 + u, u, mmv, mrstd)
            pool.wait_ge(S["slot_ready"], 1)
            pool.wait_ge(S["mxn_ready"], NT)
            pool.wait_ge(S["zero_in"], 16)
            for t in range(NT):
                g.indirect_dma_start(out=xs, out_offset=bass.IndirectOffsetOnAxis(ap=slot[:, t:t + 1], axis=0),
                                     in_=mxn[:, t, :], in_offset=None).then_inc(S["scat_done"], 16)
            for u in range(2):
                pool.wait_ge(y_out[u], 16 * (NS // 2))
            for t in range(NT):
                g.indirect_dma_start(out=yg[:, t, :], out_offset=None, in_=ys,
                                     in_offset=bass.IndirectOffsetOnAxis(ap=slot[:, t:t + 1], axis=0)).then_inc(S["gath_done"], 16)

        @block.tensor
        def _(pe):
            mm = nc.tensor.matmul

            def stem(t, u, c, first=False):
                if c == 0:
                    pe.wait_ge(x_in[u], 32 if first else 16 * (t - u) + 32)
                if not (first and c == 0):
                    pe.wait_ge(hpix_ready, IPT * t + 2 * c)
                for k in range(NK):
                    for r in range(2):
                        m = mm(stem_ps[r][:PK, k * C1:(k + 1) * C1], xcol[u][64 * r:64 * r + 49, c, k * PK:(k + 1) * PK],
                               wstem[64 * r:64 * r + 49, :], start=True, stop=True)
                        if k == NK - 1:
                            m.then_inc(stem_ready, 1)

            def turn_stem(t, u, b, first=False):
                pe.wait_ge(hpix_ready, IPT * t + b + 1)
                if not (first and b < 2):
                    pe.wait_ge(tr_evac, TG * t + b - 1)
                for k in range(NK):
                    m = nc.tensor.transpose(bank[b % 2][:C1, k * PK:(k + 1) * PK], hpix[u][:, b, k, :], ident[:PK, :PK])
                m.then_inc(tr_ready, 1)

            def offsets(t):
                pe.wait_ge(tr_evac, TG * t + IPT)
                for k in range(TAPS):
                    at = (k // KP) * G1 + k % KP
                    m = mm(off_ps, woff[:, k, :], view(hch[:, 0, :], [[PIXP, IPT], [KP * G1, G2], [KP, G2]], at),
                           start=(k == 0), stop=(k == TAPS - 1))
                m.then_inc(off_ready, 1)

            def turn_offsets(t):
                pe.wait_ge(off_evac, t + 1)
                mm(offT_ps, offsb[:], ident[:2 * TAPS, :2 * TAPS], start=True, stop=True).then_inc(offT_ready, 1)

            def turn_map(t, k):
                pe.wait_ge(wmap_ready, TAPS * t + k + 1)
                pe.wait_ge(tr_evac, TG * t + IPT + k - 1)
                for j in range(NK):
                    m = nc.tensor.transpose(bank[k % 2][:PK, j * TP:(j + 1) * TP],
                                            wmap[k % 4][:, j * PK:(j + 1) * PK], ident[:TP, :TP])
                m.then_inc(tr_ready, 1)

            def sample(t, u, b, k0, k1):
                if k0 == 0 and not (isinstance(t, int) and t == 0 and b < 2):
                    pe.wait_ge(samp_evac, IPT * t + b - 1)
                for k in range(k0, k1):
                    m = mm(samp_ps[b % 2][:C1, 0:TAPS * POS], hpix[u][:, b, k, :],
                           wmapT[u][:, k, :, b * POS:(b + 1) * POS], start=(k == 0), stop=(k == NK - 1))
                if k1 == NK:
                    m.then_inc(samp_ready, 1)

            def tile(t, u, nxt):
                n, un = t + 1, 1 - u
                if nxt:
                    stem(n, un, 0)
                pe.wait_ge(tr_evac, TG * t + TG)
                sample(t, u, 0, 0, 2)
                if nxt:
                    stem(n, un, 1)
                sample(t, u, 0, 2, 4)
                if nxt:
                    turn_stem(n, un, 0)
                    turn_stem(n, un, 1)
                sample(t, u, 1, 0, 2)
                if nxt:
                    turn_stem(n, un, 2)
                    turn_stem(n, un, 3)
                sample(t, u, 1, 2, 4)
                if nxt:
                    offsets(n)
                sample(t, u, 2, 0, 1)
                if nxt:
                    turn_offsets(n)
                sample(t, u, 2, 1, 4)
                sample(t, u, 3, 0, 3)
                if nxt:
                    turn_map(n, 0)
                sample(t, u, 3, 3, 4)
                if nxt:
                    turn_map(n, 1)
                pe.wait_ge(samp_evac, IPT * t + IPT)
                for k in range(TAPS):
                    mm(dcn_ps, view(samp[:, k, 0, 0:1], [[1, TT]]), wdcn[:, k, :], start=(k == 0), stop=False)
                    if nxt and k < TAPS - 2:
                        turn_map(n, k + 2)
                mm(dcn_ps, notcls[:], shift2[:], start=False, stop=True).then_inc(dcn_ready, 1)

            pe.wait_ge(par_ready, 4)
            pe.wait_ge(pool_const, 8)
            pe.wait_ge(ones_ready, 4)
            stem(0, 0, 0, first=True)
            stem(0, 0, 1, first=True)
            for b in range(IPT):
                turn_stem(0, 0, b, first=True)
            offsets(0)
            turn_offsets(0)
            for k in range(TAPS):
                turn_map(0, k)
            tile(0, 0, True)
            with pe.Fori(1, NT - 1, 2) as t:
                for u in (1, 0):
                    tile(t + (1 - u), u, True)
            tile(NT - 1, 1, False)

            tr = nc.tensor.transpose
            W = TOK + NREL
            pe.wait_ge(S["wt_in"], 16 * NW)
            pe.wait_ge(S["ms_small"], 6)

            def turn_tokens(l, t, u):
                pe.wait_ge(S["ln_norm"], 2 * l * NT + t + 1)
                if not (l == 0 and isinstance(t, int) and t == 0):
                    pe.wait_ge(S["v_evac"], l * NT + t)
                for c in range(2):
                    m = tr(xT_ps[:, c * TT:(c + 1) * TT], xn[u][:, c * KC:(c + 1) * KC], ident[:TT, :TT])
                m.then_inc(S["xT_tr"], 1)

            def qkv(l, t, u, first=False):
                n = l * NT + t
                pe.wait_ge(S["xT_evac"], n + 1)
                if not first:
                    pe.wait_ge(S["qx_ready"], n)
                    if l and not (isinstance(t, int) and t == 0):
                        pe.wait_ge(S["kcp_ready"], t)
                for c in range(2):
                    mm(qk_ps, xT[u][0:KC + c, c, :], wqkv[l][0:KC + c, c, 0:2 * D], start=(c == 0), stop=(c == 1))
                for c in range(2):
                    m = mm(v_ps, xT[u][0:KC + c, c, :], wqkv[l][0:KC + c, c, 2 * D:3 * D], start=(c == 0), stop=(c == 1))
                m.then_inc(S["qkv_ready"], 1)

            def project(l, t, u, dst):
                pe.wait_ge(S["oT_evac"], l * NT + t + 1)
                for c in range(2):
                    m = mm(dst, oT[u][0:KC + c, c, :], wproj[l][0:KC + c, c, :], start=(c == 0), stop=(c == 1))
                m.then_inc(S["proj_ready"], 1)

            def turn_qk0(t, u):
                pe.wait_ge(S["qx_ready"], t + 1)
                for c in range(3):
                    tr(bank[3][:, c * TT:(c + 1) * TT], view(qkp[u][:, 4 * c, :], [[1, 128]]), ident[:TT, :TT])
                    m = tr(bank[0][:, c * TT:(c + 1) * TT], view(qkp[u][:, H + 4 * c, :], [[1, 128]]), ident[:TT, :TT])
                m.then_inc(S["qT_tr"], 1)

            def scores0(t, u):
                pe.wait_ge(S["qT_evac"], t + 1)
                if not (isinstance(t, int) and t == 0):
                    pe.wait_ge(S["o_evac"], t)
                for c in range(3):
                    for j in range(4):
                        rows = slice(32 * j, 32 * j + DH + IPT)
                        m = mm(bank[4 + j][:TT, c * TT:(c + 1) * TT], qT[u][rows, 3 + c, :], qT[u][rows, c, :], start=True, stop=True)
                m.then_inc(S["s_ready"], 1)

            def values0(t, u):
                pe.wait_ge(S["exp_ready"], t + 1)
                pe.wait_ge(S["v_evac"], t + 1)
                for j in range(4):
                    for c in range(3):
                        m = mm(bank[4 + j][:TT, 320 + c * (DH + 1):320 + (c + 1) * (DH + 1)], pT0[u][:, 3 * j + c, :],
                               vaug[u][:, 4 * c + j, :], start=True, stop=True)
                m.then_inc(S["o_ready"], 1)

            def turn_out0(t, u):
                pe.wait_ge(S["o_evac"], t + 1)
                if has(t + 2):
                    pe.wait_ge(S["v_evac"], t + 3)
                for c in range(2):
                    m = tr(xT_ps[:, c * TT:(c + 1) * TT], osb[u][:, c * KC:(c + 1) * KC], ident[:TT, :TT])
                m.then_inc(S["oT_tr"], 1)

            def tile0(t, u):
                values0(t, u)
                if has(t + 1):
                    turn_qk0(t + 1, 1 - u)
                if has(t + 2):
                    turn_tokens(0, t + 2, u)
                    qkv(0, t + 2, u)
                if has(t + 1):
                    scores0(t + 1, 1 - u)
                turn_out0(t, u)
                project(0, t, u, proj0_ps)

            pe.wait_ge(S["blk_const"], 1)
            for t in range(2):
                turn_tokens(0, t, t)
                qkv(0, t, t, first=(t == 0))
            turn_qk0(0, 0)
            scores0(0, 0)
            pipelined(pe, tile0)

            pe.wait_ge(S["quant_pool"], 8)
            pe.wait_ge(S["quant_dve"], 9)
            with pe.Fori(0, NT // IPT) as c4:
                for i in range(IPT):
                    t = IPT * c4 + i
                    pe.wait_ge(S["fq3"], t + 1)
                    if i >= 2:
                        pe.wait_ge(S["xqT_evac"], t - 1)
                    for c in range(2):
                        m = tr(bank[i % 2][:KC, :].bitcast(BF16)[:, c * TT:c * TT + TT], xq[i % 2][:, c * KC:c * KC + KC], identb[:TT, :TT])
                    m.then_inc(S["xqT_tr"], 1)
                pe.wait_ge(S["xqT_evac"], IPT * c4 + IPT)
                for k in range(FM):
                    if k >= 4:
                        pe.wait_ge(S["gel_ready"], FM * c4 + k - 3)
                    for c in range(2):
                        m = mm(bank[2 + k % 4][:, 0:IPT * TT], wq1[:, c, 128 * k:128 * k + 128], xqT[:, c, :], start=(c == 0), stop=(c == 1))
                    m.then_inc(S["fh_ready"], 1)
                pe.wait_ge(S["hq_ready"], FM * c4 + FM)
                for i in range(IPT):
                    if i >= 2:
                        pe.wait_ge(S["f2_scaled"], IPT * c4 + i - 1)
                    for k in range(FM):
                        m = mm(bank[i % 2][:TT, 0:D], hq[:, k, i * TT:(i + 1) * TT], wq2[:, k, :], start=(k == 0), stop=(k == FM - 1))
                    m.then_inc(S["f2_ready"], 1)

            def turn_qk1(t, u):
                n = NT + t + 1
                pe.wait_ge(S["qx_ready"], n)
                for p in range(H // 2):
                    m = tr(bank[4 + p // 3][:, (p % 3) * TT:(p % 3 + 1) * TT], view(qx[u][:, 2 * p, :, :], [[1, 128]]), ident[:TT, :TT])
                m.then_inc(S["qT_tr"], 1)
                pe.wait_ge(S["kx_ready"], t + 1)
                if not (isinstance(t, int) and t == 0):
                    pe.wait_ge(S["se_ready"], t)
                for p in range(H // 2):
                    m = tr(bank[6 + p // 3][:, (p % 3) * TT:(p % 3 + 1) * TT], view(kx[u][:, 2 * p, :, :], [[1, 128]]), ident[:TT, :TT])
                m.then_inc(S["kT_ready"], 1)

            def scores1(t, u):
                pe.wait_ge(S["qT_evac"], NT + t + 1)
                pe.wait_ge(S["ke_ready"], t + 1)
                for p in range(H // 2):
                    for r in range(2):
                        m = mm(bank[6 + r][:TT, p * W:(p + 1) * W], qT[u][64 * r:64 * r + 64, p, :],
                               ke[u][64 * r:64 * r + 64, p, :], start=True, stop=True)
                m.then_inc(S["s_ready"], 1)

            def turn_probs(t, u):
                pe.wait_ge(S["px_ready"], t + 1)
                if not (isinstance(t, int) and t == 0):
                    pe.wait_ge(S["hattn_ready"], NT + t)
                for q in range(3):
                    if q == 2:
                        pe.wait_ge(S["pT_evac"], 3 * t + 1)
                    for k in range(4 * q, 4 * q + 4):
                        m = tr(bank[(3, 0, 3)[q]][:TT, (k % 4) * TT:(k % 4 + 1) * TT], px[u][:, k, :], ident[:TT, :TT])
                    m.then_inc(S["pT_tr"], 1)

            def values1(t, u):
                pe.wait_ge(S["pT_evac"], 3 * t + 3)
                pe.wait_ge(S["v_evac"], NT + t + 1)
                for half in range(2):
                    for i in range(6):
                        hd = 6 * half + i
                        k = 6 * (hd % 2) + hd // 2
                        m = mm(bank[0][:KC, half * TT:(half + 1) * TT], vz[u][:, half, i, :], pT[u][:, k, :],
                               start=(i == 0), stop=(i == 5))
                m.then_inc(S["oT_tr"], 1)

            def tile1(t, u):
                if has(t + 1):
                    turn_qk1(t + 1, 1 - u)
                if has(t + 2):
                    turn_tokens(1, t + 2, u)
                    qkv(1, t + 2, u)
                if has(t + 1):
                    scores1(t + 1, 1 - u)
                turn_probs(t, u)
                values1(t, u)
                project(1, t, u, proj1_ps)

            pe.wait_ge(S["attn_par"], 16 * NL)
            pe.wait_ge(S["blk_const"], 2)
            for t in range(2):
                turn_tokens(1, t, t)
                qkv(1, t, t)
            turn_qk1(0, 0)
            scores1(0, 0)
            pipelined(pe, tile1)

            pe.wait_ge(S["ms_small"], 10)
            with pe.Fori(0, NT - 1, 2) as t0:
                for u in range(2):
                    pe.wait_ge(S["ln_norm"], 3 * NT + t0 + u + 1)
                    for c in range(2):
                        m = tr(bank[4 * u][:KC, c * TT:c * TT + TT], mx1[u][:, c * KC:c * KC + KC], ident[:TT, :TT])
                    m.then_inc(S["xT_tr"], 1)
                for u in range(2):
                    pe.wait_ge(S["xT_evac"], 2 * NT + t0 + u + 1)
                    for c in range(2):
                        m = mm(bank[4 * u + 1][:TT, 0:E], mxT[u][0:KC + c, c, :], wr[0:KC + c, c, :], start=(c == 0), stop=(c == 1))
                    m.then_inc(S["lg_ready"], 1)
                for u in range(2):
                    pe.wait_ge(S["hot_ready"], t0 + u + 1)
                    for c in range(2):
                        m = mm(bank[4 * u + 2][:TT, c * E:(c + 1) * E], tri[:, c, :], hot[:, bass.ds(t0 + u, 1), :], start=True, stop=True)
                    m.then_inc(S["rk_ready"], 1)
            pe.wait_ge(S["moe_in"], 48)
            pe.wait_ge(S["owner_ready"], 1)
            with pe.Fori(0, NS - 1, 2) as j0:
                ex = []
                for u in range(2):
                    ex.append(nc.tensor.value_load(owner[0:1, bass.ds(j0 + u, 1)], min_val=0, max_val=E - 1))
                for u in range(2):
                    pe.wait_ge(xg_in[u], 8 * j0 + 16)
                    for c in range(2):
                        m = tr(bank[4 * u][:KC, c * 128:c * 128 + 128], xg[u][:, c * KC:c * KC + KC], ident[:])
                    m.then_inc(S["xgT_tr"], 1)
                for u in range(2):
                    pe.wait_ge(S["xgT_evac"], j0 + u + 1)
                    pe.wait_ge(S["y_evac"], j0 + u + 1)
                    for f in range(2):
                        for c in range(2):
                            wv = w1[0:KC + c, bass.ds(ex[u], 1), c, f * 384:(f + 1) * 384]
                            m = mm(bank[4 * u + 1 + f][:, 0:384], xgT[u][0:KC + c, c, :], wv, start=(c == 0), stop=(c == 1))
                    m.then_inc(S["hid_ready"], 1)
                for u in range(2):
                    pe.wait_ge(S["hgel_ready"], j0 + u + 1)
                    for k in range(FM):
                        m = tr(bank[4 * u + 3 * (k // 3)][:, (k % 3) * 128:(k % 3 + 1) * 128], hid[u][:, k * 128:(k + 1) * 128], ident[:])
                    m.then_inc(S["hT_tr"], 1)
                for u in range(2):
                    pe.wait_ge(S["hTa_evac"], j0 + u + 1)
                    pe.wait_ge(S["hTb_evac"], j0 + u + 1)
                    for k in range(FM):
                        mm(bank[4 * u + 1][:, 0:D], hT[u][:, k, :], w2[:, bass.ds(ex[u], 1), k, :], start=(k == 0), stop=False)
                    mm(bank[4 * u + 1][:, 0:D], ones[:], eb2[:, bass.ds(ex[u], 1), :], start=False, stop=True).then_inc(S["y_ready"], 1)

        @block.scalar
        def _(act):
            def front(t, u, first=False):
                for b in range(IPT):
                    act.wait_ge(stem_ready, IPT * t + b + 1)
                    if not (first and b < 2):
                        act.wait_ge(hpix_ready, IPT * t + b - 1)
                    nc.scalar.activation(leak[b % 2][:], stem_ps[b % 2][:PK, 0:NK * C1], ACT.Copy,
                                         scale=SLOPE).then_inc(leak_ready, 1)
                for b in range(IPT):
                    act.wait_ge(tr_ready, TG * t + b + 1)
                    nc.scalar.activation(hch[:, b, :], bank[b % 2][:C1, 0:PIXP], ACT.Copy).then_inc(tr_evac, 1)
                act.wait_ge(off_ready, t + 1)
                nc.scalar.activation(offsb[:], off_ps, ACT.Copy).then_inc(off_evac, 1)
                act.wait_ge(dist_ready, t + 1)
                nc.scalar.activation(dist[:], dist[:], ACT.Abs).then_inc(abs_ready, 1)
                act.wait_ge(abs_ready, t + 1)
                nc.scalar.activation(tent[:], dist[:], ACT.Relu, bias=1.0, scale=-1.0).then_inc(tent_ready, 1)

            def turn_map(t, u, k):
                act.wait_ge(tr_ready, TG * t + IPT + k + 1)
                nc.scalar.activation(wmapT[u][:, :, k, :],
                                     view(bank[k % 2][:PK, 0:1], [[TP, NK], [1, TP]]), ACT.Copy).then_inc(tr_evac, 1)

            def tile(t, u, nxt):
                if nxt:
                    front(t + 1, 1 - u)
                    for k in range(TAPS):
                        turn_map(t + 1, 1 - u, k)
                act.wait_ge(dcn_ready, t + 1)
                nc.scalar.activation(dleak[:], dcn_ps, ACT.Copy, scale=SLOPE).then_inc(dleak_ready, 1)

            front(0, 0, first=True)
            for k in range(TAPS):
                turn_map(0, 0, k)
            tile(0, 0, True)
            with act.Fori(1, NT - 1, 2) as t:
                for u in (1, 0):
                    tile(t + (1 - u), u, True)
            tile(NT - 1, 1, False)

            def copy(dst, src):
                return nc.scalar.activation(dst, src, ACT.Copy)

            def tokens_out(l, t, u):
                act.wait_ge(S["xT_tr"], l * NT + t + 1)
                copy(xT[u][0:KC, :, :], xT_ps).then_inc(S["xT_evac"], 1)

            def squares(t, u):
                act.wait_ge(S["qkv_ready"], t + 1)
                nc.scalar.activation(view(se[u][:], [[1, 2 * D]]), qk_ps, ACT.Square).then_inc(S["sq_ready"], 1)

            def values_out0(t, u):
                act.wait_ge(S["qkv_ready"], t + 1)
                copy(vaug[u][:, :, 0:DH], view(v_ps, [[DH, H], [1, DH]])).then_inc(S["v_evac"], 1)

            def qk_out0(t, u):
                act.wait_ge(S["qT_tr"], t + 1)
                copy(qT[u][:, 0:3, :], bank[3][:, 0:3 * TT])
                copy(qT[u][:, 3:6, :], bank[0][:, 0:3 * TT]).then_inc(S["qT_evac"], 1)

            def exp0(t, u):
                act.wait_ge(S["s_ready"], t + 1)
                nc.scalar.activation(view(pT0[u][:], [[3 * TT, 4], [1, 3 * TT]]), view(bank[4][:TT, :], [[512, 4], [1, 3 * TT]]), ACT.Exp,
                                     scale=DH ** 0.5).then_inc(S["exp_ready"], 1)

            def tile0(t, u):
                if has(t + 1):
                    qk_out0(t + 1, 1 - u)
                if has(t + 2):
                    tokens_out(0, t + 2, u)
                    squares(t + 2, u)
                    act.wait_ge(S["o_ready"], t + 1)
                    values_out0(t + 2, u)
                if has(t + 1):
                    exp0(t + 1, 1 - u)
                act.wait_ge(S["oT_tr"], t + 1)
                copy(oT[u][0:KC, :, :], xT_ps).then_inc(S["oT_evac"], 1)

            act.wait_ge(S["blk_const"], 1)
            for t in range(2):
                tokens_out(0, t, t)
                squares(t, t)
                values_out0(t, t)
            qk_out0(0, 0)
            exp0(0, 0)
            pipelined(act, tile0)

            act.wait_ge(S["quant_dve"], 9)
            with act.Fori(0, NT // IPT) as c4:
                for i in range(IPT):
                    act.wait_ge(S["xqT_tr"], IPT * c4 + i + 1)
                    copy(xqT[:, :, i * TT:(i + 1) * TT], view(bank[i % 2][:KC, :].bitcast(BF16), [[TT, 2], [1, TT]])).then_inc(S["xqT_evac"], 1)
                for k in range(FM):
                    act.wait_ge(S["fh_ready"], FM * c4 + k + 1)
                    if k >= 2:
                        act.wait_ge(S["hq_ready"], FM * c4 + k - 1)
                    nc.scalar.activation(gel[k % 2][:], bank[2 + k % 4][:, 0:IPT * TT], ACT.Gelu, bias=fb1[:, k:k + 1],
                                         scale=s1[:, k:k + 1]).then_inc(S["gel_ready"], 1)
            def keys_out(t, u):
                act.wait_ge(S["qkv_ready"], NT + t + 1)
                copy(kcp[u][:], qk_ps[:, D:2 * D]).then_inc(S["kcp_ready"], 1)

            def values_out1(t, u):
                act.wait_ge(S["qkv_ready"], NT + t + 1)
                for half in range(2):
                    m = copy(view(vz[u][:, half, 0, :], [[KC + DH, 6], [1, DH]]), view(v_ps[:, half * KC:], [[DH, 6], [1, DH]]))
                m.then_inc(S["v_evac"], 1)

            def queries_out(t, u):
                act.wait_ge(S["qT_tr"], NT + t + 1)
                copy(view(qT[u][:], [[3 * TT, 2], [1, 3 * TT]]), view(bank[4], [[512, 2], [1, 3 * TT]])).then_inc(S["qT_evac"], 1)

            def scores_out(t, u):
                act.wait_ge(S["s_ready"], NT + t + 1)
                copy(se[u][:], psum[:TT, 6:8, 0:H // 2 * (TOK + NREL)]).then_inc(S["se_ready"], 1)

            def tile1(t, u):
                if has(t + 1):
                    queries_out(t + 1, 1 - u)
                if has(t + 2):
                    tokens_out(1, t + 2, u)
                    keys_out(t + 2, u)
                if has(t + 1):
                    scores_out(t + 1, 1 - u)
                act.wait_ge(S["sc_ready"], t + 1)
                nc.scalar.activation(prob[u][:], sc[u][:], ACT.Exp, scale=DH ** -0.5).then_inc(S["exp1_ready"], 1)
                for q in range(3):
                    act.wait_ge(S["pT_tr"], 3 * t + q + 1)
                    copy(pT[u][:, 4 * q:4 * q + 4, :], bank[(3, 0, 3)[q]][:TT, 0:4 * TT]).then_inc(S["pT_evac"], 1)
                act.wait_ge(S["oT_tr"], NT + t + 1)
                copy(oT[u][0:KC, :, :], bank[0][:KC, 0:2 * TT]).then_inc(S["oT_evac"], 1)
                if has(t + 2):
                    values_out1(t + 2, u)

            act.wait_ge(S["blk_const"], 2)
            for t in range(2):
                tokens_out(1, t, t)
                keys_out(t, t)
                values_out1(t, t)
            queries_out(0, 0)
            scores_out(0, 0)
            pipelined(act, tile1)

            with act.Fori(0, NT - 1, 2) as t0:
                for u in range(2):
                    act.wait_ge(S["xT_tr"], 2 * NT + t0 + u + 1)
                    copy(mxT[u][0:KC, :, :], bank[4 * u][:KC, 0:2 * TT]).then_inc(S["xT_evac"], 1)
                for u in range(2):
                    act.wait_ge(S["lsh_ready"], t0 + u + 1)
                    nc.scalar.activation(lex[u][:], lsh[u][:], ACT.Exp).then_inc(S["lex_ready"], 1)
            with act.Fori(0, NS - 1, 2) as j0:
                for u in range(2):
                    act.wait_ge(S["xgT_tr"], j0 + u + 1)
                    copy(xgT[u][0:KC, :, :], bank[4 * u][:KC, 0:256]).then_inc(S["xgT_evac"], 1)
                for u in range(2):
                    act.wait_ge(S["hid_ready"], j0 + u + 1)
                    nc.scalar.activation(hid[u][:], psum[:, 4 * u + 1:4 * u + 3, 0:384], ACT.Gelu).then_inc(S["hgel_ready"], 1)
                for u in range(2):
                    act.wait_ge(S["hT_tr"], j0 + u + 1)
                    copy(hT[u][:, 0:3, :], bank[4 * u][:, 0:384]).then_inc(S["hTa_evac"], 1)

        @block.vector
        def _(dve):
            v = nc.vector
            def root(x, y, w, eps_, done, n, each=1):
                def step(ins):
                    nonlocal n
                    ins.then_inc(done, 1)
                    n = n + 1
                    dve.wait_ge(done, n)
                step(v.tensor_scalar(x, x, eps_, None, ALU.add))
                step(v.tensor_scalar(y.bitcast(I32), x.bitcast(I32), -0.5, float(0x5f3759df), ALU.mult, ALU.add))
                for _ in range(3):
                    step(v.scalar_tensor_tensor(w, y, -0.5, y, ALU.mult, ALU.mult))
                    step(v.tensor_tensor(w, w, x, ALU.mult))
                    step(v.scalar_tensor_tensor(y, w, 1.5, y, ALU.add, ALU.mult))
                return n

            for u in range(2):
                for r in range(2):
                    v.memset(xcol[u][64 * r:64 * r + 1, :, :], 1.0).then_inc(ones_ready, 1)

            dve.wait_ge(par_in, 16 * NPAR)
            n = root(bn1[:, 3, :], inv1[:], bnw[:64 + 49, 0:C1], EPS, bn_pow, 0)
            n = root(bn2[:, 3, :], inv2[:], bnw[:C1, :], EPS, bn_pow, n)
            v.tensor_tensor(inv1[:], inv1[:], bn1[:, 0, :], ALU.mult).then_inc(bn_pow, 1)
            v.tensor_tensor(inv2[:], inv2[:], bn2[:, 0, :], ALU.mult).then_inc(bn_pow, 1)
            dve.wait_ge(bn_pow, n + 2)
            v.tensor_tensor(wstem[:], wstem[:], inv1[:], ALU.mult).then_inc(fold, 1)
            v.tensor_tensor(wdcn[:], wdcn[:], view(inv2[:], [[0, TAPS], [1, D]]), ALU.mult).then_inc(par_ready, 1)
            v.tensor_tensor(shift1[:], bn1[:, 2, :], inv1[:], ALU.mult).then_inc(fold, 1)
            v.tensor_tensor(shift2[:], bn2[0:1, 4, :], bn2[0:1, 2, :], ALU.subtract).then_inc(fold, 1)
            v.tensor_tensor(posbase[:], base[:], off_bias[:], ALU.add).then_inc(par_ready, 1)
            dve.wait_ge(fold, 3)
            v.tensor_tensor(shift1[:], bn1[:, 1, :], shift1[:], ALU.subtract).then_inc(fold, 1)
            v.tensor_tensor(shift2[:], shift2[:], inv2[0:1, :], ALU.mult).then_inc(fold, 1)
            dve.wait_ge(fold, 5)
            v.tensor_tensor(wstem[0:1, :], wstem[0:1, :], shift1[0:1, :], ALU.add)
            v.tensor_tensor(wstem[64:65, :], wstem[64:65, :], shift1[64:65, :], ALU.add).then_inc(par_ready, 1)
            v.tensor_tensor(shift2[:], shift2[:], bn2[0:1, 1, :], ALU.add).then_inc(par_ready, 1)
            dve.wait_ge(par_ready, 4)
            dve.wait_ge(pool_const, 8)

            def leaky(t, u, b):
                dve.wait_ge(leak_ready, IPT * t + b + 1)
                v.tensor_tensor(hpix[u][:, b, :, :], stem_ps[b % 2][:PK, 0:NK * C1], leak[b % 2][:],
                                ALU.max).then_inc(hpix_ready, 1)

            def distances(t):
                dve.wait_ge(offT_ready, t + 1)
                v.tensor_tensor(pxy[:], offT_ps, posbase[:], ALU.add).then_inc(pxy_ready, 1)
                dve.wait_ge(pxy_ready, t + 1)
                v.tensor_tensor(dist[:], view(pxy[:], [[1, 2 * TAPS], [0, G1]]),
                                view(iota21[:], [[0, 2 * TAPS], [1, G1]]), ALU.subtract).then_inc(dist_ready, 1)

            def make_map(t, k):
                if k >= 4:
                    dve.wait_ge(tr_ready, TG * t + k + 1)
                v.tensor_tensor(view(wmap[k % 4][:], [[G1, G1], [1, G1]]),
                                view(tent[:, k, :], [[1, G1], [0, G1]]),
                                view(tent[:, TAPS + k, :], [[0, G1], [1, G1]]), ALU.mult).then_inc(wmap_ready, 1)

            def sampled(t, b):
                dve.wait_ge(samp_ready, IPT * t + b + 1)
                v.tensor_copy(samp[:, :, b, 1:TOK],
                              view(samp_ps[b % 2][:C1, 0:1], [[POS, TAPS], [1, POS]])).then_inc(samp_evac, 1)

            def tile(t, u, nxt):
                n, un = t + 1, 1 - u
                if nxt:
                    for b in range(IPT):
                        leaky(n, un, b)
                sampled(t, 0)
                sampled(t, 1)
                if nxt:
                    distances(n)
                sampled(t, 2)
                if nxt:
                    dve.wait_ge(tent_ready, n + 1)
                    make_map(n, 0)
                    make_map(n, 1)
                sampled(t, 3)
                if nxt:
                    for k in range(2, TAPS):
                        make_map(n, k)
                dve.wait_ge(dleak_ready, t + 1)
                v.tensor_tensor(dmax[:], dcn_ps, dleak[:], ALU.max).then_inc(dmax_ready, 1)
                dve.wait_ge(dmax_ready, t + 1)
                v.tensor_tensor(h[:, bass.ds(t, 1), :], dmax[:], clsmat[:], ALU.add).then_inc(h0_ready, 1)

            q = S["quant_dve"]
            dve.wait_ge(S["quant_in"], 16 * len(quant))
            v.tensor_reduce(am[:, 0:1], ala1[:], AX.X, ALU.add).then_inc(S["fc_done"], 1)
            v.tensor_reduce(am[:, 1:2], ala2[:], AX.X, ALU.add).then_inc(S["fc_done"], 1)
            dve.wait_ge(S["fc_done"], 2)
            v.tensor_scalar(am[:, 0:1], am[:, 0:1], 1.0 / D, None, ALU.mult).then_inc(q, 1)
            v.tensor_scalar(am[:, 1:2], am[:, 1:2], 1.0 / FF, None, ALU.mult).then_inc(q, 1)
            dve.wait_ge(q, 2)
            v.tensor_tensor(row2[:], alw2[:TT, :], view(am[:TT, 1:2], [[0, D]]), ALU.mult).then_inc(S["fc_done"], 1)
            dve.wait_ge(S["fc_done"], 3)
            v.reciprocal(alw1[:], alw1[:]).then_inc(q, 1)
            v.reciprocal(alw2[:], alw2[:]).then_inc(q, 1)
            v.reciprocal(ram[:], am[:]).then_inc(q, 1)
            v.tensor_scalar(s1[:], alw1c[:], am[:, 0:1], None, ALU.mult).then_inc(q, 1)
            v.tensor_copy(identb[:], ident[:]).then_inc(q, 3)

            for b in range(IPT):
                leaky(0, 0, b)
            distances(0)
            dve.wait_ge(tent_ready, 1)
            for k in range(TAPS):
                make_map(0, k)
            tile(0, 0, True)
            with dve.Fori(1, NT - 1, 2) as t:
                for u in (1, 0):
                    tile(t + (1 - u), u, True)
            tile(NT - 1, 1, False)

            def mean(t0, i, x_sem, stt, mvt):
                for u in range(2):
                    dve.wait_ge(x_sem, t0 + u + 1 + (NT if i == 3 else 0))
                    v.bn_stats(stt[u][:], h[:, bass.ds(t0 + u, 1), :]).then_inc(S["ln_raw"], 1)
                dve.wait_ge(S["ln_raw"], i * NT + t0 + 2)
                v.memset(tick[:], 0.0)
                for u in range(2):
                    v.bn_aggr(mvt[u][:], stt[u][:]).then_inc(S["ln_stat"], 1)

            def norm(t, i, u, mvt, rst, dst):
                dve.wait_ge(S["ln_rstd"], i * NT + t + 1)
                v.tensor_scalar(dst, h[:, bass.ds(t, 1), :], mvt[u][:, 0:1], rst[u][:, 0:1],
                                ALU.subtract, ALU.mult).then_inc(S["ln_norm"], 1)

            def ln(l, t, u):
                i = 2 * l
                dve.wait_ge(S["hffn_ready"] if l else h0_ready, t + 1)
                v.bn_stats(stat[u][:], h[:, bass.ds(t, 1), :]).then_inc(S["ln_raw"], 1)
                dve.wait_ge(S["ln_raw"], i * NT + t + 1)
                v.memset(tick[:], 0.0)
                v.bn_aggr(mv[u][:], stat[u][:]).then_inc(S["ln_stat"], 1)

            def residual(l, t, src):
                dve.wait_ge(S["proj_ready"], l * NT + t + 1)
                v.tensor_tensor(h[:, bass.ds(t, 1), :], h[:, bass.ds(t, 1), :], src, ALU.add).then_inc(S["hattn_ready"], 1)

            dve.wait_ge(S["attn_par"], 16 * NL)
            dve.wait_ge(S["wt_in"], 16 * NW)
            wc = S["wc"]
            wq_ = view(wqkv[0][:], [[3 * D, 2], [DH, 2 * H], [1, DH]])
            v.tensor_reduce(wmean[:], wq_, AX.X, ALU.add).then_inc(wc, 1)
            for u in range(2):
                v.memset(qkx[u][:], 0.0).then_inc(wc, 1)
                v.memset(vaug[u][:], 1.0).then_inc(wc, 1)
            dve.wait_ge(wc, 5)
            v.tensor_scalar(wmean[:], wmean[:], 1.0 / DH, None, ALU.mult).then_inc(wc, 1)
            for u in range(2):
                v.tensor_scalar(view(qkp[u][:, 0, DH:], [[32, H], [1, IPT]]), view(mask[:], [[0, H], [1, IPT]]), -1.0, 64.0,
                                ALU.add, ALU.mult).then_inc(wc, 1)
                v.tensor_copy(view(qkp[u][:, H, DH:], [[32, H], [1, IPT]]), view(mask[:], [[0, H], [1, IPT]])).then_inc(wc, 1)
            dve.wait_ge(wc, 10)
            v.tensor_tensor(wq_, wq_, view(wmean[:], [[2 * H, 2], [1, 2 * H], [0, DH]]), ALU.subtract).then_inc(S["blk_const"], 1)

            def head_norm(t, u):
                n = root(hvar[u][:], hroot[u][:], hwork[u][:], DH * EPS, S["hr_ready"], 11 * t)
                v.tensor_tensor(qkp[u][:, :, 0:DH], view(qk_ps, [[DH, 2 * H], [1, DH]]), view(hroot[u][:], [[1, 2 * H], [0, DH]]),
                                ALU.mult).then_inc(S["qx_ready"], 1)

            def head_squares(t, u):
                dve.wait_ge(S["sq_ready"], t + 1)
                v.tensor_reduce(hvar[u][:], view(se[u][:], [[DH, 2 * H], [1, DH]]), AX.X, ALU.add).then_inc(S["hv_ready"], 1)
                dve.wait_ge(S["hv_ready"], t + 1)

            def tile0(t, u):
                dve.wait_ge(S["o_ready"], t + 1)
                o = view(bank[4][:TT, 320:], [[DH + 1, 3], [512, 4], [1, DH]])
                v.reciprocal(view(rsum[u][:], [[4, 3], [1, 4]]), view(bank[4][:TT, 320 + DH:], [[DH + 1, 3], [512, 4]])).then_inc(S["rr_ready"], 1)
                dve.wait_ge(S["rr_ready"], t + 1)
                v.tensor_tensor(view(osb[u][:], [[4 * DH, 3], [DH, 4], [1, DH]]), o, view(rsum[u][:], [[4, 3], [1, 4], [0, DH]]),
                                ALU.mult).then_inc(S["o_evac"], 1)
                if has(t + 2):
                    head_squares(t + 2, u)
                    head_norm(t + 2, u)
                if has(t + 3):
                    ln(0, t + 3, 1 - u)
                residual(0, t, proj0_ps)
                if has(t + 3):
                    norm(t + 3, 0, 1 - u, mv, rstd, xn[1 - u][:])

            for t in range(2):
                ln(0, t, t)
                norm(t, 0, t, mv, rstd, xn[t][:])
            for t in range(2):
                head_squares(t, t)
                head_norm(t, t)
                if t == 0:
                    ln(0, 2, 0)
                    norm(2, 0, 0, mv, rstd, xn[0][:])
            pipelined(dve, tile0)

            with dve.Fori(0, NT // IPT) as c4:
                for i in range(IPT):
                    u, t = i % 2, IPT * c4 + i
                    if u == 0:
                        mean(t, 1, S["hattn_ready"], stat, mv)
                    norm(t, 1, u, mv, rstd, xn[u][:])
                    dve.wait_ge(S["ln_norm"], NT + t + 1)
                    v.tensor_scalar(xn[u][:], xn[u][:], ram[:TT, 0:1], -8.0, ALU.mult, ALU.max).then_inc(S["fq1"], 1)
                    dve.wait_ge(S["fq1"], t + 1)
                    v.tensor_scalar(xn[u][:], xn[u][:], 7.0, MAGIC, ALU.min, ALU.add).then_inc(S["fq2"], 1)
                    dve.wait_ge(S["fq2"], t + 1)
                    if i >= 2:
                        dve.wait_ge(S["xqT_tr"], t - 1)
                    v.tensor_scalar(xq[u][:], xn[u][:], -MAGIC, None, ALU.add).then_inc(S["fq3"], 1)
                for k in range(FM):
                    gk, base_ = gel[k % 2], 3 * FM * c4 + 3 * k + 3
                    dve.wait_ge(S["gel_ready"], FM * c4 + k + 1)
                    v.tensor_scalar(gk[:], gk[:], -10.0, 10.0, ALU.max, ALU.min).then_inc(S["fc_done"], 1)
                    dve.wait_ge(S["fc_done"], base_ + 1)
                    v.tensor_scalar(gk[:], gk[:], ram[:, 1:2], -8.0, ALU.mult, ALU.max).then_inc(S["fc_done"], 1)
                    dve.wait_ge(S["fc_done"], base_ + 2)
                    v.tensor_scalar(gk[:], gk[:], 7.0, MAGIC, ALU.min, ALU.add).then_inc(S["fc_done"], 1)
                    dve.wait_ge(S["fc_done"], base_ + 3)
                    v.tensor_scalar(hq[:, k, :], gk[:], -MAGIC, None, ALU.add).then_inc(S["hq_ready"], 1)
                for i in range(IPT):
                    u, t = i % 2, IPT * c4 + i
                    ht = h[:, bass.ds(t, 1), :]
                    dve.wait_ge(S["f2_ready"], t + 1)
                    v.tensor_tensor(f2[u][:], bank[u][:TT, 0:D], row2[:], ALU.mult).then_inc(S["f2_scaled"], 1)
                    dve.wait_ge(S["f2_scaled"], t + 1)
                    v.tensor_tensor(f2[u][:], f2[u][:], ht, ALU.add).then_inc(S["f2_sum"], 1)
                    dve.wait_ge(S["f2_sum"], t + 1)
                    v.tensor_tensor(ht, f2[u][:], fb2[:], ALU.add).then_inc(S["hffn_ready"], 1)

            for u in range(2):
                v.memset(vz[u][:], 0.0).then_inc(wc, 1)
            dve.wait_ge(wc, 12)
            v.memset(tick[:], 0.0).then_inc(S["blk_const"], 1)

            def spread_queries(t, u):
                dve.wait_ge(S["qkv_ready"], NT + t + 1)
                v.tensor_tensor(qx[u], view(qk_ps, [[DH, H], [0, IPT], [1, DH]]),
                                view(bmask[:], [[IPT, H], [1, IPT], [0, DH]]), ALU.mult).then_inc(S["qx_ready"], 1)

            def keys(t, u):
                dve.wait_ge(S["kT_ready"], t + 1)
                for half in range(2):
                    m = v.tensor_reduce(ke[u][:, 3 * half:3 * half + 3, 0:TOK],
                                        view(bank[6 + half], [[TT, 3], [1, TOK], [TOK, IPT]]), AX.X, ALU.add)
                m.then_inc(S["ke_ready"], 1)

            def shifted(t, u):
                dve.wait_ge(S["se_ready"], t + 1)
                dve.wait_ge(rel_in[u], 32 * (t - u) + 64)
                v.tensor_tensor(sc[u][:], view(se[u][:], [[TOK + NREL, H], [1, TOK]]), rel[u][:], ALU.add).then_inc(S["sr_ready"], 1)
                dve.wait_ge(S["sr_ready"], t + 1)
                v.tensor_reduce(smax[u][:], sc[u][:], AX.X, ALU.max).then_inc(S["smax_ready"], 1)
                dve.wait_ge(S["smax_ready"], t + 1)
                v.tensor_tensor(sc[u][:], sc[u][:], view(smax[u][:], [[1, H], [0, TOK]]), ALU.subtract).then_inc(S["sc_ready"], 1)

            def probabilities(t, u):
                dve.wait_ge(S["exp1_ready"], t + 1)
                v.tensor_reduce(rsum[u][:], prob[u][:], AX.X, ALU.add).then_inc(S["rs_ready"], 1)
                dve.wait_ge(S["rs_ready"], t + 1)
                v.reciprocal(rsum[u][:], rsum[u][:]).then_inc(S["rr_ready"], 1)
                dve.wait_ge(S["rr_ready"], NT + t + 1)
                v.tensor_tensor(pmask[u][:], view(rsum[u][:], [[1, H], [0, IPT]]), view(mask[:], [[0, H], [1, IPT]]),
                                ALU.mult).then_inc(S["pmask_ready"], 1)
                dve.wait_ge(S["pmask_ready"], t + 1)
                v.tensor_tensor(view(px[u][:], [[TT, H], [TOK, IPT], [1, TOK]]), view(prob[u][:], [[TOK, H], [0, IPT], [1, TOK]]),
                                view(pmask[u][:], [[IPT, H], [1, IPT], [0, TOK]]), ALU.mult).then_inc(S["px_ready"], 1)

            def tile1(t, u):
                if has(t + 1):
                    keys(t + 1, 1 - u)
                probabilities(t, u)
                if has(t + 3):
                    ln(1, t + 3, 1 - u)
                if has(t + 2):
                    spread_queries(t + 2, u)
                if has(t + 3):
                    norm(t + 3, 2, 1 - u, mv, rstd, xn[1 - u][:])
                residual(1, t, proj1_ps)
                if has(t + 1):
                    shifted(t + 1, 1 - u)

            for t in range(2):
                ln(1, t, t)
                norm(t, 2, t, mv, rstd, xn[t][:])
            for t in range(2):
                spread_queries(t, t)
                if t == 0:
                    ln(1, 2, 0)
                    norm(2, 2, 0, mv, rstd, xn[0][:])
            keys(0, 0)
            shifted(0, 0)
            pipelined(dve, tile1)

            v.memset(cnt[1][:], 0.0).then_inc(S["cnt_ready"], 1)
            with dve.Fori(0, NT - 1, 2) as t0:
                mean(t0, 3, S["hattn_ready"], mstat, mmv)
                for u in range(2):
                    norm(t0 + u, 3, u, mmv, mrstd, mx1[u][:])
                for u in range(2):
                    t = t0 + u
                    dve.wait_ge(S["ln_norm"], 3 * NT + t + 1)
                    v.tensor_copy(mxn[:, bass.ds(t, 1), :], mx1[u][:]).then_inc(S["mxn_ready"], 1)
                for u in range(2):
                    t, n, lg = t0 + u, t0 + u + 1, bank[4 * u + 1][:TT, 0:E]
                    dve.wait_ge(S["lg_ready"], n)
                    v.tensor_reduce(lmax[u][:], lg, AX.X, ALU.max).then_inc(S["lmax_ready"], 1)
                    dve.wait_ge(S["lmax_ready"], n)
                    v.tensor_scalar(lsh[u][:], lg, lmax[u][:, 0:1], None, ALU.subtract).then_inc(S["lsh_ready"], 1)
                    dve.wait_ge(S["lsh_ready"], n)
                    v.scalar_tensor_tensor(cand[u][:], lsh[u][:], 0.0, rev[:], ALU.is_ge, ALU.mult).then_inc(S["cand_ready"], 1)
                    dve.wait_ge(S["cand_ready"], n)
                    v.tensor_reduce(cmax[u][:], cand[u][:], AX.X, ALU.max).then_inc(S["cmax_ready"], 1)
                    dve.wait_ge(S["cmax_ready"], n)
                    v.tensor_scalar(hot[:, bass.ds(t, 1), :], cand[u][:], cmax[u][:, 0:1], None, ALU.is_equal).then_inc(S["hot_ready"], 1)
                for u in range(2):
                    t, n = t0 + u, t0 + u + 1
                    dve.wait_ge(S["lex_ready"], n)
                    v.tensor_reduce(lsum[u][:], lex[u][:], AX.X, ALU.add).then_inc(S["lsum_ready"], 1)
                    dve.wait_ge(S["lsum_ready"], n)
                    v.reciprocal(pmax[:, bass.ds(t, 1)], lsum[u][:]).then_inc(S["pmax_ready"], 1)
                for u in range(2):
                    t, n = t0 + u, t0 + u + 1
                    dve.wait_ge(S["rk_ready"], n)
                    dve.wait_ge(S["cnt_ready"], n)
                    v.tensor_tensor(rank[:, bass.ds(t, 1), :], bank[4 * u + 2][:TT, 0:E], cnt[1 - u][:], ALU.add).then_inc(S["rank_ready"], 1)
                    v.tensor_tensor(cnt[u][:], bank[4 * u + 2][:TT, E:2 * E], cnt[1 - u][:], ALU.add).then_inc(S["cnt_ready"], 1)
            done = S["plan"]
            dve.wait_ge(S["cnt_ready"], NT + 1)
            v.tensor_scalar(ntile[:], cnt[1][:], 63.5, 1.0 / 128, ALU.add, ALU.mult).then_inc(done, 1)
            dve.wait_ge(done, 1)
            v.tensor_scalar(ntile[:], ntile[:], MAGIC, None, ALU.add).then_inc(done, 1)
            dve.wait_ge(done, 2)
            v.tensor_scalar(ntile[:], ntile[:], -MAGIC, None, ALU.add).then_inc(done, 1)
            dve.wait_ge(done, 3)
            v.tensor_tensor(cum[:], view(ntile[:], [[0, E], [1, E]]), upto[:], ALU.mult).then_inc(done, 1)
            dve.wait_ge(done, 4)
            v.tensor_reduce(ends[:], cum[:], AX.X, ALU.add).then_inc(done, 1)
            dve.wait_ge(done, 5)
            v.tensor_tensor(start[:], ends[:], ntile[:], ALU.subtract).then_inc(done, 1)
            dve.wait_ge(done, 6)
            v.tensor_scalar(start[:], start[:], 128.0, None, ALU.mult).then_inc(done, 1)
            dve.wait_ge(done, 7)
            dve.wait_ge(S["rank_ready"], NT)
            v.tensor_tensor(slotw[:], rank[:], view(start[:], [[0, NT], [1, E]]), ALU.add).then_inc(done, 1)
            dve.wait_ge(done, 8)
            v.tensor_tensor(slotw[:], slotw[:], hot[:], ALU.mult).then_inc(done, 1)
            dve.wait_ge(done, 9)
            v.tensor_reduce(slotf[:], slotw[:], AX.X, ALU.add).then_inc(done, 1)
            dve.wait_ge(done, 10)
            v.tensor_copy(slot[:], slotf[:]).then_inc(S["slot_ready"], 1)
            v.tensor_tensor(past[:], view(ends[0:1, :], [[0, NS], [1, E]]), view(tidx[:], [[1, NS], [0, E]]), ALU.is_le).then_inc(done, 1)
            dve.wait_ge(done, 11)
            v.tensor_reduce(own[:], past[:], AX.X, ALU.add).then_inc(done, 1)
            dve.wait_ge(done, 12)
            v.tensor_scalar(own[:], own[:], float(E - 1), None, ALU.min).then_inc(done, 1)
            dve.wait_ge(done, 13)
            v.tensor_copy(owner[:], own[:]).then_inc(S["owner_ready"], 1)
            v.memset(lsum[0][:], 0.0).then_inc(S["y_evac"], 2)
            with dve.Fori(0, NS - 1, 2) as j0:
                for u in range(2):
                    dve.wait_ge(S["hT_tr"], j0 + u + 1)
                    v.tensor_copy(hT[u][:, 3:6, :], bank[4 * u + 3][:, 0:384]).then_inc(S["hTb_evac"], 1)
                for u in range(2):
                    dve.wait_ge(S["y_ready"], j0 + u + 1)
                    v.tensor_copy(yo[:, bass.ds(j0 + u, 1), :], bank[4 * u + 1][:, 0:D]).then_inc(S["y_evac"], 1)
            dve.wait_ge(S["gath_done"], 16 * NT)
            dve.wait_ge(S["pmax_ready"], NT)
            with dve.Fori(0, NT) as t:
                ht = h[:, bass.ds(t, 1), :]
                v.scalar_tensor_tensor(ht, yg[:, bass.ds(t, 1), :], pmax[:, bass.ds(t, 1)], ht, ALU.mult, ALU.add).then_inc(S["hout"], 1)


def kernel(**a):
    import numpy as np
    import concourse.bacc as bacc
    from concourse import mybir as mb
    from concourse.bass_utils import run_bass_kernel_spmd

    n = {k: np.asarray(v) for k, v in a.items()}
    f = np.float32
    arr = {}
    x = n["x"].reshape(NT, IPT, CIN, G1, KP, G1, KP).transpose(0, 2, 4, 6, 1, 3, 5)
    x = x.reshape(NT, 48, IPT // 2, 2, PIX).transpose(0, 3, 1, 2, 4)
    arr["xcol"] = np.pad(x, ((0, 0), (0, 0), (0, 0), (0, 0), (0, PIXP - PIX)))
    arr["ident"] = np.eye(128, dtype=f)
    arr["iota21"] = np.broadcast_to(np.arange(G1, dtype=f), (TP, G1))
    pos = np.arange(TP) % POS
    tap = np.arange(TAPS)
    arr["base"] = np.concatenate([(KP * (pos // G2))[:, None] + (tap // KP)[None],
                                  (KP * (pos % G2))[:, None] + (tap % KP)[None]], 1).astype(f)
    arr["off_b"] = n["L0_tok_off_b"].reshape(TAPS, 2).T.reshape(1, -1)
    arr["off_w"] = n["L0_tok_off_w"].reshape(TAPS, 2, C1, TAPS).transpose(2, 3, 1, 0).reshape(C1, TAPS, 2 * TAPS)
    arr["notcls"] = (np.arange(TT) % TOK != 0).astype(f)[None]
    arr["cls"] = n["cls_tok"].reshape(1, D)
    stem = np.concatenate([n["L0_tok_stem_b"][None], n["L0_tok_stem_w"].reshape(C1, 48).T], 0)
    arr["stem_rows"] = np.concatenate([stem, np.zeros((15, C1), f), stem], 0)
    arr["bn1"] = np.stack([n["L0_tok_bn1_" + s] for s in "gbmv"])
    arr["bn2"] = np.stack([n["L0_tok_bn2_" + s] for s in "gbmv"] + [n["L0_tok_dcn_b"]])
    arr["dcn_w"] = n["L0_tok_dcn_w"].reshape(D, C1, TAPS).transpose(1, 2, 0)

    def rows(w, b=None):
        wt = w.T.reshape(2, KC, -1).transpose(1, 0, 2)
        last = np.zeros((1, 2, w.shape[0]), f)
        if b is not None:
            last[0, 1] = b
        return np.concatenate([wt, last], 0)

    arr["qkv0"] = rows(n["L0_attn_qkv_weight"])
    arr["qkv1"] = rows(n["L1_attn_qkv_w"], n["L1_attn_qkv_b"])
    arr["proj0"] = rows(n["L0_attn_proj_weight"])
    arr["proj1"] = rows(n["L1_attn_out_w"], n["L1_attn_out_b"])
    arr["router"] = rows(n["L1_ffn_Ws"].T, n["L1_ffn_bs"])
    tok = np.arange(TT)
    arr["mask"] = (tok[:, None] // TOK == np.arange(IPT)).astype(f)
    arr["bmask"] = np.broadcast_to(arr["mask"][:, None, :], (TT, 2 * H, IPT))
    arr["sel"] = (tok[:, None] % TOK == np.arange(TOK)).astype(f)
    emb = n["L1_attn_rel_pos_emb"][np.clip(np.arange(NREL) - (TOK - 1), -MAXREL, MAXREL) + MAXREL]
    arr["rel_emb"] = np.broadcast_to(np.tile(emb.T, (2 * IPT, 1))[:, None, :], (128, H // 2, NREL))
    arr["f_b1"] = n["L0_ffn_b1"].reshape(FM, 128).T
    arr["f_b2"] = n["L0_ffn_b2"][None]
    arr["f_w1"] = n["L0_ffn_w1"].T.reshape(2, KC, FF).transpose(1, 0, 2)
    arr["f_w2"] = n["L0_ffn_w2"].T.reshape(FM, 128, D).transpose(1, 0, 2)
    arr["f_aw1"] = n["L0_ffn_alpha_w1"][None]
    arr["f_aw1c"] = n["L0_ffn_alpha_w1"].reshape(FM, 128).T
    arr["f_aw2"] = n["L0_ffn_alpha_w2"][None]
    arr["f_aa1"] = n["L0_ffn_alpha_a1"][None]
    arr["f_aa2"] = n["L0_ffn_alpha_a2"][None]
    arr["tri"] = np.stack([np.triu(np.ones((TT, TT), f), 1), np.ones((TT, TT), f)], 1)
    arr["rev"] = np.broadcast_to(E - np.arange(E, dtype=f), (TT, E))
    arr["upto"] = np.broadcast_to(np.tril(np.ones((E, E), f)), (TT, E, E))
    arr["tidx"] = np.arange(NS, dtype=f)[None]
    ew = n["L1_ffn_W1"].reshape(E, 2, KC, FF).transpose(2, 0, 1, 3)
    eb = np.stack([np.zeros((E, FF), f), n["L1_ffn_b1"]], 1)[None]
    arr["e_w1"] = np.concatenate([ew, eb], 0)
    arr["e_w2"] = n["L1_ffn_W2"].reshape(E, FM, 128, D).transpose(2, 0, 1, 3)
    arr["e_b2"] = n["L1_ffn_b2"][None]

    nc = bacc.Bacc("TRN2", target_bir_lowering=False, num_devices=1)
    io, feed = {}, {}
    for k, v in arr.items():
        v = np.ascontiguousarray(v)
        feed[f"in_{k}"] = v
        io[k] = nc.dram_tensor(f"in_{k}", v.shape, mb.dt.from_np(v.dtype), kind="ExternalInput").ap()
    out = nc.dram_tensor("out_0", (B, TOK, D), F32, kind="ExternalOutput").ap()
    build(nc, io, out)
    r = run_bass_kernel_spmd(nc, [feed], core_ids=[0])
    return r.results[0]["out_0"]
```

```python
import numpy as np
import concourse.bass as bass
from concourse import mybir
from contextlib import ExitStack

F32 = mybir.dt.float32
BF16 = mybir.dt.bfloat16
U32 = mybir.dt.uint32
I32 = mybir.dt.int32
ALU = mybir.AluOpType
ACT = mybir.ActivationFunctionType
AX = mybir.AxisListType

B, CIN, IMG = 64, 3, 84
KP = 4
G1 = IMG // KP
PIX = G1 * G1
G2 = (G1 - KP) // KP + 1
POS = G2 * G2
TOK = POS + 1
TAPS = KP * KP
C1, D = 96, 192
IPT = 4
NT = B // IPT
TT = IPT * TOK
TP = IPT * POS
PK = 111
NK = 4
PIXP = NK * PK
H, DH = 12, 16
KC = 96
FF, FM = 768, 6
E = 8
NREL, MAXREL = 2 * TOK - 1, 16
NS = (B * TOK + E * 127) // 128
R_H, R_P, R_ID, ROW = D, 2 * D, 2 * D + 1, 2 * D + 2
EPS = 1e-5
SLOPE = 0.01
MAGIC = 12582912.0


def view(ap, dims, off=0, whole=False):
    return bass.AP(ap.tensor, ap.offset + off, ([] if whole else [list(ap.ap[0])]) + [list(d) for d in dims])


def build(nc, io, out):
    ctx = ExitStack()
    with ctx:
        def sb(name, shape, dt=F32, scope=ctx):
            return scope.enter_context(nc.sbuf_tensor(name, shape, dt))

        def sem(name):
            return ctx.enter_context(nc.semaphore(name))

        psum = ctx.enter_context(nc.psum_tensor("psum", [128, 8, 512], F32))
        bank = [psum[:, i, :] for i in range(8)]

        ident = sb("ident", [128, 128])
        eps = sb("eps", [128, 1])
        mhalf = sb("mhalf", [128, 1])

        h = sb("h", [TT, NT, D])

        wqkv = [sb(f"wqkv{l}", [KC + 1, 2, 3 * D]) for l in range(2)]
        wproj = [sb("wproj0", [D // 3, 3, D]), sb("wproj1", [KC + 1, 2, D])]
        mask = sb("mask", [TT, IPT])
        wq1 = sb("wq1", [KC, 2, FF], BF16)
        wq2 = sb("wq2", [128, FM, D], BF16)
        s1 = sb("s1", [128, FM])
        fb1 = sb("fb1", [128, FM])
        row2 = sb("row2", [TT, D])
        fb2 = sb("fb2", [TT, D])
        am = sb("am", [128, 2])
        ram = sb("ram", [128, 2])
        bound = sb("bound", [128, 3])
        identb = sb("identb", [128, 128], BF16)
        tri = sb("tri", [TT, 2, TT])
        rev = sb("rev", [TT, E])
        upto = sb("upto", [TT, E, E])
        tidx = sb("tidx", [1, NS + 2])
        ones = sb("ones", [1, 128])
        tokid = sb("tokid", [TT, NT], U32)
        mstat = [sb(f"mstat{u}", [TT, 6]) for u in range(2)]
        mvr = [sb(f"mvr{u}", [TT, 2]) for u in range(2)]
        mmv = sb("mmv", [TT, NT, 2])
        tick = sb("tick", [1, 1])
        wmean = sb("wmean", [KC + 1, 2, 2 * H])

        wr = sb("wr", [KC + 1, 2, E])

        tk = ExitStack()
        iota21 = sb("iota21", [TP, G1], scope=tk)
        base = sb("base", [TP, 2 * TAPS], scope=tk)
        off_bias = sb("off_bias", [TP, 2 * TAPS], scope=tk)
        posbase = sb("posbase", [TP, 2 * TAPS], scope=tk)
        notcls = sb("notcls", [1, TT], scope=tk)
        clsmat = sb("clsmat", [TT, D], scope=tk)
        wstem = sb("wstem", [64 + 49, C1], scope=tk)
        bn1 = sb("bn1", [64 + 49, 4, C1], scope=tk)
        inv1 = sb("inv1", [64 + 49, C1], scope=tk)
        shift1 = sb("shift1", [64 + 49, C1], scope=tk)
        woff = sb("woff", [C1, TAPS, 2 * TAPS], scope=tk)
        wdcn = sb("wdcn", [C1, TAPS, D], scope=tk)
        bn2 = sb("bn2", [C1, 5, D], scope=tk)
        inv2 = sb("inv2", [C1, D], scope=tk)
        bnw = sb("bnw", [128, D], scope=tk)
        ala2 = sb("ala2", [128, FF], scope=tk)
        ala1 = sb("ala1", [128, D], scope=tk)
        alw2 = sb("alw2", [128, D], scope=tk)
        alw1c = sb("alw1c", [128, FM], scope=tk)
        alw1 = sb("alw1", [KC, FF], scope=tk)
        raw2 = sb("raw2", [128, FM, D], scope=tk)
        raw1 = sb("raw1", [KC, 2, FF], scope=tk)
        shift2 = sb("shift2", [1, D], scope=tk)
        xcol = [sb(f"xcol{u}", [64 + 49, IPT // 2, PIXP], scope=tk) for u in range(2)]
        leak = [sb(f"leak{i}", [PK, NK * C1], scope=tk) for i in range(2)]
        hpix = [sb(f"hpix{u}", [PK, IPT, NK, C1], scope=tk) for u in range(2)]
        hch = sb("hch", [C1, IPT, PIXP], scope=tk)
        offsb = sb("offsb", [2 * TAPS, TP], scope=tk)
        pxy = sb("pxy", [TP, 2 * TAPS], scope=tk)
        dist = sb("dist", [TP, 2 * TAPS, G1], scope=tk)
        tent = sb("tent", [TP, 2 * TAPS, G1], scope=tk)
        wmap = [sb(f"wmap{i}", [TP, PIXP], scope=tk) for i in range(4)]
        wmapT = [sb(f"wmapT{u}", [PK, NK, TAPS, TP], scope=tk) for u in range(2)]
        samp = sb("samp", [C1, TAPS, IPT, TOK], scope=tk)
        dleak = sb("dleak", [TT, D], scope=tk)
        dmax = sb("dmax", [TT, D], scope=tk)

        tk.close()

        w1 = sb("w1", [KC + 1, E, 2, FF])
        w2 = sb("w2", [128, E, FM, D])
        eb2 = sb("eb2", [1, E, D])
        xgT = [sb(f"xgT{u}", [KC + 1, 2, 128]) for u in range(2)]
        blk = ExitStack()
        a2 = lambda name, shape, dt=F32: [sb(f"{name}{u}", shape, dt, scope=blk) for u in range(2)]
        stat = a2("stat", [TT, 6])
        mv = a2("mv", [TT, 2])
        rstd = a2("rstd", [TT, 1])
        xn = a2("xn", [TT, D])
        xT = a2("xT", [KC + 1, 2, TT])
        hvar = a2("hvar", [TT, 2 * H])
        hroot = a2("hroot", [TT, 2 * H])
        hwork = a2("hwork", [TT, 2 * H])
        kcp = a2("kcp", [TT, D])
        qkx = a2("qkx", [128, 2, H, IPT, DH])
        qx = [qkx[u][:TT, 0] for u in range(2)]
        kx = [qkx[u][:TT, 1] for u in range(2)]
        qkp = [view(qkx[u][:TT], [[32, 2 * H], [1, 32]]) for u in range(2)]
        qT = a2("qT", [128, H // 2, TT])
        ke = a2("ke", [128, H // 2, TOK + NREL])
        vz = a2("vz", [TT, H, 128])
        rden = sb("rden", [D // 3, 3, TT], scope=blk)
        oT0 = a2("oT0", [D // 3, 3, TT])
        se = a2("se", [TT, 2, H // 2 * (TOK + NREL)])
        rel = a2("rel", [TT, H, TOK])
        sc = a2("sc", [TT, H, TOK])
        smax = a2("smax", [TT, H])
        prob = a2("prob", [TT, H, TOK])
        rsum = a2("rsum", [TT, H])
        pmask = a2("pmask", [TT, H, IPT])
        px = a2("px", [TT, H, TT])
        pT0 = px
        turned = sb("turned", [128, H * TT], scope=blk)
        pT = [view(turned[:TT], [[TT, H], [1, TT]])] * 2
        osb = a2("osb", [TT, D])
        oT = a2("oT", [KC + 1, 2, TT])
        bmask = sb("bmask", [TT, 2 * H, IPT], scope=blk)
        fmv = sb("fmv", [TT, NT, 2], scope=blk)
        frs = sb("frs", [TT, NT, 1], scope=blk)
        xq = a2("xq", [TT, D], BF16)
        xqT = a2("xqT", [KC, 2, IPT * TT], BF16)
        gel = [turned[:, u * IPT * TT:(u + 1) * IPT * TT] for u in range(H // IPT)]
        hq = [view(qkx[u][:].bitcast(BF16), [[IPT * TT, FM], [1, IPT * TT]]) for u in range(2)]
        f2 = osb
        blk.close()

        m2 = lambda name, shape, dt=F32: [sb(f"{name}{u}", shape, dt) for u in range(2)]
        mxT = [sb(f"mxT{k}", [KC + 1, 2, TT]) for k in range(4)]
        mrs = sb("mrs", [TT, NT, 1])
        mrw = sb("mrw", [TT, NT, 1])
        mrow = sb("mrow", [TT, NT, ROW])
        lmax = sb("lmax", [TT, NT])
        lsh = sb("lsh", [TT, NT, E])
        lex = sb("lex", [TT, NT, E])
        lsum = sb("lsum", [TT, NT])
        cand = sb("cand", [TT, NT, E])
        cmax = sb("cmax", [TT, NT])
        pre = m2("pre", [TT, NT // 2 + NT, E])
        hot = sb("hot", [TT, NT, E])
        rank = sb("rank", [TT, NT, E])
        ntile = sb("ntile", [TT, E])
        cum = sb("cum", [TT, E, E])
        ends = sb("ends", [TT, E])
        start = sb("start", [TT, E])
        slotw = sb("slotw", [TT, NT, E])
        slotf = sb("slotf", [TT, NT])
        slot = sb("slot", [TT, NT], U32)
        past = sb("past", [1, NS + 2, E])
        own = sb("own", [1, NS + 2])
        owner = sb("owner", [1, NS + 2], I32)
        xg = [sb(f"xg{q}", [128, ROW]) for q in range(4)]
        w1s = m2("w1s", [KC + 1, 2, FF])
        hT = m2("hT", [128, FM, 128])
        yo = [sb(f"yo{q}", [128, D]) for q in range(4)]
        yrow = [sb(f"yrow{q}", [128, 1], U32) for q in range(4)]

        stem_in = sem("stem_in")
        par_in = sem("par_in")
        x_in = [sem(f"x_in{u}") for u in range(2)]
        pool_const = sem("pool_const")
        bn_pow = sem("bn_pow")
        fold = sem("fold")
        par_ready = sem("par_ready")
        stem_ready = sem("stem_ready")
        leak_ready = sem("leak_ready")
        hpix_ready = sem("hpix_ready")
        tr_ready = sem("tr_ready")
        tr_evac = sem("tr_evac")
        ones_ready = sem("ones_ready")
        off_ready = sem("off_ready")
        off_evac = sem("off_evac")
        offT_ready = sem("offT_ready")
        pxy_ready = sem("pxy_ready")
        dist_ready = sem("dist_ready")
        abs_ready = sem("abs_ready")
        tent_ready = sem("tent_ready")
        wmap_ready = sem("wmap_ready")
        samp_ready = sem("samp_ready")
        samp_evac = sem("samp_evac")
        dcn_ready = sem("dcn_ready")
        dleak_ready = sem("dleak_ready")
        dmax_ready = sem("dmax_ready")
        h0_ready = sem("h0_ready")

        names = ("quant_in mx_ones kcp_ready ke_ready blk_const cw vz_clear hr_ready exp1_ready wc wt_in "
                 "moe_in ms_small attn_par quant_pool quant_dve ln_raw ln_stat ln_eps ln_rstd ln_norm "
                 "xT_tr xT_evac qk_ready v_ready v_evac sq_ready hv_ready qx_ready kx_ready qT_tr kT_ready "
                 "qT_evac s_ready se_ready sr_ready smax_ready sc_ready exp_ready rs_ready rr_ready "
                 "pmask_ready px_ready pT_tr pT_evac o_ready o_evac oT_tr oT_evac proj_ready hattn_ready "
                 "f_raw f_stat f_eps f_root f_norm fq1 fq2 fq3 bound_ready hb_ready gc_ready gq_ready "
                 "xqT_tr xqT_evac fh_ready gel_ready fc_done hq_ready f2_ready f2_scaled hffn_ready r_raw "
                 "r_aggr r_stat root_done lg_ready lmax_ready lsh_ready lex_ready cand_ready cmax_ready "
                 "pmax_ready hot_ready rk_ready pre_ready plan slot_ready owner_ready rows_in rows_ready "
                 "scat_done xgT_tr xgT_evac w1_ready hid_ready hgel_ready y_ready y_evac").split()
        S = {k: sem(k) for k in names}
        qr_out = [sem(f"qr_out{u}") for u in range(2)]
        rel_in = [sem(f"rel_in{u}") for u in range(2)]
        xg_in = [sem(f"xg_in{q}") for q in range(4)]
        y_out = [sem(f"y_out{q}") for q in range(4)]

        TG = IPT + TAPS
        stem_ps = [bank[2], bank[3]]
        samp_ps = [bank[4], bank[5]]
        off_ps = bank[6][:2 * TAPS, 0:TP]
        qk_ps, xT_ps = bank[1][:TT, 0:2 * D], bank[2][:KC, D:D + 2 * TT]
        v_ps = [bank[5][:TT, 3 * TT:3 * TT + D], bank[2][:TT, 0:D]]
        proj_ps = [bank[4][:TT, 3 * TT:3 * TT + D], bank[3][:TT, 0:D]]
        offT_ps = bank[6][:TP, 128:128 + 2 * TAPS]
        dcn_ps = bank[7][:TT, 0:D]

        small = [(ident, "ident"), (woff, "off_w"), (iota21, "iota21"), (base, "base"), (off_bias, "off_b"),
                 (notcls, "notcls"), (wdcn, "dcn_w")]
        NPAR = len(small) + 1 + IPT
        weights = [(wqkv[0], "qkv0"), (wqkv[1], "qkv1"), (wproj[0], "proj0"), (wproj[1], "proj1"), (mask, "mask"),
                   (fb1, "f_b1"), (fb2, "f_b2"), (tri, "tri"), (rev, "rev"), (upto, "upto"),
                   (tidx, "tidx"), (wr, "router"), (tokid, "tokid")]
        NW = len(weights)
        quant = [(raw1, "f_w1"), (raw2, "f_w2"), (alw1, "f_aw1"), (alw1c, "f_aw1c"), (alw2, "f_aw2"),
                 (ala1, "f_aa1"), (ala2, "f_aa2")]
        late = [(bmask, "bmask")]
        NL = len(late) + 2
        NQ = IPT * (TOK * H * NREL)
        scr = nc.dram_tensor("rel_scratch", [NT, NQ], F32).ap()
        xs = nc.dram_tensor("slots_in", [NS * 128, ROW], F32).ap()

        def bcast(name, dst):
            src = io[name]
            if src.shape[0] == 1 and dst.shape[0] > 1:
                n = int(np.prod(src.shape))
                return bass.AP(src.tensor, 0, [[0, dst.shape[0]], [1, n]])
            return src

        def has(t):
            return not isinstance(t, int) or 0 <= t < NT

        def before(t, n):
            return isinstance(t, int) and t < n

        def pipelined(eng, body):
            for t in range(-4, 2):
                body(t, t % 2)
            with eng.Fori(2, NT - 5, 2) as t0:
                for u in range(2):
                    body(t0 + u, u)
            for t in range(NT - 4, NT):
                body(t, t % 2)

        block = ctx.enter_context(nc.Block())

        def load_x(eng, t, u):
            for r in range(2):
                eng.dma_start(xcol[u][64 * r + 1:64 * r + 49, :, :], io["xcol"][bass.ds(t, 1), r, :, :, :]).then_inc(x_in[u], 16)

        @block.sync
        def _(sp):
            sp.dma_start(bn1[:], bass.AP(io["bn1"].tensor, 0, [[0, 64 + 49], [1, 4 * C1]])).then_inc(stem_in, 16)
            sp.dma_start(wstem[:], io["stem_rows"]).then_inc(stem_in, 16)
            load_x(sp, 0, 0)
            for dst, name in small:
                src = io[name]
                if name == "off_b":
                    src = bass.AP(src.tensor, src.offset, [[0, TP], [1, 2 * TAPS]])
                sp.dma_start(dst[:], src).then_inc(par_in, 16)
            sp.dma_start(bn2[:], bass.AP(io["bn2"].tensor, 0, [[0, C1], [1, 5 * D]])).then_inc(par_in, 16)
            load_x(sp, 1, 1)
            sp.wait_ge(pool_const, 1)
            for i in range(IPT):
                sp.dma_start(clsmat[TOK * i:TOK * i + 1, :], io["cls"]).then_inc(par_in, 16)
            for dst, name in quant:
                sp.dma_start(dst[:], bcast(name, dst)).then_inc(S["quant_in"], 16)
            sp.wait_ge(stem_ready, IPT)
            load_x(sp, 2, 0)
            with sp.Fori(1, NT - 3, 2) as t1:
                for u in (1, 0):
                    t = t1 + (1 - u)
                    sp.wait_ge(stem_ready, IPT * t + IPT)
                    load_x(sp, t + 2, u)
            sp.wait_ge(stem_ready, IPT * (NT - 3) + IPT)
            load_x(sp, NT - 1, 1)
            for dst, name in weights:
                sp.dma_start(dst[:], bcast(name, dst)).then_inc(S["wt_in"], 16)
            sp.dma_start(xs.rearrange("(j p) d -> j p d", p=128),
                         bass.AP(io["empty"].tensor, 0, [[0, NS], [ROW, 128], [1, ROW]])).then_inc(S["rows_in"], 16)
            sp.wait_ge(h0_ready, NT)
            sp.wait_ge(S["quant_pool"], 8)
            for dst, name in late:
                sp.dma_start(dst[:], bcast(name, dst)).then_inc(S["attn_par"], 16)
            for u in range(2):
                sp.dma_start(ke[u][:, :, TOK:], io["rel_emb"]).then_inc(S["attn_par"], 16)
            for dst, name in ((w1, "e_w1"), (w2, "e_w2"), (eb2, "e_b2")):
                sp.dma_start(dst[:], io[name]).then_inc(S["moe_in"], 16)
            with sp.Fori(0, NT - 1, 2) as t0:
                for u in range(2):
                    t = t0 + u
                    sp.wait_ge(S["se_ready"], t + 1)
                    sp.dma_start(view(scr[bass.ds(t, 1), :], [[H * NREL, TT], [NREL, H], [1, NREL]], whole=True),
                                 view(se[u][:], [[TOK + NREL, H], [1, NREL]], TOK)).then_inc(qr_out[u], 16)
                    sp.wait_ge(qr_out[u], 8 * t0 + 16)
                    for i in range(IPT):
                        sp.dma_start(rel[u][TOK * i:TOK * i + TOK, :, :],
                                     view(scr[bass.ds(t, 1), :], [[H * NREL - 1, TOK], [NREL, H], [1, TOK]],
                                          i * TOK * H * NREL + TOK - 1, whole=True)).then_inc(rel_in[u], 16)
            sp.wait_ge(S["scat_done"], 16 * NT)
            for q in range(4):
                sp.dma_start(xg[q][:], xs[128 * q:128 * q + 128, :]).then_inc(xg_in[q], 16)
            with sp.Fori(0, NS - 7, 4) as j0:
                for q in range(4):
                    sp.wait_ge(S["y_evac"], j0 + q + 3)
                    sp.dma_start(xg[q][:], xs[bass.ds((j0 + q + 4) * 128, 128), :]).then_inc(xg_in[q], 16)
            for q in range(4):
                sp.wait_ge(y_out[q], 16 * (NS // 4))

        @block.gpsimd
        def _(pool):
            g = nc.gpsimd
            g.memset(clsmat[:], 0.0).then_inc(pool_const, 1)
            g.memset(eps[:], EPS).then_inc(pool_const, 1)
            g.memset(mhalf[:], -0.5).then_inc(pool_const, 1)
            g.memset(samp[:, :, :, 0:1], 0.0).then_inc(pool_const, 1)
            for i in range(4):
                g.memset(wmap[i][:, PIX:PIXP], 0.0).then_inc(pool_const, 1)
            pool.wait_ge(S["quant_dve"], 4)
            c = S["quant_pool"]
            for n, (raw, al, q) in enumerate(((raw1, view(alw1[:], [[0, 2], [1, FF]]), wq1),
                                              (raw2, view(alw2[:], [[0, FM], [1, D]]), wq2))):
                g.tensor_tensor(raw[:], raw[:], al, ALU.mult).then_inc(c, 1)
                pool.wait_ge(c, 4 * n + 1)
                g.tensor_scalar(raw[:], raw[:], -8.0, 7.0, ALU.max, ALU.min).then_inc(c, 1)
                pool.wait_ge(c, 4 * n + 2)
                g.tensor_scalar(raw[:], raw[:], MAGIC, None, ALU.add).then_inc(c, 1)
                pool.wait_ge(c, 4 * n + 3)
                g.tensor_scalar(q[:], raw[:], -MAGIC, None, ALU.add).then_inc(c, 1)

            g.memset(ones[:], 1.0).then_inc(S["ms_small"], 1)
            pool.wait_ge(S["ms_small"], 1)

            def ln_root(i, t, u, mvt, rst):
                n = i * NT + t + 1
                pool.wait_ge(S["ln_stat"], n)
                g.tensor_tensor(rst[u][:], mvt[u][:, 1:2], eps[:TT, 0:1], ALU.add).then_inc(S["ln_eps"], 1)
                pool.wait_ge(S["ln_eps"], n)
                g.tensor_tensor(rst[u][:], rst[u][:], mhalf[:TT, 0:1], ALU.pow).then_inc(S["ln_rstd"], 1)

            pool.wait_ge(h0_ready, NT)
            for u in range(2):
                g.memset(xT[u][KC:KC + 1, :, :], 1.0).then_inc(S["ms_small"], 1)
                g.memset(oT[u][KC:KC + 1, :, :], 1.0).then_inc(S["ms_small"], 1)
                g.memset(xgT[u][KC:KC + 1, :, :], 1.0).then_inc(S["ms_small"], 1)
            pool.wait_ge(S["ms_small"], 7)
            pool.wait_ge(S["wt_in"], 16 * NW)

            for u in range(2):
                g.memset(vz[u][:], 0.0).then_inc(S["vz_clear"], 1)
            pool.wait_ge(S["vz_clear"], 2)
            for u in range(2):
                g.memset(view(vz[u][:, 0, 64:], [[4 * 128, 3], [128 + DH, 4], [1, DH]]), 1.0).then_inc(S["vz_clear"], 1)
            def roots0(t, u):
                if has(t + 4):
                    ln_root(0, t + 4, u, mv, rstd)
            pipelined(pool, roots0)

            def ffn_root(t):
                if t < NT:
                    pool.wait_ge(S["f_stat"], t + 1)
                    g.tensor_tensor(frs[:, t, :], fmv[:, t, 1:2], eps[:TT, 0:1], ALU.add).then_inc(S["f_eps"], 1)
                    pool.wait_ge(S["f_eps"], t + 1)
                    g.tensor_tensor(frs[:, t, :], frs[:, t, :], mhalf[:TT, 0:1], ALU.pow).then_inc(S["f_root"], 1)

            def add_bias(t):
                pool.wait_ge(S["f_norm"], t + 1)
                g.tensor_tensor(h[:, t, :], h[:, t, :], fb2[:], ALU.add).then_inc(S["hb_ready"], 1)

            ffn_root(0)
            for t in range(IPT):
                ffn_root(t + 1)
                add_bias(t)
            pool.wait_ge(S["hattn_ready"], NT)
            for u in range(2):
                g.memset(vz[u][:], 0.0).then_inc(S["vz_clear"], 1)
            for c in range(NT // IPT + 1):
                for t in range(IPT * c, IPT * c + IPT):
                    if c > 0:
                        pool.wait_ge(S["f2_scaled"], t - IPT + 1)
                        pool.wait_ge(S["hb_ready"], t - IPT + 1)
                        g.tensor_tensor(h[:, t - IPT, :], h[:, t - IPT, :], f2[t % 2][:], ALU.add).then_inc(S["hffn_ready"], 1)
                    if t + IPT < NT:
                        ffn_root(t + IPT + 1)
                        add_bias(t + IPT)

            pool.wait_ge(S["attn_par"], 16 * NL)
            def spread_keys(t, u):
                pool.wait_ge(S["kcp_ready"], t + 1)
                g.tensor_tensor(kx[u], view(kcp[u][:], [[DH, H], [0, IPT], [1, DH]]),
                                view(bmask[:], [[IPT, H], [1, IPT], [0, DH]]), ALU.mult).then_inc(S["kx_ready"], 1)

            def roots1(t, u):
                if has(t + 4):
                    ln_root(1, t + 4, u, mv, rstd)
                if has(t + 3):
                    spread_keys(t + 3, 1 - u)
            pipelined(pool, roots1)

            pool.wait_ge(S["hattn_ready"], 2 * NT)
            for k in range(4):
                g.memset(mxT[k][KC:KC + 1, :, :], 1.0).then_inc(S["mx_ones"], 1)
            pool.wait_ge(S["mx_ones"], 4)
            g.tensor_copy(mrow[:, :, R_H:R_H + D], h[:]).then_inc(S["rows_ready"], 1)
            g.tensor_copy(mrow[:, :, R_ID].bitcast(U32), tokid[:]).then_inc(S["rows_ready"], 1)
            pool.wait_ge(S["slot_ready"], 1)
            pool.wait_ge(S["pmax_ready"], 1)
            pool.wait_ge(S["ln_norm"], 3 * NT)
            pool.wait_ge(S["rows_ready"], 2)
            pool.wait_ge(S["rows_in"], 16)
            for t in range(NT):
                g.indirect_dma_start(out=xs, out_offset=bass.IndirectOffsetOnAxis(ap=slot[:, t:t + 1], axis=0),
                                     in_=mrow[:, t, :], in_offset=None).then_inc(S["scat_done"], 16)
            for j in range(NS):
                q = j % 4
                pool.wait_ge(S["y_evac"], j + 3)
                g.indirect_dma_start(out=out.rearrange("b n d -> (b n) d"),
                                     out_offset=bass.IndirectOffsetOnAxis(ap=yrow[q][:], axis=0),
                                     in_=yo[q][:], in_offset=None, bounds_check=B * TOK - 1,
                                     oob_is_err=False).then_inc(y_out[q], 16)

        @block.tensor
        def _(pe):
            mm = nc.tensor.matmul

            def stem(t, u, c, first=False):
                if c == 0:
                    pe.wait_ge(x_in[u], 32 if first else 16 * (t - u) + 32)
                if not (first and c == 0):
                    pe.wait_ge(hpix_ready, IPT * t + 2 * c)
                for k in range(NK):
                    for r in range(2):
                        m = mm(stem_ps[r][:PK, k * C1:(k + 1) * C1], xcol[u][64 * r:64 * r + 49, c, k * PK:(k + 1) * PK],
                               wstem[64 * r:64 * r + 49, :], start=True, stop=True)
                        if k == NK - 1:
                            m.then_inc(stem_ready, 1)

            def turn_stem(t, u, b, first=False):
                pe.wait_ge(hpix_ready, IPT * t + b + 1)
                if not (first and b < 2):
                    pe.wait_ge(tr_evac, TG * t + b - 1)
                for k in range(NK):
                    m = nc.tensor.transpose(bank[b % 2][:C1, k * PK:(k + 1) * PK], hpix[u][:, b, k, :], ident[:PK, :PK])
                m.then_inc(tr_ready, 1)

            def offsets(t):
                pe.wait_ge(tr_evac, TG * t + IPT)
                for k in range(TAPS):
                    at = (k // KP) * G1 + k % KP
                    m = mm(off_ps, woff[:, k, :], view(hch[:, 0, :], [[PIXP, IPT], [KP * G1, G2], [KP, G2]], at),
                           start=(k == 0), stop=(k == TAPS - 1))
                m.then_inc(off_ready, 1)

            def turn_offsets(t):
                pe.wait_ge(off_evac, t + 1)
                mm(offT_ps, offsb[:], ident[:2 * TAPS, :2 * TAPS], start=True, stop=True).then_inc(offT_ready, 1)

            def turn_map(t, k):
                pe.wait_ge(wmap_ready, TAPS * t + k + 1)
                pe.wait_ge(tr_evac, TG * t + IPT + k - 1)
                for j in range(NK):
                    m = nc.tensor.transpose(bank[k % 2][:PK, j * TP:(j + 1) * TP],
                                            wmap[k % 4][:, j * PK:(j + 1) * PK], ident[:TP, :TP])
                m.then_inc(tr_ready, 1)

            def sample(t, u, b, k0, k1):
                if k0 == 0 and not (isinstance(t, int) and t == 0 and b < 2):
                    pe.wait_ge(samp_evac, IPT * t + b - 1)
                for k in range(k0, k1):
                    m = mm(samp_ps[b % 2][:C1, 0:TAPS * POS], hpix[u][:, b, k, :],
                           wmapT[u][:, k, :, b * POS:(b + 1) * POS], start=(k == 0), stop=(k == NK - 1))
                if k1 == NK:
                    m.then_inc(samp_ready, 1)

            def tile(t, u, nxt):
                n, un = t + 1, 1 - u
                if nxt:
                    stem(n, un, 0)
                pe.wait_ge(tr_evac, TG * t + TG)
                sample(t, u, 0, 0, 2)
                if nxt:
                    stem(n, un, 1)
                sample(t, u, 0, 2, 4)
                if nxt:
                    turn_stem(n, un, 0)
                    turn_stem(n, un, 1)
                sample(t, u, 1, 0, 2)
                if nxt:
                    turn_stem(n, un, 2)
                    turn_stem(n, un, 3)
                sample(t, u, 1, 2, 4)
                if nxt:
                    offsets(n)
                sample(t, u, 2, 0, 1)
                if nxt:
                    turn_offsets(n)
                sample(t, u, 2, 1, 4)
                sample(t, u, 3, 0, 3)
                if nxt:
                    turn_map(n, 0)
                sample(t, u, 3, 3, 4)
                if nxt:
                    turn_map(n, 1)
                pe.wait_ge(samp_evac, IPT * t + IPT)
                for k in range(TAPS):
                    mm(dcn_ps, view(samp[:, k, 0, 0:1], [[1, TT]]), wdcn[:, k, :], start=(k == 0), stop=False)
                    if nxt and k < TAPS - 2:
                        turn_map(n, k + 2)
                mm(dcn_ps, notcls[:], shift2[:], start=False, stop=True).then_inc(dcn_ready, 1)

            pe.wait_ge(par_ready, 1)
            pe.wait_ge(ones_ready, 4)
            stem(0, 0, 0, first=True)
            stem(0, 0, 1, first=True)
            pe.wait_ge(par_in, 16 * NPAR)
            pe.wait_ge(pool_const, 8)
            for b in range(IPT):
                turn_stem(0, 0, b, first=True)
            offsets(0)
            turn_offsets(0)
            for k in range(TAPS):
                turn_map(0, k)
            pe.wait_ge(par_ready, 4)
            tile(0, 0, True)
            with pe.Fori(1, NT - 1, 2) as t:
                for u in (1, 0):
                    tile(t + (1 - u), u, True)
            tile(NT - 1, 1, False)

            tr = nc.tensor.transpose
            W = TOK + NREL
            pe.wait_ge(S["wt_in"], 16 * NW)
            pe.wait_ge(S["ms_small"], 7)

            def turn_tokens(l, t, u):
                pe.wait_ge(S["ln_norm"], l * NT + t + 1)
                if l:
                    pe.wait_ge(S["v_evac"], NT + t - 1)
                elif not before(t, 2):
                    pe.wait_ge(S["qT_evac"], t - 1)
                for c in range(2):
                    m = tr(xT_ps[:, c * TT:(c + 1) * TT], xn[u][:, c * KC:(c + 1) * KC], ident[:TT, :TT])
                m.then_inc(S["xT_tr"], 1)

            def queries_keys(l, t, u):
                n = l * NT + t
                pe.wait_ge(S["xT_evac"], n + 1)
                if not (l == 0 and before(t, 1)):
                    pe.wait_ge(S["qx_ready"], n)
                if l and not before(t, 1):
                    pe.wait_ge(S["kcp_ready"], t)
                for c in range(2):
                    m = mm(qk_ps, xT[u][0:KC + c, c, :], wqkv[l][0:KC + c, c, 0:2 * D], start=(c == 0), stop=(c == 1))
                m.then_inc(S["qk_ready"], 1)

            def values(l, t, u):
                for c in range(2):
                    m = mm(v_ps[l], xT[u][0:KC + c, c, :], wqkv[l][0:KC + c, c, 2 * D:3 * D], start=(c == 0), stop=(c == 1))
                m.then_inc(S["v_ready"], 1)

            def turn_qk0(t, u):
                pe.wait_ge(S["qx_ready"], t + 1)
                if has(t + 1):
                    pe.wait_ge(S["xT_evac"], t + 2)
                for c in range(2 * H // 4):
                    dst = bank[0][:, c * TT:(c + 1) * TT] if c < 4 else bank[2][:, (c - 4) * TT + 0:(c - 3) * TT]
                    m = tr(dst, view(qkp[u][:, 4 * c, :], [[1, 128]]), ident[:TT, :TT])
                m.then_inc(S["qT_tr"], 1)

            def scores0(t, u, c):
                if c == 0:
                    pe.wait_ge(S["qT_evac"], t + 1)
                    if not before(t, 1):
                        pe.wait_ge(S["exp_ready"], t)
                    if not before(t, 2):
                        pe.wait_ge(S["hattn_ready"], t - 1)
                    pe.wait_ge(S["v_evac"], t + 1)
                for j in range(4):
                    rows = slice(32 * j, 32 * j + 32)
                    m = mm(bank[4 + j][:TT, c * TT:(c + 1) * TT], qT[u][rows, 3 + c, :], qT[u][rows, c, :],
                           start=True, stop=True)
                if c == 2:
                    m.then_inc(S["s_ready"], 1)

            def weighted0(t, u, c):
                if c == 0:
                    pe.wait_ge(S["exp_ready"], t + 1)
                    pe.wait_ge(S["v_evac"], t + 1)
                    if not before(t, 1):
                        pe.wait_ge(S["o_evac"], t)
                for j in range(4):
                    m = mm(bank[3][:, c * TT:(c + 1) * TT], vz[u][:, 4 * c + j, :], pT0[u][:, 3 * j + c, :],
                           start=(j == 0), stop=(j == 3))
                if c == 2:
                    m.then_inc(S["o_ready"], 1)

            def project0(t, u):
                pe.wait_ge(S["o_evac"], t + 1)
                if has(t + 1):
                    pe.wait_ge(S["exp_ready"], t + 2)
                for c in range(3):
                    m = mm(proj_ps[0], oT0[u][:, c, :], wproj[0][:, c, :], start=(c == 0), stop=(c == 2))
                m.then_inc(S["proj_ready"], 1)

            def tile0(t, u):
                if has(t + 3):
                    turn_tokens(0, t + 3, 1 - u)
                for c in range(3):
                    if has(t):
                        weighted0(t, u, c)
                    if has(t + 1):
                        scores0(t + 1, 1 - u, c)
                if has(t + 2):
                    turn_qk0(t + 2, u)
                if has(t + 3):
                    queries_keys(0, t + 3, 1 - u)
                if has(t + 2):
                    if has(t + 1):
                        pe.wait_ge(S["exp_ready"], t + 2)
                    values(0, t + 2, u)
                if has(t):
                    project0(t, u)

            pe.wait_ge(S["cw"], 3)
            pe.wait_ge(S["blk_const"], 1)
            pipelined(pe, tile0)

            pe.wait_ge(S["quant_pool"], 8)
            pe.wait_ge(S["quant_dve"], 9)

            def turn_quant(t):
                pe.wait_ge(S["fq3"], t + 1)
                if t >= 2:
                    pe.wait_ge(S["xqT_evac"], t - 1)
                for c in range(2):
                    m = tr(bank[t % 2][:KC, :].bitcast(BF16)[:, c * TT:c * TT + TT], xq[t % 2][:, c * KC:c * KC + KC], identb[:TT, :TT])
                m.then_inc(S["xqT_tr"], 1)

            def hidden(n):
                c, k = n // FM, n % FM
                if k == 0:
                    pe.wait_ge(S["xqT_evac"], IPT * c + IPT)
                if n >= 4:
                    pe.wait_ge(S["gel_ready"], n - 3)
                for j in range(2):
                    m = mm(bank[2 + n % 4][:, 0:IPT * TT], wq1[:, j, 128 * k:128 * k + 128], xqT[c % 2][:, j, :],
                           start=(j == 0), stop=(j == 1))
                m.then_inc(S["fh_ready"], 1)

            for t in range(IPT):
                turn_quant(t)
            for k in range(4):
                hidden(k)
            for c in range(NT // IPT):
                for k in range(4, FM + 2):
                    if k < FM:
                        hidden(FM * c + k)
                    if c + 1 < NT // IPT:
                        turn_quant(IPT * (c + 1) + k - 4)
                if c + 1 < NT // IPT:
                    for k in range(4):
                        hidden(FM * (c + 1) + k)
                pe.wait_ge(S["hq_ready"], FM * c + FM)
                for i in range(IPT):
                    t = IPT * c + i
                    if t >= 2:
                        pe.wait_ge(S["f2_scaled"], t - 1)
                    for k in range(FM):
                        m = mm(bank[6 + t % 2][:TT, 0:D], hq[c % 2][:, k, i * TT:(i + 1) * TT], wq2[:, k, :], start=(k == 0), stop=(k == FM - 1))
                    m.then_inc(S["f2_ready"], 1)

            def turn_qk1(t, u):
                n = NT + t + 1
                pe.wait_ge(S["qx_ready"], n)
                for p in range(H // 2):
                    m = tr(bank[4 + p // 3][:, (p % 3) * TT:(p % 3 + 1) * TT], view(qx[u][:, 2 * p, :, :], [[1, 128]]),
                           ident[:TT, :TT])
                m.then_inc(S["qT_tr"], 1)
                pe.wait_ge(S["kx_ready"], t + 1)
                if not before(t, 1):
                    pe.wait_ge(S["se_ready"], t)
                for p in range(H // 2):
                    m = tr(bank[6 + p // 3][:, (p % 3) * TT:(p % 3 + 1) * TT], view(kx[u][:, 2 * p, :, :], [[1, 128]]),
                           ident[:TT, :TT])
                m.then_inc(S["kT_ready"], 1)

            def scores1(t, u):
                pe.wait_ge(S["qT_evac"], NT + t + 1)
                pe.wait_ge(S["ke_ready"], t + 1)
                for p in range(H // 2):
                    for r in range(2):
                        m = mm(bank[6 + r][:TT, p * W:(p + 1) * W], qT[u][64 * r:64 * r + 64, p, :],
                               ke[u][64 * r:64 * r + 64, p, :], start=True, stop=True)
                m.then_inc(S["s_ready"], 1)

            def turn_probs(t, u, q):
                if q == 0:
                    pe.wait_ge(S["px_ready"], t + 1)
                    pe.wait_ge(S["hattn_ready"], NT + t)
                if q == 2:
                    pe.wait_ge(S["pT_evac"], 3 * t + 1)
                for k in range(4 * q, 4 * q + 4):
                    m = tr(bank[(3, 0, 3)[q]][:TT, (k % 4) * TT:(k % 4 + 1) * TT], px[u][:, k, :], ident[:TT, :TT])
                m.then_inc(S["pT_tr"], 1)

            def weighted1(t, u):
                pe.wait_ge(S["pT_evac"], 3 * t + 3)
                pe.wait_ge(S["v_evac"], NT + t + 1)
                for half in range(2):
                    for i in range(6):
                        hd = 6 * half + i
                        k = 6 * (hd % 2) + hd // 2
                        m = mm(bank[0][:KC, half * TT:(half + 1) * TT], vz[u][:, hd, 0:KC], pT[u][:, k, :],
                               start=(i == 0), stop=(i == 5))
                m.then_inc(S["oT_tr"], 1)

            def project1(t, u):
                pe.wait_ge(S["oT_evac"], t + 1)
                for c in range(2):
                    m = mm(proj_ps[1], oT[u][0:KC + c, c, :], wproj[1][0:KC + c, c, :], start=(c == 0), stop=(c == 1))
                m.then_inc(S["proj_ready"], 1)

            def tile1(t, u):
                if has(t + 2):
                    turn_qk1(t + 2, u)
                if has(t):
                    turn_probs(t, u, 0)
                    turn_probs(t, u, 1)
                if has(t + 3):
                    turn_tokens(1, t + 3, 1 - u)
                if has(t):
                    turn_probs(t, u, 2)
                if has(t + 2):
                    scores1(t + 2, u)
                if has(t + 3):
                    queries_keys(1, t + 3, 1 - u)
                if has(t):
                    weighted1(t, u)
                if has(t + 2):
                    values(1, t + 2, u)
                if has(t):
                    project1(t, u)

            pe.wait_ge(S["attn_par"], 16 * NL)
            pe.wait_ge(S["vz_clear"], 6)
            pipelined(pe, tile1)

            def turn_router(t, k):
                pe.wait_ge(S["ln_norm"], 2 * NT + t + 1)
                for c in range(2):
                    m = tr(bank[2 * k][:KC, c * TT:c * TT + TT],
                           mrow[:, t, c * KC:c * KC + KC], ident[:TT, :TT])
                m.then_inc(S["xT_tr"], 1)

            def logits(t, k):
                pe.wait_ge(S["xT_evac"], 2 * NT + t + 1)
                for c in range(2):
                    m = mm(bank[1][:TT, E * t:E * t + E], mxT[k][0:KC + c, c, :], wr[0:KC + c, c, :],
                           start=(c == 0), stop=(c == 1))
                m.then_inc(S["lg_ready"], 1)

            for t in range(2):
                turn_router(t, t)
            pe.wait_ge(S["mx_ones"], 4)
            for t in range(NT):
                if t + 2 < NT:
                    turn_router(t + 2, (t + 2) % 4)
                logits(t, t % 4)
            pe.wait_ge(S["hot_ready"], 1)
            for c in range(2):
                m = mm(bank[2][:TT, c * NT * E:(c + 1) * NT * E], tri[:, c, :], hot[:], start=True, stop=True)
            m.then_inc(S["rk_ready"], 1)
            pe.wait_ge(S["moe_in"], 48)
            pe.wait_ge(S["owner_ready"], 1)

            def turn_slots(j, q):
                pe.wait_ge(xg_in[q], 4 * (j - q) + 16)
                for c in range(2):
                    m = tr(bank[4 * (q % 2)][:KC, c * 128:c * 128 + 128], xg[q][:, c * KC:c * KC + KC], ident[:])
                m.then_inc(S["xgT_tr"], 1)

            def expert_pair(j, q0, more):
                for u in range(2):
                    pe.wait_ge(S["xgT_evac"], j + u + 1)
                    pe.wait_ge(S["w1_ready"], j + u + 1)
                    for k in range(FM):
                        for c in range(2):
                            m = mm(bank[4 * u + 1 + k // 3][:, (k % 3) * 128:(k % 3 + 1) * 128], w1s[u][0:KC + c, c, k * 128:(k + 1) * 128],
                                   xgT[u][0:KC + c, c, :], start=(c == 0), stop=(c == 1))
                    m.then_inc(S["hid_ready"], 1)
                if more:
                    for u in range(2):
                        turn_slots(j + u + 2, (q0 + 2) % 4 + u)
                ex = [nc.tensor.value_load(owner[0:1, bass.ds(j + u, 1)], min_val=0, max_val=E - 1) for u in range(2)]
                for u in range(2):
                    pe.wait_ge(S["hgel_ready"], j + u + 1)
                    pe.wait_ge(S["y_evac"], j + u + 1)
                    for k in range(FM):
                        mm(bank[4 * u + 3][:, 0:D], hT[u][:, k, :], w2[:, bass.ds(ex[u], 1), k, :], start=(k == 0), stop=False)
                    mm(bank[4 * u + 3][:, 0:D], ones[:], eb2[:, bass.ds(ex[u], 1), :], start=False, stop=True).then_inc(S["y_ready"], 1)

            for q in range(2):
                turn_slots(q, q)
            with pe.Fori(0, NS - 7, 4) as j0:
                for q0 in (0, 2):
                    expert_pair(j0 + q0, q0, True)
            for q0 in (0, 2):
                expert_pair(NS - 4 + q0, q0, q0 == 0)

        @block.scalar
        def _(act):
            def front(t, u, first=False):
                for b in range(IPT):
                    act.wait_ge(stem_ready, IPT * t + b + 1)
                    if not (first and b < 2):
                        act.wait_ge(hpix_ready, IPT * t + b - 1)
                    nc.scalar.activation(leak[b % 2][:], stem_ps[b % 2][:PK, 0:NK * C1], ACT.Copy,
                                         scale=SLOPE).then_inc(leak_ready, 1)
                for b in range(IPT):
                    act.wait_ge(tr_ready, TG * t + b + 1)
                    nc.scalar.activation(hch[:, b, :], bank[b % 2][:C1, 0:PIXP], ACT.Copy).then_inc(tr_evac, 1)
                act.wait_ge(off_ready, t + 1)
                nc.scalar.activation(offsb[:], off_ps, ACT.Copy).then_inc(off_evac, 1)
                act.wait_ge(dist_ready, t + 1)
                nc.scalar.activation(dist[:], dist[:], ACT.Abs).then_inc(abs_ready, 1)
                act.wait_ge(abs_ready, t + 1)
                nc.scalar.activation(tent[:], dist[:], ACT.Relu, bias=1.0, scale=-1.0).then_inc(tent_ready, 1)

            def turn_map(t, u, k):
                act.wait_ge(tr_ready, TG * t + IPT + k + 1)
                nc.scalar.activation(wmapT[u][:, :, k, :],
                                     view(bank[k % 2][:PK, 0:1], [[TP, NK], [1, TP]]), ACT.Copy).then_inc(tr_evac, 1)

            def tile(t, u, nxt):
                if nxt:
                    front(t + 1, 1 - u)
                    for k in range(TAPS):
                        turn_map(t + 1, 1 - u, k)
                act.wait_ge(dcn_ready, t + 1)
                nc.scalar.activation(dleak[:], dcn_ps, ACT.Copy, scale=SLOPE).then_inc(dleak_ready, 1)

            front(0, 0, first=True)
            for k in range(TAPS):
                turn_map(0, 0, k)
            tile(0, 0, True)
            with act.Fori(1, NT - 1, 2) as t:
                for u in (1, 0):
                    tile(t + (1 - u), u, True)
            tile(NT - 1, 1, False)

            def copy(dst, src):
                return nc.scalar.activation(dst, src, ACT.Copy)

            def tokens_out(l, t, u):
                act.wait_ge(S["xT_tr"], l * NT + t + 1)
                copy(xT[u][0:KC, :, :], xT_ps).then_inc(S["xT_evac"], 1)

            def squares(t, u):
                act.wait_ge(S["qk_ready"], t + 1)
                nc.scalar.activation(view(se[u][:], [[1, 2 * D]]), qk_ps, ACT.Square).then_inc(S["sq_ready"], 1)

            def values_out0(t, u):
                act.wait_ge(S["v_ready"], t + 1)
                copy(view(vz[u][:], [[4 * 128, 3], [128 + DH, 4], [1, DH]]), view(v_ps[0], [[4 * DH, 3], [DH, 4], [1, DH]])).then_inc(S["v_evac"], 1)

            def qk_out0(t, u):
                act.wait_ge(S["qT_tr"], t + 1)
                copy(qT[u][:, 0:4, :], bank[0][:, 0:4 * TT])
                copy(qT[u][:, 4:6, :], bank[2][:, 0:2 * TT]).then_inc(S["qT_evac"], 1)

            def exp0(t, u):
                act.wait_ge(S["s_ready"], t + 1)
                nc.scalar.activation(view(pT0[u][:], [[3 * TT, 4], [1, 3 * TT]]), view(bank[4][:TT, :], [[512, 4], [1, 3 * TT]]), ACT.Exp,
                                     scale=DH ** 0.5).then_inc(S["exp_ready"], 1)

            def tile0(t, u):
                if has(t + 3):
                    tokens_out(0, t + 3, 1 - u)
                if has(t + 1):
                    exp0(t + 1, 1 - u)
                if has(t + 2):
                    qk_out0(t + 2, u)
                if has(t + 3):
                    squares(t + 3, 1 - u)
                if has(t + 2):
                    values_out0(t + 2, u)

            act.wait_ge(S["vz_clear"], 4)
            pipelined(act, tile0)

            act.wait_ge(S["quant_dve"], 9)

            def quant_last(t):
                act.wait_ge(S["fq2"], t + 1)
                if t >= 2:
                    act.wait_ge(S["xqT_tr"], t - 1)
                nc.scalar.activation(xq[t % 2][:], xn[t % 2][:], ACT.Copy, bias=-MAGIC).then_inc(S["fq3"], 1)

            def quant_out(t):
                act.wait_ge(S["xqT_tr"], t + 1)
                i = t % IPT
                copy(xqT[t // IPT % 2][:, :, i * TT:(i + 1) * TT], view(bank[t % 2][:KC, :].bitcast(BF16), [[TT, 2], [1, TT]])).then_inc(S["xqT_evac"], 1)

            def hidden_quant(n):
                act.wait_ge(S["gq_ready"], n + 1)
                nc.scalar.activation(hq[n // FM % 2][:, n % FM, :], gel[n % 3][:], ACT.Copy, bias=-MAGIC).then_inc(S["hq_ready"], 1)

            for t in range(IPT):
                quant_last(t)
                quant_out(t)
            for c in range(NT // IPT):
                for k in range(FM):
                    n = FM * c + k
                    act.wait_ge(S["fh_ready"], n + 1)
                    if n >= 3:
                        act.wait_ge(S["hq_ready"], n - 2)
                    nc.scalar.activation(gel[n % 3][:], bank[2 + n % 4][:, 0:IPT * TT], ACT.Gelu, bias=fb1[:, k:k + 1],
                                         scale=s1[:, k:k + 1]).then_inc(S["gel_ready"], 1)
                    if n > 0:
                        hidden_quant(n - 1)
                    if c + 1 < NT // IPT:
                        if 1 <= k <= IPT:
                            quant_last(IPT * (c + 1) + k - 1)
                        if 3 <= k:
                            quant_out(IPT * (c + 1) + k - 3)
                if c + 1 < NT // IPT:
                    quant_out(IPT * (c + 1) + 3)
            hidden_quant(NT // IPT * FM - 1)

            def keys_out(t, u):
                act.wait_ge(S["qk_ready"], NT + t + 1)
                copy(kcp[u][:], qk_ps[:, D:2 * D]).then_inc(S["kcp_ready"], 1)

            def values_out1(t, u):
                act.wait_ge(S["v_ready"], NT + t + 1)
                for half in range(2):
                    m = copy(view(vz[u][:, 6 * half, :], [[128 + DH, 6], [1, DH]]), view(v_ps[1][:, half * KC:], [[DH, 6], [1, DH]]))
                m.then_inc(S["v_evac"], 1)

            def queries_out(t, u):
                act.wait_ge(S["qT_tr"], NT + t + 1)
                copy(view(qT[u][:], [[3 * TT, 2], [1, 3 * TT]]), view(bank[4], [[512, 2], [1, 3 * TT]])).then_inc(S["qT_evac"], 1)

            def scores_out(t, u):
                act.wait_ge(S["s_ready"], NT + t + 1)
                copy(se[u][:], psum[:TT, 6:8, 0:H // 2 * (TOK + NREL)]).then_inc(S["se_ready"], 1)

            def probs_out(t, u, q):
                act.wait_ge(S["pT_tr"], 3 * t + q + 1)
                copy(pT[u][:, 4 * q:4 * q + 4, :], bank[(3, 0, 3)[q]][:TT, 0:4 * TT]).then_inc(S["pT_evac"], 1)

            def tile1(t, u):
                if has(t + 2):
                    queries_out(t + 2, u)
                if has(t):
                    probs_out(t, u, 0)
                    probs_out(t, u, 1)
                if has(t + 3):
                    tokens_out(1, t + 3, 1 - u)
                if has(t):
                    probs_out(t, u, 2)
                if has(t + 2):
                    scores_out(t + 2, u)
                if has(t + 3):
                    keys_out(t + 3, 1 - u)
                if has(t + 1):
                    act.wait_ge(S["sc_ready"], t + 2)
                    nc.scalar.activation(prob[1 - u][:], sc[1 - u][:], ACT.Exp, scale=DH ** -0.5).then_inc(S["exp1_ready"], 1)
                if has(t):
                    act.wait_ge(S["oT_tr"], t + 1)
                    copy(oT[u][0:KC, :, :], bank[0][:KC, 0:2 * TT]).then_inc(S["oT_evac"], 1)
                if has(t + 2):
                    values_out1(t + 2, u)

            act.wait_ge(S["vz_clear"], 6)
            pipelined(act, tile1)

            with act.Fori(0, NT - 3, 4) as t0:
                for k in range(4):
                    act.wait_ge(S["xT_tr"], 2 * NT + t0 + k + 1)
                    copy(mxT[k][0:KC, :, :], bank[2 * k][:KC, 0:2 * TT]).then_inc(S["xT_evac"], 1)
            act.wait_ge(S["lsh_ready"], 1)
            nc.scalar.activation(lex[:], lsh[:], ACT.Exp).then_inc(S["lex_ready"], 1)
            with act.Fori(0, NS - 1, 2) as j0:
                for u in range(2):
                    act.wait_ge(S["hid_ready"], j0 + u + 1)
                    nc.scalar.activation(hT[u][:], psum[:, 4 * u + 1:4 * u + 3, 0:384], ACT.Gelu).then_inc(S["hgel_ready"], 1)

        @block.vector
        def _(dve):
            v = nc.vector
            def root(x, y, w, eps_, done, n, each=1):
                def step(ins):
                    nonlocal n
                    ins.then_inc(done, 1)
                    n = n + 1
                    dve.wait_ge(done, n)
                step(v.tensor_scalar(x, x, eps_, None, ALU.add))
                step(v.tensor_scalar(y.bitcast(I32), x.bitcast(I32), -0.5, float(0x5f3759df), ALU.mult, ALU.add))
                for _ in range(3):
                    step(v.scalar_tensor_tensor(w, y, -0.5, y, ALU.mult, ALU.mult))
                    step(v.tensor_tensor(w, w, x, ALU.mult))
                    step(v.scalar_tensor_tensor(y, w, 1.5, y, ALU.add, ALU.mult))
                return n

            for u in range(2):
                for r in range(2):
                    v.memset(xcol[u][64 * r:64 * r + 1, :, :], 1.0).then_inc(ones_ready, 1)

            dve.wait_ge(stem_in, 32)
            n = root(bn1[:, 3, :], inv1[:], bnw[:64 + 49, 0:C1], EPS, bn_pow, 0) + 1
            v.tensor_tensor(inv1[:], inv1[:], bn1[:, 0, :], ALU.mult).then_inc(bn_pow, 1)
            dve.wait_ge(bn_pow, n)
            v.tensor_tensor(wstem[:], wstem[:], inv1[:], ALU.mult).then_inc(fold, 1)
            v.tensor_tensor(shift1[:], bn1[:, 2, :], inv1[:], ALU.mult).then_inc(fold, 1)
            dve.wait_ge(fold, 2)
            v.tensor_tensor(shift1[:], bn1[:, 1, :], shift1[:], ALU.subtract).then_inc(fold, 1)
            dve.wait_ge(fold, 3)
            v.tensor_tensor(wstem[0:1, :], wstem[0:1, :], shift1[0:1, :], ALU.add)
            v.tensor_tensor(wstem[64:65, :], wstem[64:65, :], shift1[64:65, :], ALU.add).then_inc(par_ready, 1)

            def fold_second(n):
                dve.wait_ge(par_in, 16 * NPAR)
                n = root(bn2[:, 3, :], inv2[:], bnw[:C1, :], EPS, bn_pow, n) + 1
                v.tensor_tensor(inv2[:], inv2[:], bn2[:, 0, :], ALU.mult).then_inc(bn_pow, 1)
                v.tensor_tensor(posbase[:], base[:], off_bias[:], ALU.add).then_inc(par_ready, 1)
                v.tensor_tensor(shift2[:], bn2[0:1, 4, :], bn2[0:1, 2, :], ALU.subtract).then_inc(fold, 1)
                dve.wait_ge(bn_pow, n)
                v.tensor_tensor(wdcn[:], wdcn[:], view(inv2[:], [[0, TAPS], [1, D]]), ALU.mult).then_inc(par_ready, 1)
                dve.wait_ge(fold, 4)
                v.tensor_tensor(shift2[:], shift2[:], inv2[0:1, :], ALU.mult).then_inc(fold, 1)
                dve.wait_ge(fold, 5)
                v.tensor_tensor(shift2[:], shift2[:], bn2[0:1, 1, :], ALU.add).then_inc(par_ready, 1)
                dve.wait_ge(par_ready, 4)
                dve.wait_ge(pool_const, 8)

            def leaky(t, u, b):
                dve.wait_ge(leak_ready, IPT * t + b + 1)
                v.tensor_tensor(hpix[u][:, b, :, :], stem_ps[b % 2][:PK, 0:NK * C1], leak[b % 2][:],
                                ALU.max).then_inc(hpix_ready, 1)

            def distances(t):
                dve.wait_ge(offT_ready, t + 1)
                v.tensor_tensor(pxy[:], offT_ps, posbase[:], ALU.add).then_inc(pxy_ready, 1)
                dve.wait_ge(pxy_ready, t + 1)
                v.tensor_tensor(dist[:], view(pxy[:], [[1, 2 * TAPS], [0, G1]]),
                                view(iota21[:], [[0, 2 * TAPS], [1, G1]]), ALU.subtract).then_inc(dist_ready, 1)

            def make_map(t, k):
                if k >= 4:
                    dve.wait_ge(tr_ready, TG * t + k + 1)
                v.tensor_tensor(view(wmap[k % 4][:], [[G1, G1], [1, G1]]),
                                view(tent[:, k, :], [[1, G1], [0, G1]]),
                                view(tent[:, TAPS + k, :], [[0, G1], [1, G1]]), ALU.mult).then_inc(wmap_ready, 1)

            def sampled(t, b):
                dve.wait_ge(samp_ready, IPT * t + b + 1)
                v.tensor_copy(samp[:, :, b, 1:TOK],
                              view(samp_ps[b % 2][:C1, 0:1], [[POS, TAPS], [1, POS]])).then_inc(samp_evac, 1)

            def tile(t, u, nxt, between=None):
                n, un = t + 1, 1 - u
                if nxt:
                    for b in range(IPT):
                        leaky(n, un, b)
                sampled(t, 0)
                if between:
                    between(0)
                sampled(t, 1)
                if between:
                    between(1)
                if nxt:
                    distances(n)
                sampled(t, 2)
                if nxt:
                    dve.wait_ge(tent_ready, n + 1)
                    make_map(n, 0)
                    make_map(n, 1)
                sampled(t, 3)
                if nxt:
                    for k in range(2, TAPS):
                        make_map(n, k)
                if between:
                    between(2)
                dve.wait_ge(dleak_ready, t + 1)
                v.tensor_tensor(dmax[:], dcn_ps, dleak[:], ALU.max).then_inc(dmax_ready, 1)
                dve.wait_ge(dmax_ready, t + 1)
                v.tensor_tensor(h[:, bass.ds(t, 1), :], dmax[:], clsmat[:], ALU.add).then_inc(h0_ready, 1)

            def quant_constants(part):
                q = S["quant_dve"]
                if part == 0:
                    dve.wait_ge(S["quant_in"], 16 * len(quant))
                    v.tensor_reduce(am[:, 0:1], ala1[:], AX.X, ALU.add).then_inc(S["fc_done"], 1)
                    v.tensor_reduce(am[:, 1:2], ala2[:], AX.X, ALU.add).then_inc(S["fc_done"], 1)
                    dve.wait_ge(S["fc_done"], 2)
                    v.tensor_scalar(am[:, 0:1], am[:, 0:1], 1.0 / D, None, ALU.mult).then_inc(q, 1)
                    v.tensor_scalar(am[:, 1:2], am[:, 1:2], 1.0 / FF, None, ALU.mult).then_inc(q, 1)
                elif part == 1:
                    dve.wait_ge(q, 2)
                    v.tensor_tensor(row2[:], alw2[:TT, :], view(am[:TT, 1:2], [[0, D]]), ALU.mult).then_inc(S["fc_done"], 1)
                    dve.wait_ge(S["fc_done"], 3)
                    v.reciprocal(alw2[:], alw2[:]).then_inc(q, 1)
                else:
                    v.reciprocal(alw1[:], alw1[:]).then_inc(q, 1)
                    v.reciprocal(ram[:], am[:]).then_inc(q, 1)
                    v.tensor_scalar(s1[:], alw1c[:], am[:, 0:1], None, ALU.mult).then_inc(q, 1)
                    v.tensor_copy(identb[:], ident[:]).then_inc(q, 3)

            for b in range(IPT):
                leaky(0, 0, b)
            fold_second(n)
            distances(0)
            dve.wait_ge(tent_ready, 1)
            for k in range(TAPS):
                make_map(0, k)
            tile(0, 0, True, quant_constants)
            with dve.Fori(1, NT - 1, 2) as t:
                for u in (1, 0):
                    tile(t + (1 - u), u, True)
            dve.wait_ge(S["wt_in"], 16 * NW)
            cw = S["cw"]
            wq_ = view(wqkv[0][:], [[3 * D, 2], [DH, 2 * H], [1, DH]])
            v.tensor_reduce(wmean[:], wq_, AX.X, ALU.add).then_inc(cw, 1)
            dve.wait_ge(cw, 1)
            v.tensor_scalar(wmean[:], wmean[:], 1.0 / DH, None, ALU.mult).then_inc(cw, 1)
            dve.wait_ge(cw, 2)
            v.tensor_tensor(wq_, wq_, view(wmean[:], [[2 * H, 2], [1, 2 * H], [0, DH]]), ALU.subtract).then_inc(cw, 1)
            tile(NT - 1, 1, False)

            def norm(t, i, u, mvt, rst, dst):
                dve.wait_ge(S["ln_rstd"], i * NT + t + 1)
                v.tensor_scalar(dst, h[:, bass.ds(t, 1), :], mvt[u][:, 0:1], rst[u][:, 0:1],
                                ALU.subtract, ALU.mult).then_inc(S["ln_norm"], 1)

            def ln(l, t, u):
                dve.wait_ge(S["hffn_ready"] if l else h0_ready, t + 1)
                v.bn_stats(stat[u][:], h[:, bass.ds(t, 1), :]).then_inc(S["ln_raw"], 1)
                dve.wait_ge(S["ln_raw"], l * NT + t + 1)
                v.memset(tick[:], 0.0)
                v.bn_aggr(mv[u][:], stat[u][:]).then_inc(S["ln_stat"], 1)

            def residual(l, t):
                dve.wait_ge(S["proj_ready"], l * NT + t + 1)
                v.tensor_tensor(h[:, bass.ds(t, 1), :], h[:, bass.ds(t, 1), :], proj_ps[l], ALU.add).then_inc(S["hattn_ready"], 1)

            wc = S["wc"]
            for u in range(2):
                v.memset(qkp[u][:, :, DH + IPT:], 0.0).then_inc(wc, 1)
                v.tensor_scalar(view(qkp[u][:, 0, DH:], [[32, H], [1, IPT]]), view(mask[:], [[0, H], [1, IPT]]), -1.0, 64.0,
                                ALU.add, ALU.mult).then_inc(wc, 1)
                v.tensor_copy(view(qkp[u][:, H, DH:], [[32, H], [1, IPT]]), view(mask[:], [[0, H], [1, IPT]])).then_inc(wc, 1)
            dve.wait_ge(wc, 6)
            v.memset(tick[:], 0.0).then_inc(S["blk_const"], 1)

            def head_norm(t, u):
                n = root(hvar[u][:], hroot[u][:], hwork[u][:], DH * EPS, S["hr_ready"], 11 * t)
                v.tensor_tensor(qkp[u][:, :, 0:DH], view(qk_ps, [[DH, 2 * H], [1, DH]]), view(hroot[u][:], [[1, 2 * H], [0, DH]]),
                                ALU.mult).then_inc(S["qx_ready"], 1)

            def head_squares(t, u):
                dve.wait_ge(S["sq_ready"], t + 1)
                v.tensor_reduce(hvar[u][:], view(se[u][:], [[DH, 2 * H], [1, DH]]), AX.X, ALU.add).then_inc(S["hv_ready"], 1)
                dve.wait_ge(S["hv_ready"], t + 1)

            def divide(t, u):
                dve.wait_ge(S["o_ready"], t + 1)
                v.reciprocal(rden[:], bank[3][64:128, 0:3 * TT]).then_inc(S["rr_ready"], 1)
                dve.wait_ge(S["rr_ready"], t + 1)
                v.tensor_tensor(oT0[u][:], bank[3][:64, 0:3 * TT], rden[:], ALU.mult).then_inc(S["o_evac"], 1)

            def tile0(t, u):
                if has(t + 4):
                    ln(0, t + 4, u)
                if has(t):
                    divide(t, u)
                if has(t + 4):
                    norm(t + 4, 0, u, mv, rstd, xn[u][:])
                if has(t + 3):
                    head_squares(t + 3, 1 - u)
                if has(t):
                    residual(0, t)
                if has(t + 3):
                    head_norm(t + 3, 1 - u)
            pipelined(dve, tile0)

            b, br = bound, S["bound_ready"]
            v.tensor_scalar(b[:, 0:1], ram[:, 1:2], -10.0, None, ALU.mult).then_inc(br, 1)
            dve.wait_ge(br, 1)
            v.scalar_tensor_tensor(b[:, 0:1], ram[:, 1:2], 10.0, b[:, 0:1], ALU.mult, ALU.max).then_inc(br, 1)
            dve.wait_ge(br, 2)
            v.tensor_scalar(b[:, 1:2], b[:, 0:1], -1.0, -8.0, ALU.mult, ALU.max).then_inc(br, 1)
            v.tensor_scalar(b[:, 2:3], b[:, 0:1], 7.0, None, ALU.min).then_inc(br, 1)
            dve.wait_ge(br, 4)

            def stats(t):
                if t < NT:
                    dve.wait_ge(S["hattn_ready"], t + 1)
                    v.bn_stats(stat[t % 2][:], h[:, t, :]).then_inc(S["f_raw"], 1)
                    dve.wait_ge(S["f_raw"], t + 1)
                    v.bn_aggr(fmv[:, t, :], stat[t % 2][:]).then_inc(S["f_stat"], 1)

            def quant_first(t):
                x = xn[t % 2][:]
                if t >= 2:
                    dve.wait_ge(S["fq3"], t - 1)
                dve.wait_ge(S["f_root"], t + 1)
                v.tensor_scalar(x, h[:, t, :], fmv[:, t, 0:1], frs[:, t, :], ALU.subtract, ALU.mult).then_inc(S["f_norm"], 1)
                dve.wait_ge(S["f_norm"], t + 1)
                v.tensor_scalar(x, x, ram[:TT, 0:1], -8.0, ALU.mult, ALU.max).then_inc(S["fq1"], 1)
                dve.wait_ge(S["fq1"], t + 1)
                v.tensor_scalar(x, x, 7.0, MAGIC, ALU.min, ALU.add).then_inc(S["fq2"], 1)

            def scale_out(t):
                dve.wait_ge(S["f2_ready"], t + 1)
                if t >= 2:
                    dve.wait_ge(S["hffn_ready"], t - 1)
                v.tensor_tensor(f2[t % 2][:], bank[6 + t % 2][:TT, 0:D], row2[:], ALU.mult).then_inc(S["f2_scaled"], 1)

            def clip(n):
                gk = gel[n % 3]
                dve.wait_ge(S["gel_ready"], n + 1)
                v.tensor_scalar(gk[:], gk[:], ram[:, 1:2], b[:, 1:2], ALU.mult, ALU.max).then_inc(S["gc_ready"], 1)
                dve.wait_ge(S["gc_ready"], n + 1)
                v.tensor_scalar(gk[:], gk[:], b[:, 2:3], MAGIC, ALU.min, ALU.add).then_inc(S["gq_ready"], 1)

            stats(0)
            stats(1)
            for t in range(IPT):
                stats(t + 2)
                quant_first(t)
            for c in range(NT // IPT):
                for k in range(FM):
                    clip(FM * c + k)
                    if k < IPT and c > 0:
                        scale_out(IPT * (c - 1) + k)
                    if k < IPT and c + 1 < NT // IPT:
                        stats(IPT * (c + 1) + k + 2)
                        quant_first(IPT * (c + 1) + k)
            for i in range(IPT):
                scale_out(NT - IPT + i)

            dve.wait_ge(S["attn_par"], 16 * NL)

            def spread_queries(t, u):
                dve.wait_ge(S["kcp_ready"], t + 1)
                v.tensor_tensor(qx[u], view(qk_ps, [[DH, H], [0, IPT], [1, DH]]),
                                view(bmask[:], [[IPT, H], [1, IPT], [0, DH]]), ALU.mult).then_inc(S["qx_ready"], 1)

            def keys(t, u):
                dve.wait_ge(S["kT_ready"], t + 1)
                for half in range(2):
                    m = v.tensor_reduce(ke[u][:, 3 * half:3 * half + 3, 0:TOK],
                                        view(bank[6 + half], [[TT, 3], [1, TOK], [TOK, IPT]]), AX.X, ALU.add)
                m.then_inc(S["ke_ready"], 1)

            def shifted(t, u):
                dve.wait_ge(S["se_ready"], t + 1)
                dve.wait_ge(rel_in[u], 32 * (t - u) + 64)
                v.tensor_tensor(sc[u][:], view(se[u][:], [[TOK + NREL, H], [1, TOK]]), rel[u][:], ALU.add).then_inc(S["sr_ready"], 1)
                dve.wait_ge(S["sr_ready"], t + 1)
                v.tensor_reduce(smax[u][:], sc[u][:], AX.X, ALU.max).then_inc(S["smax_ready"], 1)
                dve.wait_ge(S["smax_ready"], t + 1)
                v.tensor_tensor(sc[u][:], sc[u][:], view(smax[u][:], [[1, H], [0, TOK]]), ALU.subtract).then_inc(S["sc_ready"], 1)

            def probabilities(t, u):
                dve.wait_ge(S["exp1_ready"], t + 1)
                v.tensor_reduce(rsum[u][:], prob[u][:], AX.X, ALU.add).then_inc(S["rs_ready"], 1)
                dve.wait_ge(S["rs_ready"], t + 1)
                v.reciprocal(rsum[u][:], rsum[u][:]).then_inc(S["rr_ready"], 1)
                dve.wait_ge(S["rr_ready"], NT + t + 1)
                v.tensor_tensor(pmask[u][:], view(rsum[u][:], [[1, H], [0, IPT]]), view(mask[:], [[0, H], [1, IPT]]),
                                ALU.mult).then_inc(S["pmask_ready"], 1)
                dve.wait_ge(S["pmask_ready"], t + 1)
                v.tensor_tensor(view(px[u][:], [[TT, H], [TOK, IPT], [1, TOK]]), view(prob[u][:], [[TOK, H], [0, IPT], [1, TOK]]),
                                view(pmask[u][:], [[IPT, H], [1, IPT], [0, TOK]]), ALU.mult).then_inc(S["px_ready"], 1)

            def tile1(t, u):
                if has(t + 2):
                    keys(t + 2, u)
                if has(t + 1):
                    shifted(t + 1, 1 - u)
                if has(t + 4):
                    ln(1, t + 4, u)
                if has(t + 3):
                    spread_queries(t + 3, 1 - u)
                if has(t + 1):
                    probabilities(t + 1, 1 - u)
                if has(t):
                    residual(1, t)
                if has(t + 4):
                    norm(t + 4, 1, u, mv, rstd, xn[u][:])
                if has(t):
                    dve.wait_ge(S["hattn_ready"], NT + t + 1)
                    v.memset(tick[:], 0.0)
                    v.bn_stats(mstat[u][:], h[:, bass.ds(t, 1), :]).then_inc(S["r_raw"], 1)
                    dve.wait_ge(S["r_raw"], t + 1)
                    v.memset(tick[:], 0.0)
                    v.bn_aggr(mvr[u][:], mstat[u][:]).then_inc(S["r_aggr"], 1)
                    dve.wait_ge(S["r_aggr"], t + 1)
                    v.tensor_copy(mmv[:, bass.ds(t, 1), :], mvr[u][:]).then_inc(S["r_stat"], 1)
            pipelined(dve, tile1)

            dve.wait_ge(S["r_stat"], NT)
            root(mmv[:, :, 1:2], mrs[:], mrw[:], EPS, S["root_done"], 0)

            with dve.Fori(0, NT - 3, 4) as t0:
                for k in range(4):
                    v.tensor_scalar(mrow[:, bass.ds(t0 + k, 1), 0:D], h[:, bass.ds(t0 + k, 1), :],
                                    mmv[:, bass.ds(t0 + k, 1), 0:1], mrs[:, bass.ds(t0 + k, 1), :],
                                    ALU.subtract, ALU.mult).then_inc(S["ln_norm"], 1)
            for u in range(2):
                v.memset(pre[u][:, 0:NT // 2, :], 0.0).then_inc(S["pre_ready"], 1)
            over_e = lambda ap: view(ap, [[1, NT], [0, E]])
            lg = bank[1][:TT, 0:NT * E]
            dve.wait_ge(S["lg_ready"], NT)
            v.tensor_reduce(lmax[:], view(lg, [[E, NT], [1, E]]), AX.X, ALU.max).then_inc(S["lmax_ready"], 1)
            dve.wait_ge(S["lmax_ready"], 1)
            v.tensor_tensor(lsh[:], view(lg, [[E, NT], [1, E]]), over_e(lmax[:]), ALU.subtract).then_inc(S["lsh_ready"], 1)
            dve.wait_ge(S["lsh_ready"], 1)
            v.scalar_tensor_tensor(cand[:], lsh[:], 0.0, view(rev[:], [[0, NT], [1, E]]), ALU.is_ge, ALU.mult).then_inc(S["cand_ready"], 1)
            dve.wait_ge(S["cand_ready"], 1)
            v.tensor_reduce(cmax[:], cand[:], AX.X, ALU.max).then_inc(S["cmax_ready"], 1)
            dve.wait_ge(S["cmax_ready"], 1)
            v.tensor_tensor(hot[:], cand[:], over_e(cmax[:]), ALU.is_equal).then_inc(S["hot_ready"], 1)
            dve.wait_ge(S["lex_ready"], 1)
            v.tensor_reduce(lsum[:], lex[:], AX.X, ALU.add).then_inc(S["pre_ready"], 1)
            dve.wait_ge(S["pre_ready"], 3)
            v.reciprocal(mrow[:, :, R_P], lsum[:]).then_inc(S["pmax_ready"], 1)
            dve.wait_ge(S["rk_ready"], 1)
            v.tensor_copy(pre[0][:, NT // 2:, :], bank[2][:TT, NT * E:2 * NT * E]).then_inc(S["pre_ready"], 1)
            for k in range(4):
                src, dst, step = pre[k % 2], pre[1 - k % 2], 1 << k
                dve.wait_ge(S["pre_ready"], 4 + k)
                v.tensor_tensor(dst[:, NT // 2:, :], src[:, NT // 2:, :], src[:, NT // 2 - step:NT // 2 + NT - step, :],
                                ALU.add).then_inc(S["pre_ready"], 1)
            dve.wait_ge(S["pre_ready"], 8)
            v.tensor_tensor(rank[:], bank[2][:TT, 0:NT * E], pre[0][:, NT // 2 - 1:NT // 2 - 1 + NT, :], ALU.add).then_inc(S["plan"], 1)
            done = S["plan"]
            v.tensor_scalar(ntile[:], pre[0][:, NT // 2 + NT - 1, :], 63.5, 1.0 / 128, ALU.add, ALU.mult).then_inc(done, 1)
            dve.wait_ge(done, 2)
            v.tensor_scalar(ntile[:], ntile[:], MAGIC, None, ALU.add).then_inc(done, 1)
            dve.wait_ge(done, 3)
            v.tensor_scalar(ntile[:], ntile[:], -MAGIC, None, ALU.add).then_inc(done, 1)
            dve.wait_ge(done, 4)
            v.tensor_tensor(cum[:], view(ntile[:], [[0, E], [1, E]]), upto[:], ALU.mult).then_inc(done, 1)
            dve.wait_ge(done, 5)
            v.tensor_reduce(ends[:], cum[:], AX.X, ALU.add).then_inc(done, 1)
            dve.wait_ge(done, 6)
            v.tensor_tensor(start[:], ends[:], ntile[:], ALU.subtract).then_inc(done, 1)
            v.tensor_tensor(past[:], view(ends[0:1, :], [[0, NS + 2], [1, E]]), view(tidx[:], [[1, NS + 2], [0, E]]), ALU.is_le).then_inc(done, 1)
            dve.wait_ge(done, 8)
            v.scalar_tensor_tensor(slotw[:], view(start[:], [[0, NT], [1, E]]), 128.0, rank[:], ALU.mult, ALU.add).then_inc(done, 1)
            v.tensor_reduce(own[:], past[:], AX.X, ALU.add).then_inc(done, 1)
            dve.wait_ge(done, 10)
            v.tensor_tensor(slotw[:], slotw[:], hot[:], ALU.mult).then_inc(done, 1)
            v.tensor_scalar(own[:], own[:], float(E - 1), None, ALU.min).then_inc(done, 1)
            dve.wait_ge(done, 12)
            v.tensor_reduce(slotf[:], slotw[:], AX.X, ALU.add).then_inc(done, 1)
            v.tensor_copy(owner[:], own[:]).then_inc(S["owner_ready"], 1)
            dve.wait_ge(done, 13)
            v.tensor_copy(slot[:], slotf[:]).then_inc(S["slot_ready"], 1)
            v.memset(tick[:], 0.0).then_inc(S["y_evac"], 2)

            def expert_weights(j, u, first=False):
                ex = nc.vector.value_load(owner[0:1, bass.ds(j, 1)], min_val=0, max_val=E - 1)
                if not first:
                    dve.wait_ge(S["hid_ready"], j - 1)
                v.tensor_copy(w1s[u][:], w1[:, bass.ds(ex, 1), :, :]).then_inc(S["w1_ready"], 1)

            dve.wait_ge(S["owner_ready"], 1)
            dve.wait_ge(S["moe_in"], 48)

            def slots_out(j, u):
                dve.wait_ge(S["xgT_tr"], j + 1)
                v.tensor_copy(xgT[u][0:KC, :, :], bank[4 * u][:KC, 0:256]).then_inc(S["xgT_evac"], 1)

            def results(j0):
                for q0 in (0, 2):
                    for u in range(2):
                        expert_weights(j0 + q0 + u + 2, u)
                    for u in range(2):
                        if not (isinstance(j0, int) and j0 + q0 + u + 2 >= NS):
                            slots_out(j0 + q0 + u + 2, u)
                    for u in range(2):
                        q = q0 + u
                        dve.wait_ge(S["y_ready"], j0 + q + 1)
                        if not (isinstance(j0, int) and j0 == 0):
                            dve.wait_ge(y_out[q], 4 * j0)
                        v.tensor_copy(yrow[q][:], xg[q][:, R_ID:R_ID + 1].bitcast(U32))
                        v.scalar_tensor_tensor(yo[q][:], bank[4 * u + 3][:, 0:D], xg[q][:, R_P:R_P + 1], xg[q][:, R_H:R_H + D],
                                               ALU.mult, ALU.add).then_inc(S["y_evac"], 1)

            for u in range(2):
                expert_weights(u, u, first=True)
            for u in range(2):
                slots_out(u, u)
            results(0)
            with dve.Fori(4, NS - 7, 4) as j0:
                results(j0)
            results(NS - 4)


def kernel(**a):
    import numpy as np
    import concourse.bacc as bacc
    from concourse import mybir as mb
    from concourse.bass_utils import run_bass_kernel_spmd

    n = {k: np.asarray(v) for k, v in a.items()}
    f = np.float32
    arr = {}
    x = n["x"].reshape(NT, IPT, CIN, G1, KP, G1, KP).transpose(0, 2, 4, 6, 1, 3, 5)
    x = x.reshape(NT, 48, IPT // 2, 2, PIX).transpose(0, 3, 1, 2, 4)
    arr["xcol"] = np.pad(x, ((0, 0), (0, 0), (0, 0), (0, 0), (0, PIXP - PIX)))
    arr["ident"] = np.eye(128, dtype=f)
    arr["iota21"] = np.broadcast_to(np.arange(G1, dtype=f), (TP, G1))
    pos = np.arange(TP) % POS
    tap = np.arange(TAPS)
    arr["base"] = np.concatenate([(KP * (pos // G2))[:, None] + (tap // KP)[None],
                                  (KP * (pos % G2))[:, None] + (tap % KP)[None]], 1).astype(f)
    arr["off_b"] = n["L0_tok_off_b"].reshape(TAPS, 2).T.reshape(1, -1)
    arr["off_w"] = n["L0_tok_off_w"].reshape(TAPS, 2, C1, TAPS).transpose(2, 3, 1, 0).reshape(C1, TAPS, 2 * TAPS)
    arr["notcls"] = (np.arange(TT) % TOK != 0).astype(f)[None]
    arr["cls"] = n["cls_tok"].reshape(1, D)
    stem = np.concatenate([n["L0_tok_stem_b"][None], n["L0_tok_stem_w"].reshape(C1, 48).T], 0)
    arr["stem_rows"] = np.concatenate([stem, np.zeros((15, C1), f), stem], 0)
    arr["bn1"] = np.stack([n["L0_tok_bn1_" + s] for s in "gbmv"])
    arr["bn2"] = np.stack([n["L0_tok_bn2_" + s] for s in "gbmv"] + [n["L0_tok_dcn_b"]])
    arr["dcn_w"] = n["L0_tok_dcn_w"].reshape(D, C1, TAPS).transpose(1, 2, 0)

    def rows(w, b=None):
        wt = w.T.reshape(2, KC, -1).transpose(1, 0, 2)
        last = np.zeros((1, 2, w.shape[0]), f)
        if b is not None:
            last[0, 1] = b
        return np.concatenate([wt, last], 0)

    arr["qkv0"] = rows(n["L0_attn_qkv_weight"])
    arr["qkv1"] = rows(n["L1_attn_qkv_w"], n["L1_attn_qkv_b"])
    arr["proj0"] = n["L0_attn_proj_weight"].T.reshape(3, D // 3, D).transpose(1, 0, 2)
    arr["proj1"] = rows(n["L1_attn_out_w"], n["L1_attn_out_b"])
    arr["router"] = rows(n["L1_ffn_Ws"].T, n["L1_ffn_bs"])
    tok = np.arange(TT)
    arr["mask"] = (tok[:, None] // TOK == np.arange(IPT)).astype(f)
    arr["bmask"] = np.broadcast_to(arr["mask"][:, None, :], (TT, 2 * H, IPT))
    emb = n["L1_attn_rel_pos_emb"][np.clip(np.arange(NREL) - (TOK - 1), -MAXREL, MAXREL) + MAXREL]
    arr["rel_emb"] = np.broadcast_to(np.tile(emb.T, (2 * IPT, 1))[:, None, :], (128, H // 2, NREL))
    arr["f_b1"] = n["L0_ffn_b1"].reshape(FM, 128).T
    arr["f_b2"] = n["L0_ffn_b2"][None]
    arr["f_w1"] = n["L0_ffn_w1"].T.reshape(2, KC, FF).transpose(1, 0, 2)
    arr["f_w2"] = n["L0_ffn_w2"].T.reshape(FM, 128, D).transpose(1, 0, 2)
    arr["f_aw1"] = n["L0_ffn_alpha_w1"][None]
    arr["f_aw1c"] = n["L0_ffn_alpha_w1"].reshape(FM, 128).T
    arr["f_aw2"] = n["L0_ffn_alpha_w2"][None]
    arr["f_aa1"] = n["L0_ffn_alpha_a1"][None]
    arr["f_aa2"] = n["L0_ffn_alpha_a2"][None]
    arr["tri"] = np.stack([np.triu(np.ones((TT, TT), f), 1), np.ones((TT, TT), f)], 1)
    arr["rev"] = np.broadcast_to(E - np.arange(E, dtype=f), (TT, E))
    arr["upto"] = np.broadcast_to(np.tril(np.ones((E, E), f)), (TT, E, E))
    arr["tokid"] = (np.arange(NT)[None] * TT + np.arange(TT)[:, None]).astype(np.uint32)
    empty = np.zeros((128, ROW), np.uint32)
    empty[:, R_ID] = B * TOK + np.arange(128)
    arr["empty"] = empty.view(f)
    arr["tidx"] = np.arange(NS + 2, dtype=f)[None]
    ew = n["L1_ffn_W1"].reshape(E, 2, KC, FF).transpose(2, 0, 1, 3)
    eb = np.stack([np.zeros((E, FF), f), n["L1_ffn_b1"]], 1)[None]
    arr["e_w1"] = np.concatenate([ew, eb], 0)
    arr["e_w2"] = n["L1_ffn_W2"].reshape(E, FM, 128, D).transpose(2, 0, 1, 3)
    arr["e_b2"] = n["L1_ffn_b2"][None]

    nc = bacc.Bacc("TRN2", target_bir_lowering=False, num_devices=1)
    io, feed = {}, {}
    for k, v in arr.items():
        v = np.ascontiguousarray(v)
        feed[f"in_{k}"] = v
        io[k] = nc.dram_tensor(f"in_{k}", v.shape, mb.dt.from_np(v.dtype), kind="ExternalInput").ap()
    out = nc.dram_tensor("out_0", (B, TOK, D), F32, kind="ExternalOutput").ap()
    build(nc, io, out)
    r = run_bass_kernel_spmd(nc, [feed], core_ids=[0])
    return r.results[0]["out_0"]
```
